# Optimizing a Trainium2 kernel written in Bass

```python
import numpy as np
import jax
import jax.numpy as jnp

def _softmax(x, axis=-1):
    return jax.nn.softmax(x, axis=axis)

def _gelu(x):
    return jax.nn.gelu(x, approximate=True)

def _silu(x):
    return jax.nn.silu(x)

def _sigmoid(x):
    return jax.nn.sigmoid(x)

def _layernorm(x, axis=-1, eps=1e-05):
    m = jnp.mean(x, axis=axis, keepdims=True)
    v = jnp.var(x, axis=axis, keepdims=True)
    return (x - m) / jnp.sqrt(v + eps)

def _scatter_add(tgt, idx, src, axis=0):
    return tgt.at[idx].add(src)

def _segment_sum(src, seg, n):
    return jax.ops.segment_sum(src, seg, n)
kernel_name = 'mk_metaformer_d2_conv_nhwc1024_r4_06e03b'

def setup_inputs(seed: int=0):
    np.random.seed(seed)
    _w = jnp.asarray

    def _rec_inputs():
        import jax
        import jax.numpy as jnp
        _gk = jax.random.key(seed)
        x = -7.109e-05 + 0.9999 * jax.random.normal(jax.random.fold_in(_gk, 1), (16, 16, 16, 256), jnp.float32)
        return x
    x = _rec_inputs()

    def _L0_conv_setup():
        import jax, jax.numpy as jnp
        import numpy as np
        import math
        B, T, IN_CH, OUT_CH, L = (16, 16, 16, 16, 256)
        MODES = 16
        HEADS = 4
        MIDCH = 32
        C_CONST = 1.0

        def timestep_embedding(t, dim):
            half = dim // 2
            freqs = jnp.exp(-math.log(10000.0) * jnp.arange(half, dtype=jnp.float32) / half)
            args = t[:, None] * freqs[None, :]
            return jnp.concatenate([jnp.sin(args), jnp.cos(args)], axis=-1)
        key = jax.random.key(seed)
        k1, k2, k3, k4 = jax.random.split(key, 4)
        scale_w = 1.0 / (IN_CH * OUT_CH)
        scale_e = 1.0 / (MIDCH * MODES)
        x = jax.random.normal(k1, (B, T, IN_CH, L), dtype=jnp.float32)
        t = jax.random.uniform(k2, (T,), dtype=jnp.float32) * 1000.0
        weights1 = scale_w * jax.random.uniform(k3, (IN_CH, OUT_CH, MODES, 2), dtype=jnp.float32)
        ke_weights = scale_e * jax.random.uniform(k4, (HEADS, MIDCH // HEADS, 2 * MODES), dtype=jnp.float32)
        ke_bias = jnp.zeros((1, 1, 2 * MODES), dtype=jnp.float32)
        return {'x': x, 't': t, 'weights1': weights1, 'ke_weights': ke_weights, 'ke_bias': ke_bias}
    _L0_conv_all = _L0_conv_setup()
    _L0_conv_in = {k: v for k, v in _L0_conv_all.items() if k in ('t', 'weights1', 'ke_weights', 'ke_bias')}
    del _L0_conv_all

    def _L0_ffn_setup():
        import jax, jax.numpy as jnp
        import numpy as np
        TOP_K = 2
        key = jax.random.key(seed)
        ks = jax.random.split(key, 5)
        B, S, H, I, E = (4, 1024, 256, 512, 8)
        scale = 0.02
        return {'hidden_states': jax.random.normal(ks[0], (B, S, H), dtype=jnp.float32), 'router_w': jax.random.normal(ks[1], (E, H), dtype=jnp.float32) * scale, 'gate_w': jax.random.normal(ks[2], (E, I, H), dtype=jnp.float32) * scale, 'up_w': jax.random.normal(ks[3], (E, I, H), dtype=jnp.float32) * scale, 'down_w': jax.random.normal(ks[4], (E, H, I), dtype=jnp.float32) * scale}
    _L0_ffn_all = _L0_ffn_setup()
    _L0_ffn_in = {k: v for k, v in _L0_ffn_all.items() if k in ('router_w', 'gate_w', 'up_w', 'down_w')}
    del _L0_ffn_all

    def _L1_conv_setup():
        import jax, jax.numpy as jnp
        import numpy as np
        LEAK = 0.2

        def conv1x1_bn_relu(x, w, s, b):
            y = jnp.einsum('nhwc,cd->nhwd', x, w)
            return jax.nn.relu(y * s + b)

        def ca_gate(x, w0, wh, we):
            x = jax.nn.leaky_relu(x @ w0, LEAK)
            for k in range(wh.shape[0]):
                x = jax.nn.leaky_relu(x @ wh[k], LEAK)
            return jax.nn.sigmoid(x @ we)

        def _forward(x, entry_w, entry_s, entry_b, vqk_w, vqk_s, vqk_b, hqk_w, hqk_s, hqk_b, val_w, val_s, val_b, vca_w0, vca_wh, vca_we, hca_w0, hca_wh, hca_we, end_w, end_s, end_b, il_w, il_s, il_b):
            N, H, W, _ = x.shape
            inputs = x
            y = jax.lax.conv_general_dilated(x, entry_w, (1, 1), 'SAME', dimension_numbers=('NHWC', 'HWIO', 'NHWC'))
            y = jax.nn.relu(y * entry_s + entry_b)
            qv = conv1x1_bn_relu(y, vqk_w, vqk_s, vqk_b)
            qh = conv1x1_bn_relu(y, hqk_w, hqk_s, hqk_b)
            A_v = jax.nn.softmax(jnp.einsum('niwg,njwg->nwij', qv, qv), axis=-1)
            A_h = jax.nn.softmax(jnp.einsum('nhig,nhjg->nhij', qh, qh), axis=-1)
            feat = conv1x1_bn_relu(y, val_w, val_s, val_b)
            inv_hw = 1.0 / (H * W)
            s_v = jnp.einsum('nwij,njwc->niwc', A_v, feat)
            gate_v = ca_gate(s_v.sum(axis=2) * inv_hw, vca_w0, vca_wh, vca_we)
            x_v = s_v * gate_v[:, :, None, :]
            s_h = jnp.einsum('nhij,nhjc->nhic', A_h, x_v)
            gate_h = ca_gate(s_h.sum(axis=1) * inv_hw, hca_w0, hca_wh, hca_we)
            x_h = s_h * gate_h[:, None, :, :]
            out_main = conv1x1_bn_relu(x_h, end_w, end_s, end_b)
            pooled = inputs.mean(axis=(1, 2), keepdims=True)
            il = conv1x1_bn_relu(pooled, il_w, il_s, il_b)
            il = jnp.broadcast_to(il, (N, H, W, il.shape[-1]))
            return jnp.concatenate([out_main, il], axis=-1)
        key = jax.random.key(seed)
        ks = jax.random.split(key, 32)
        N, H, W, Cin, F, G, Hd = (2, 65, 65, 256, 128, 16, 32)
        NH = 4

        def w(k, shape):
            fan = int(np.prod(shape[:-1]))
            return (jax.random.normal(k, shape, jnp.float32) / np.sqrt(fan)).astype(jnp.float32)

        def bn(k, c):
            k1, k2 = jax.random.split(k)
            s = 1.0 + 0.1 * jax.random.normal(k1, (c,), jnp.float32)
            b = 0.1 * jax.random.normal(k2, (c,), jnp.float32)
            return (s, b)
        entry_s, entry_b = bn(ks[1], F)
        vqk_s, vqk_b = bn(ks[3], G)
        hqk_s, hqk_b = bn(ks[5], G)
        val_s, val_b = bn(ks[7], F)
        end_s, end_b = bn(ks[9], F)
        il_s, il_b = bn(ks[11], F)
        return {'x': jax.random.normal(ks[0], (N, H, W, Cin), jnp.float32), 'entry_w': w(ks[12], (3, 3, Cin, F)), 'entry_s': entry_s, 'entry_b': entry_b, 'vqk_w': w(ks[13], (F, G)), 'vqk_s': vqk_s, 'vqk_b': vqk_b, 'hqk_w': w(ks[14], (F, G)), 'hqk_s': hqk_s, 'hqk_b': hqk_b, 'val_w': w(ks[15], (F, F)), 'val_s': val_s, 'val_b': val_b, 'vca_w0': w(ks[16], (F, Hd)), 'vca_wh': w(ks[17], (NH, Hd, Hd)) * np.sqrt(NH), 'vca_we': w(ks[18], (Hd, F)), 'hca_w0': w(ks[19], (F, Hd)), 'hca_wh': w(ks[20], (NH, Hd, Hd)) * np.sqrt(NH), 'hca_we': w(ks[21], (Hd, F)), 'end_w': w(ks[22], (F, F)), 'end_s': end_s, 'end_b': end_b, 'il_w': w(ks[23], (Cin, F)), 'il_s': il_s, 'il_b': il_b}
    _L1_conv_all = _L1_conv_setup()
    _L1_conv_in = {k: v for k, v in _L1_conv_all.items() if k in ('entry_w', 'entry_s', 'entry_b', 'vqk_w', 'vqk_s', 'vqk_b', 'hqk_w', 'hqk_s', 'hqk_b', 'val_w', 'val_s', 'val_b', 'vca_w0', 'vca_wh', 'vca_we', 'hca_w0', 'hca_wh', 'hca_we', 'end_w', 'end_s', 'end_b', 'il_w', 'il_s', 'il_b')}
    del _L1_conv_all

    def _L1_ffn_setup():
        import jax, jax.numpy as jnp
        import numpy as np
        B, T, C = (2, 512, 256)
        E, F = (8, 256)
        FS = 512
        TOP_K = 2
        key = jax.random.key(seed)
        ks = jax.random.split(key, 6)
        s = lambda *d: 1.0 / np.sqrt(d[-1])
        return {'hidden_tensor': jax.random.normal(ks[0], (B, T, C), jnp.float32), 'w_router': jax.random.normal(ks[1], (E, C), jnp.float32) * s(C), 'w1_stack': jax.random.normal(ks[2], (E, F, C), jnp.float32) * s(C), 'w2_stack': jax.random.normal(ks[3], (E, C, F), jnp.float32) * s(F), 'ws1': jax.random.normal(ks[4], (FS, C), jnp.float32) * s(C), 'ws2': jax.random.normal(ks[5], (C, FS), jnp.float32) * s(FS)}
    _L1_ffn_all = _L1_ffn_setup()
    _L1_ffn_in = {k: v for k, v in _L1_ffn_all.items() if k in ('w_router', 'w1_stack', 'w2_stack', 'ws1', 'ws2')}
    del _L1_ffn_all
    return {'x': x, 'L0_conv_t': _L0_conv_in['t'], 'L0_conv_weights1': _L0_conv_in['weights1'], 'L0_conv_ke_weights': _L0_conv_in['ke_weights'], 'L0_conv_ke_bias': _L0_conv_in['ke_bias'], 'L0_ffn_router_w': _L0_ffn_in['router_w'], 'L0_ffn_gate_w': _L0_ffn_in['gate_w'], 'L0_ffn_up_w': _L0_ffn_in['up_w'], 'L0_ffn_down_w': _L0_ffn_in['down_w'], 'L1_conv_entry_w': _L1_conv_in['entry_w'], 'L1_conv_entry_s': _L1_conv_in['entry_s'], 'L1_conv_entry_b': _L1_conv_in['entry_b'], 'L1_conv_vqk_w': _L1_conv_in['vqk_w'], 'L1_conv_vqk_s': _L1_conv_in['vqk_s'], 'L1_conv_vqk_b': _L1_conv_in['vqk_b'], 'L1_conv_hqk_w': _L1_conv_in['hqk_w'], 'L1_conv_hqk_s': _L1_conv_in['hqk_s'], 'L1_conv_hqk_b': _L1_conv_in['hqk_b'], 'L1_conv_val_w': _L1_conv_in['val_w'], 'L1_conv_val_s': _L1_conv_in['val_s'], 'L1_conv_val_b': _L1_conv_in['val_b'], 'L1_conv_vca_w0': _L1_conv_in['vca_w0'], 'L1_conv_vca_wh': _L1_conv_in['vca_wh'], 'L1_conv_vca_we': _L1_conv_in['vca_we'], 'L1_conv_hca_w0': _L1_conv_in['hca_w0'], 'L1_conv_hca_wh': _L1_conv_in['hca_wh'], 'L1_conv_hca_we': _L1_conv_in['hca_we'], 'L1_conv_end_w': _L1_conv_in['end_w'], 'L1_conv_end_s': _L1_conv_in['end_s'], 'L1_conv_end_b': _L1_conv_in['end_b'], 'L1_conv_il_w': _L1_conv_in['il_w'], 'L1_conv_il_s': _L1_conv_in['il_s'], 'L1_conv_il_b': _L1_conv_in['il_b'], 'L1_ffn_w_router': _L1_ffn_in['w_router'], 'L1_ffn_w1_stack': _L1_ffn_in['w1_stack'], 'L1_ffn_w2_stack': _L1_ffn_in['w2_stack'], 'L1_ffn_ws1': _L1_ffn_in['ws1'], 'L1_ffn_ws2': _L1_ffn_in['ws2']}

def reference(x, L0_conv_t, L0_conv_weights1, L0_conv_ke_weights, L0_conv_ke_bias, L0_ffn_router_w, L0_ffn_gate_w, L0_ffn_up_w, L0_ffn_down_w, L1_conv_entry_w, L1_conv_entry_s, L1_conv_entry_b, L1_conv_vqk_w, L1_conv_vqk_s, L1_conv_vqk_b, L1_conv_hqk_w, L1_conv_hqk_s, L1_conv_hqk_b, L1_conv_val_w, L1_conv_val_s, L1_conv_val_b, L1_conv_vca_w0, L1_conv_vca_wh, L1_conv_vca_we, L1_conv_hca_w0, L1_conv_hca_wh, L1_conv_hca_we, L1_conv_end_w, L1_conv_end_s, L1_conv_end_b, L1_conv_il_w, L1_conv_il_s, L1_conv_il_b, L1_ffn_w_router, L1_ffn_w1_stack, L1_ffn_w2_stack, L1_ffn_ws1, L1_ffn_ws2):
    import jax
    import jax.numpy as jnp

    def _L0_conv_ref(x, t, weights1, ke_weights, ke_bias):
        import jax, jax.numpy as jnp
        import numpy as np
        import math
        B, T, IN_CH, OUT_CH, L = (16, 16, 16, 16, 256)
        MODES = 16
        HEADS = 4
        MIDCH = 32
        C_CONST = 1.0

        def timestep_embedding(t, dim):
            half = dim // 2
            freqs = jnp.exp(-math.log(10000.0) * jnp.arange(half, dtype=jnp.float32) / half)
            args = t[:, None] * freqs[None, :]
            return jnp.concatenate([jnp.sin(args), jnp.cos(args)], axis=-1)
        emb = timestep_embedding(t, MIDCH)
        thc = emb.reshape(T, HEADS, MIDCH // HEADS)
        thm = jnp.einsum('thc,hcm->thm', thc, ke_weights)
        thm = jnp.tile(thm, (1, IN_CH // HEADS, 1)) + ke_bias
        wt = thm.reshape(T, IN_CH, MODES, 2)
        w_temb = wt[..., 0] + 1j * wt[..., 1]
        w = weights1[..., 0] + 1j * weights1[..., 1]
        x_ft = jnp.fft.rfft(x, axis=-1)[..., :MODES]
        out = x_ft * w_temb[None]
        out = jnp.einsum('btix,iox->btox', out, w)
        norm = jnp.einsum('tix,iox->tox', jnp.abs(w_temb), jnp.abs(w)) + 1e-12
        norm = jax.nn.relu(norm / C_CONST - 1.0) + 1.0
        out = out / norm[None]
        nf = L // 2 + 1
        out_ft = jnp.zeros((B, T, OUT_CH, nf), dtype=out.dtype).at[..., :MODES].set(out)
        return jnp.fft.irfft(out_ft, n=L, axis=-1)

    def _L0_ffn_ref(hidden_states, router_w, gate_w, up_w, down_w):
        import jax, jax.numpy as jnp
        import numpy as np
        TOP_K = 2
        B, S, H = hidden_states.shape
        E = router_w.shape[0]
        flat = hidden_states.reshape(-1, H)
        logits = flat @ router_w.T
        probs = jax.nn.softmax(logits.astype(jnp.float32), axis=-1)
        topk_prob, topk_idx = jax.lax.top_k(probs, TOP_K)
        topk_prob = topk_prob / jnp.sum(topk_prob, axis=-1, keepdims=True)
        topk_prob = topk_prob.astype(logits.dtype)
        out = jnp.zeros_like(flat)
        for e in range(E):
            w_e = jnp.sum(topk_prob * (topk_idx == e), axis=-1)
            g = jax.nn.silu(flat @ gate_w[e].T)
            u = flat @ up_w[e].T
            y = g * u @ down_w[e].T
            out = out + w_e[:, None] * y
        return out.reshape(B, S, H)

    def _L1_conv_ref(x, entry_w, entry_s, entry_b, vqk_w, vqk_s, vqk_b, hqk_w, hqk_s, hqk_b, val_w, val_s, val_b, vca_w0, vca_wh, vca_we, hca_w0, hca_wh, hca_we, end_w, end_s, end_b, il_w, il_s, il_b):
        import jax, jax.numpy as jnp
        import numpy as np
        LEAK = 0.2

        def conv1x1_bn_relu(x, w, s, b):
            y = jnp.einsum('nhwc,cd->nhwd', x, w)
            return jax.nn.relu(y * s + b)

        def ca_gate(x, w0, wh, we):
            x = jax.nn.leaky_relu(x @ w0, LEAK)
            for k in range(wh.shape[0]):
                x = jax.nn.leaky_relu(x @ wh[k], LEAK)
            return jax.nn.sigmoid(x @ we)

        def _forward(x, entry_w, entry_s, entry_b, vqk_w, vqk_s, vqk_b, hqk_w, hqk_s, hqk_b, val_w, val_s, val_b, vca_w0, vca_wh, vca_we, hca_w0, hca_wh, hca_we, end_w, end_s, end_b, il_w, il_s, il_b):
            N, H, W, _ = x.shape
            inputs = x
            y = jax.lax.conv_general_dilated(x, entry_w, (1, 1), 'SAME', dimension_numbers=('NHWC', 'HWIO', 'NHWC'))
            y = jax.nn.relu(y * entry_s + entry_b)
            qv = conv1x1_bn_relu(y, vqk_w, vqk_s, vqk_b)
            qh = conv1x1_bn_relu(y, hqk_w, hqk_s, hqk_b)
            A_v = jax.nn.softmax(jnp.einsum('niwg,njwg->nwij', qv, qv), axis=-1)
            A_h = jax.nn.softmax(jnp.einsum('nhig,nhjg->nhij', qh, qh), axis=-1)
            feat = conv1x1_bn_relu(y, val_w, val_s, val_b)
            inv_hw = 1.0 / (H * W)
            s_v = jnp.einsum('nwij,njwc->niwc', A_v, feat)
            gate_v = ca_gate(s_v.sum(axis=2) * inv_hw, vca_w0, vca_wh, vca_we)
            x_v = s_v * gate_v[:, :, None, :]
            s_h = jnp.einsum('nhij,nhjc->nhic', A_h, x_v)
            gate_h = ca_gate(s_h.sum(axis=1) * inv_hw, hca_w0, hca_wh, hca_we)
            x_h = s_h * gate_h[:, None, :, :]
            out_main = conv1x1_bn_relu(x_h, end_w, end_s, end_b)
            pooled = inputs.mean(axis=(1, 2), keepdims=True)
            il = conv1x1_bn_relu(pooled, il_w, il_s, il_b)
            il = jnp.broadcast_to(il, (N, H, W, il.shape[-1]))
            return jnp.concatenate([out_main, il], axis=-1)
        return _forward(x, entry_w, entry_s, entry_b, vqk_w, vqk_s, vqk_b, hqk_w, hqk_s, hqk_b, val_w, val_s, val_b, vca_w0, vca_wh, vca_we, hca_w0, hca_wh, hca_we, end_w, end_s, end_b, il_w, il_s, il_b)

    def _L1_ffn_ref(hidden_tensor, w_router, w1_stack, w2_stack, ws1, ws2):
        import jax, jax.numpy as jnp
        import numpy as np
        B, T, C = (2, 512, 256)
        E, F = (8, 256)
        FS = 512
        TOP_K = 2
        Bb, Tt, Cc = hidden_tensor.shape
        x = hidden_tensor.reshape(-1, Cc)
        t = x.shape[0]
        logits = x @ w_router.T
        probs = jax.nn.softmax(logits, axis=-1)
        expert_weight, expert_idx = jax.lax.top_k(probs, TOP_K)
        expert_weight = expert_weight / jnp.sum(expert_weight, axis=-1, keepdims=True)
        flat_e = expert_idx.reshape(-1)
        order = jnp.argsort(flat_e, stable=True)
        sorted_e = flat_e[order]
        flat_tok = jnp.repeat(jnp.arange(t), TOP_K)
        sorted_tok = flat_tok[order]
        sorted_w = expert_weight.reshape(-1)[order]
        counts = jnp.bincount(sorted_e, length=E)
        offsets = jnp.concatenate([jnp.zeros((1,), counts.dtype), jnp.cumsum(counts)])
        local_pos = jnp.arange(t * TOP_K) - offsets[sorted_e]
        cap = t * TOP_K
        binned = jnp.zeros((E, cap, Cc), x.dtype).at[sorted_e, local_pos].set(x[sorted_tok])
        inter = jnp.einsum('ecd,efd->ecf', binned, w1_stack)
        inter = jnp.square(jax.nn.relu(inter))
        outb = jnp.einsum('ecf,edf->ecd', inter, w2_stack)
        flat_out = outb[sorted_e, local_pos] * sorted_w[:, None]
        moe_out = jnp.zeros((t, Cc), x.dtype).at[sorted_tok].add(flat_out)
        moe_out = moe_out.reshape(Bb, Tt, Cc)
        sh = jnp.square(jax.nn.relu(jnp.einsum('btc,fc->btf', hidden_tensor, ws1)))
        shared_out = jnp.einsum('btf,cf->btc', sh, ws2)
        return shared_out + moe_out

    def _gn(v, G=32, eps=1e-05):
        B_, H_, W_, C_ = v.shape
        g = v.reshape(B_, H_, W_, G, C_ // G)
        m = jnp.mean(g, axis=(1, 2, 4), keepdims=True)
        s = jnp.var(g, axis=(1, 2, 4), keepdims=True)
        return ((g - m) / jnp.sqrt(s + eps)).reshape(v.shape)

    def _ln_c(v, eps=1e-06):
        m = jnp.mean(v, axis=-1, keepdims=True)
        s = jnp.var(v, axis=-1, keepdims=True)
        return (v - m) / jnp.sqrt(s + eps)

    def _ln_t(v, eps=1e-05):
        m = jnp.mean(v, axis=-1, keepdims=True)
        s = jnp.var(v, axis=-1, keepdims=True)
        return (v - m) / jnp.sqrt(s + eps)

    def _to_tokens(v):
        B_, H_, W_, C_ = v.shape
        return v.reshape(B_, H_ * W_, C_)

    def _from_tokens(t, like):
        return t.reshape(like.shape)
    x = x + _L0_conv_ref(_ln_c(x), L0_conv_t, L0_conv_weights1, L0_conv_ke_weights, L0_conv_ke_bias)
    t = _to_tokens(x)
    t = t + _L0_ffn_ref(_ln_t(t), L0_ffn_router_w, L0_ffn_gate_w, L0_ffn_up_w, L0_ffn_down_w)
    x = _from_tokens(t, x)
    x = x + _L1_conv_ref(_ln_c(x), L1_conv_entry_w, L1_conv_entry_s, L1_conv_entry_b, L1_conv_vqk_w, L1_conv_vqk_s, L1_conv_vqk_b, L1_conv_hqk_w, L1_conv_hqk_s, L1_conv_hqk_b, L1_conv_val_w, L1_conv_val_s, L1_conv_val_b, L1_conv_vca_w0, L1_conv_vca_wh, L1_conv_vca_we, L1_conv_hca_w0, L1_conv_hca_wh, L1_conv_hca_we, L1_conv_end_w, L1_conv_end_s, L1_conv_end_b, L1_conv_il_w, L1_conv_il_s, L1_conv_il_b)
    t = _to_tokens(x)
    t = t + _L1_ffn_ref(_ln_t(t), L1_ffn_w_router, L1_ffn_w1_stack, L1_ffn_w2_stack, L1_ffn_ws1, L1_ffn_ws2)
    x = _from_tokens(t, x)
    return x

_drawn_inputs = setup_inputs


def setup_inputs(seed=0):
    import zlib

    import numpy as np

    out = dict(_drawn_inputs(seed))
    spreads = {'L0_conv_ke_bias': (0.0, 0.8)}
    factors = {'L0_conv_t': 8.0,
     'L0_conv_weights1': 8.0,
     'L0_conv_ke_weights': 8.0,
     'L1_conv_entry_s': 3.451,
     'L1_conv_vqk_s': 5.245,
     'L1_conv_vqk_b': 6.132,
     'L1_conv_hqk_s': 8.0,
     'L1_conv_hqk_b': 5.083,
     'L1_conv_vca_w0': 8.0,
     'L1_conv_vca_wh': 8.0,
     'L1_conv_vca_we': 8.0,
     'L1_conv_hca_w0': 8.0,
     'L1_conv_hca_wh': 8.0,
     'L1_conv_hca_we': 8.0,
     'L1_conv_end_s': 4.598,
     'L1_conv_il_s': 13.569}
    for name, (base, spread) in spreads.items():
        noise = np.random.default_rng([zlib.crc32(name.encode()), seed]).standard_normal(out[name].shape)
        drawn = base * np.exp(spread * noise) if base else spread * noise
        out[name] = jnp.asarray(drawn.astype(out[name].dtype))
    for name, factor in factors.items():
        out[name] = (out[name] * factor).astype(out[name].dtype)
    return out
```

```python
from contextlib import ExitStack

import numpy as np

import concourse.bass as bass
from concourse import mybir

ALU = mybir.AluOpType
ACT = mybir.ActivationFunctionType
AX_X = mybir.AxisListType.X
F32 = mybir.dt.float32
I32 = mybir.dt.int32

P = 128
IMAGES, ROWS, COLS, C = 16, 16, 16, 256
TOKENS = IMAGES * ROWS * COLS
TILES = TOKENS // P
KC = C // P
HALVES = TILES // IMAGES
ROWS_T = ROWS // HALVES
MODES = 16
E = 8
I0, I1, IS = 512, 256, 512
F = 128
G = 16
HID = 32
SLOT_TILES = (2 * TOKENS // P + E - 1 + 3) // 4 * 4
CHUNKS, CHUNK_T = 4, 8
RING = 2
ROUND = 1.5 * 2.0 ** 23
BIG = 2.0 ** 100
TWO_PI = 2.0 * np.pi


def constants():
    parts = {}
    c = np.arange(C)[:, None]
    m = np.arange(MODES)[None, :]
    angle = 2 * np.pi * c * m / C
    dft = np.concatenate([np.cos(angle), -np.sin(angle)], 1)
    parts["dft"] = dft.reshape(KC, P, 2 * MODES).transpose(1, 0, 2).reshape(P, -1)
    twice = np.where(m == 0, 1.0, 2.0)
    idft = np.concatenate([twice * np.cos(angle), -twice * np.sin(angle) * (m > 0)], 1).T / C
    parts["idft"] = np.tile(idft, (4, 1))
    parts["ident"] = np.eye(P)
    parts["ramp"] = np.tile(np.arange(P)[None, :], (P, 1))
    parts["column"] = np.arange(P)[:, None]
    parts["tile_base"] = np.tile(P * np.arange(TILES)[None, :], (P, 1))
    parts["first_wins"] = np.tile(E - np.arange(E)[None, :], (P, 1))
    parts["row_of"] = (np.arange(P)[:, None] // COLS == np.arange(ROWS_T)[None, :])
    parts["before"] = (np.arange(P)[:, None] < np.arange(P)[None, :])
    parts["ones"] = np.ones((P, P))
    j = np.arange(2 * MODES)
    freq = np.exp(-np.log(10000.0).astype(np.float32) * (j % MODES).astype(np.float32) / np.float32(MODES))
    parts["freq"] = np.pad(freq[:, None], ((0, P - 2 * MODES), (0, 0)))
    parts["phase"] = np.pad(np.where(j >= MODES, np.pi / 2, 0.0)[:, None], ((0, P - 2 * MODES), (0, 0)))
    head = (np.arange(COLS)[None, :] % 4 == j[:, None] // 8)
    parts["head"] = np.pad(head, ((0, P - 2 * MODES), (0, 0)))
    for name, group in (("same_col", np.arange(P) % 8), ("same_row", np.arange(P) // COLS)):
        member = (group[None, :] == np.arange(8)[:, None]).astype(np.float64)
        left = np.concatenate([np.ones((1, P)), member])
        right = np.concatenate([-BIG * np.ones((1, P)), BIG * member])
        parts[name + "_l"] = np.pad(left, ((0, P - 9), (0, 0)))
        parts[name + "_r"] = np.pad(right, ((0, P - 9), (0, 0)))
    pick = np.repeat(np.eye(IMAGES), P, axis=1)
    parts["pick"] = np.pad(pick, ((0, P - IMAGES), (0, 0)))
    at, where, arrays = 0, {}, []
    for name, a in parts.items():
        a = np.asarray(a, np.float32)
        where[name] = (at, a.shape[1])
        at += a.shape[1]
        arrays.append(a)
    return np.ascontiguousarray(np.concatenate(arrays, 1)), where


class Chain:

    def __init__(self, eng, sem):
        self.eng, self.sem, self.n = eng, sem, 0

    def __call__(self, ins):
        ins.then_inc(self.sem, 1)
        self.n = self.n + 1
        self.eng.wait_ge(self.sem, self.n)


def build(nc, A, out, upto=4):
    _, where = constants()
    ctx = ExitStack()
    with ctx:
        live = []

        def sem(name):
            live.append(nc.alloc_semaphore(name=name))
            return live[-1]

        def clear_semaphores():
            nc.clear_and_free_semaphores(live)
            live.clear()
            nc.all_engine_barrier()

        def sb(name, shape, dt=F32, on=ctx):
            return on.enter_context(nc.sbuf_tensor(name, shape, dt))

        def pb(name, width, on=ctx):
            return on.enter_context(nc.psum_tensor(name, [P, width], F32))

        konst = sb("konst_sb", [P, sum(w for _, w in where.values())])

        def K(name, parts=P):
            at, w = where[name]
            return konst[0:parts, at:at + w]

        x_res = sb("x_res", [P, TILES * C])
        h_dram = nc.dram_tensor("h_rows", (TOKENS, C), F32, kind="Internal").ap()
        y_dram = nc.dram_tensor("y_rows", (SLOT_TILES * P, C), F32, kind="Internal").ap()

        router0 = sb("router0_sb", [P, KC * E])
        stats = sb("stats", [P, CHUNK_T * 6])
        mean = sb("mean", [P, CHUNK_T])
        var_eps = sb("var_eps", [P, CHUNK_T])
        sqrt_v = sb("sqrt_v", [P, CHUNK_T])
        rstd = sb("rstd", [P, CHUNK_T])
        newton = sb("newton", [P, CHUNK_T])
        xn = [sb(f"xn{b}", [P, HALVES * C]) for b in range(RING)]

        w_top = sb("w_top", [P, 2 * TILES])
        pos_i = sb("pos_i", [P, 2 * TILES], I32)
        ids_i = sb("ids_i", [P, SLOT_TILES], I32)
        etile_i = sb("etile_i", [1, SLOT_TILES], I32)

        moe0 = ExitStack()
        gate0 = sb("gate0", [P, E * KC * I0], on=moe0)
        up0 = sb("up0", [P, E * KC * I0], on=moe0)
        down0 = sb("down0", [P, E * (I0 // P) * C], on=moe0)

        loads = {n: nc.alloc_semaphore(name=f"loaded_{n}") for n in ("konst", "x", "spectral", "router0", "w0", "router1", "w1", "ws", "conv", "attn")}

        def x_tile(j, width=C, n=1):
            return x_res[:, bass.ds(j * C, n * C)]

        def layer_norm(dve, chain, s, eps):
            at = chain.n
            per = 3 + 5
            st = stats[:, :].rearrange("p (t f) -> p t f", f=6)
            with dve.Fori(0, CHUNKS) as c:
                chain.n = c * per + at
                for t in range(CHUNK_T):
                    last = nc.vector.bn_stats(stats[:, 6 * t:6 * t + 6], x_tile(c * CHUNK_T + t))
                chain(last)
                nc.vector.tensor_tensor(mean[:, :], st[:, :, 1], st[:, :, 4], ALU.add)
                nc.vector.tensor_tensor(newton[:, :], st[:, :, 1], st[:, :, 4], ALU.subtract)
                chain(nc.vector.tensor_tensor(var_eps[:, :], st[:, :, 2], st[:, :, 5], ALU.add))
                nc.vector.tensor_scalar(mean[:, :], mean[:, :], 0.5, None, ALU.mult)
                nc.vector.tensor_scalar(var_eps[:, :], var_eps[:, :], 1.0 / C, eps, ALU.mult, ALU.add)
                chain(nc.vector.scalar_tensor_tensor(out=newton[:, :], in0=newton[:, :], scalar=0.25, in1=newton[:, :],
                                                     op0=ALU.mult, op1=ALU.mult))
                nc.vector.tensor_tensor(var_eps[:, :], var_eps[:, :], newton[:, :], ALU.add).then_inc(s["var"], 1)
                dve.wait_ge(s["sqrt"], c + 1)
                chain(nc.vector.reciprocal(rstd[:, :], sqrt_v[:, :]))
                chain(nc.vector.tensor_tensor(newton[:, :], var_eps[:, :], rstd[:, :], ALU.mult))
                chain(nc.vector.tensor_tensor(newton[:, :], newton[:, :], rstd[:, :], ALU.mult))
                chain(nc.vector.tensor_scalar(newton[:, :], newton[:, :], -0.5, 1.5, ALU.mult, ALU.add))
                chain(nc.vector.tensor_tensor(rstd[:, :], rstd[:, :], newton[:, :], ALU.mult))
                for i in range(CHUNK_T // HALVES):
                    n = c * (CHUNK_T // HALVES) + i
                    dve.wait_ge(s["transposed"], n + 1)
                    if "stored" in s:
                        dve.wait_ge(s["stored"][i % RING], (c * (CHUNK_T // HALVES // RING) + i // RING + 1) * 16)
                    for h in range(HALVES):
                        t = i * HALVES + h
                        last = nc.vector.tensor_scalar(
                            xn[i % RING][:, h * C:(h + 1) * C], x_tile(n * HALVES + h),
                            mean[:, t:t + 1], rstd[:, t:t + 1], ALU.subtract, ALU.mult)
                    last.then_inc(s["xn"], 1)
            chain.n = at + CHUNKS * per

        def layer_norm_sqrt(act, s, c):
            act.wait_ge(s["var"], c + 1)
            nc.scalar.activation(sqrt_v[:, :], var_eps[:, :], ACT.Sqrt).then_inc(s["sqrt"], 1)

        def transpose_image(pe, s, n, b, bank):
            pe.wait_ge(s["xn"], n + 1)
            pe.wait_ge(s["copied"], n + 1)
            for kc in range(KC):
                for h in range(HALVES):
                    last = nc.tensor.transpose(bank[:, (kc * HALVES + h) * P:(kc * HALVES + h + 1) * P],
                                               xn[b][:, h * C + kc * P:h * C + (kc + 1) * P], K("ident"))
            last.then_inc(s["transposed"], 1)

        def router(tag, w_router, load):
            on = ExitStack()
            with on:
                s = {n: sem(f"{tag}_{n}") for n in ("var", "sqrt", "xn", "transposed", "copied", "logits", "chain", "shifted",
                                                    "exp", "totals", "bases", "one_hot", "spread", "filled")}
                s["stored"] = [sem(f"{tag}_stored{b}") for b in range(RING)]
                xT = [sb(f"{tag}_xT{b}", [P, KC * HALVES * P], on=on) for b in range(RING)]
                bankT = [pb(f"{tag}_bankT{b}", 512, on=on) for b in range(RING)]
                logits_ps = pb(f"{tag}_logits", TILES * E, on=on)
                sums_ps = pb(f"{tag}_sums", 2 * E, on=on)
                ids_ps = pb(f"{tag}_ids", SLOT_TILES, on=on)
                prob = sb(f"{tag}_prob", [P, TILES * E], on=on)
                work = sb(f"{tag}_work", [P, TILES * E], on=on)
                one_hot = [sb(f"{tag}_choice{k}", [P, TILES * E], on=on) for k in range(2)]
                chosen = sb(f"{tag}_chosen", [P, TILES * E], on=on)
                count = sb(f"{tag}_count", [P, E * TILES], on=on)
                zeros = sb(f"{tag}_zeros", [P, SLOT_TILES], on=on)
                top = [sb(f"{tag}_top{k}", [P, TILES], on=on) for k in range(2)]
                row = sb(f"{tag}_row", [P, TILES], on=on)
                tiles_of = sb(f"{tag}_tiles_of", [P, E], on=on)
                ends = sb(f"{tag}_ends", [P, E], on=on)
                offset = sb(f"{tag}_offset", [P, E], on=on)
                pos = sb(f"{tag}_pos", [P, 2 * TILES], on=on)
                slot_tile = sb(f"{tag}_slot_tile", [P, 2 * TILES], on=on)
                slot_row = sb(f"{tag}_slot_row", [P, 2 * TILES], on=on)
                token = sb(f"{tag}_token", [P, TILES], on=on)
                past = sb(f"{tag}_past", [1, SLOT_TILES * E], on=on)
                etile = sb(f"{tag}_etile", [1, SLOT_TILES], on=on)
                at_row = [sb(f"{tag}_at_row{k}", [P, P], on=on) for k in range(2)]
                at_tile = [sb(f"{tag}_at_tile{k}", [P, SLOT_TILES], on=on) for k in range(2)]
                block = on.enter_context(nc.Block())

                @block.sync
                def _(sp):
                    rows = h_dram.rearrange("(j p) c -> p j c", p=P)
                    for b in range(RING):
                        sp.sem_inc(s["stored"][b], 16)
                    with sp.Fori(0, IMAGES // RING) as q:
                        for b in range(RING):
                            n = q * RING + b
                            sp.wait_ge(s["xn"], n + 1)
                            sp.dma_start(rows[:, bass.ds(n * HALVES, HALVES), :],
                                         xn[b][:, :].rearrange("p (h c) -> p h c", c=C)).then_inc(s["stored"][b], 16)
                    for b in range(RING):
                        sp.wait_ge(s["stored"][b], IMAGES // RING * 16 + 16)

                @block.scalar
                def _(act):
                    act.sem_inc(s["copied"], RING)
                    with act.Fori(0, CHUNKS) as c:
                        layer_norm_sqrt(act, s, c)
                        for i in range(CHUNK_T // HALVES):
                            n = c * (CHUNK_T // HALVES) + i
                            act.wait_ge(s["transposed"], n + 1 + RING)
                            act.wait_ge(s["logits"], n + 1)
                            nc.scalar.activation(xT[i % RING][:, :], bankT[i % RING][:, :], ACT.Copy).then_inc(s["copied"], 1)
                    act.wait_ge(s["shifted"], 1)
                    nc.scalar.activation(work[:, :], prob[:, :], ACT.Exp).then_inc(s["exp"], 1)

                @block.tensor
                def _(pe):
                    pe.sem_inc(s["transposed"], RING)
                    pe.sem_inc(s["logits"], RING)
                    pe.sem_inc(s["spread"], RING)
                    pe.wait_ge(loads[load], 16)
                    with pe.Fori(0, IMAGES // RING) as q:
                        for b in range(RING):
                            transpose_image(pe, s, q * RING + b, b, bankT[b])
                        for b in range(RING):
                            n = q * RING + b
                            pe.wait_ge(s["copied"], n + 1 + RING)
                            for h in range(HALVES):
                                for kc in range(KC):
                                    last = nc.tensor.matmul(logits_ps[:, bass.ds((n * HALVES + h) * E, E)],
                                                            xT[b][:, (kc * HALVES + h) * P:(kc * HALVES + h + 1) * P],
                                                            w_router[:, kc * E:(kc + 1) * E], start=(kc == 0), stop=(kc == KC - 1))
                            last.then_inc(s["logits"], 1)
                    pe.wait_ge(s["totals"], 1)
                    totals = count[:, :].rearrange("p (e j) -> p e j", e=E)[:, :, TILES - 1]
                    nc.tensor.matmul(sums_ps[:, 0:E], K("before"), totals, start=True, stop=True)
                    nc.tensor.matmul(sums_ps[:, E:2 * E], K("ones"), totals, start=True, stop=True).then_inc(s["bases"], 1)
                    nc.tensor.matmul(ids_ps[:, :], K("ident"), zeros[:, :], start=True, stop=False)
                    with pe.Fori(0, TILES) as j:
                        for k in range(2):
                            pe.wait_ge(s["one_hot"], j * 2 + k + 1)
                            nc.tensor.matmul(ids_ps[:, :], at_row[k][:, :], at_tile[k][:, :],
                                             start=False, stop=False).then_inc(s["spread"], 1)
                    nc.tensor.matmul(ids_ps[:, :], K("ident"), zeros[:, :], start=False, stop=True).then_inc(s["filled"], 1)

                @block.vector
                def _(dve):
                    chain = Chain(dve, s["chain"])
                    chain(nc.vector.memset(zeros[:, :], 0.0))
                    layer_norm(dve, chain, s, 1e-5)

                    def by_token(t):
                        return t[:, :].rearrange("p (j e) -> p j e", e=E)

                    def over_e(t):
                        return t.unsqueeze(2).broadcast_to([P, TILES, E])

                    def over_j(t):
                        return t.unsqueeze(1).broadcast_to([P, TILES, E])
                    dve.wait_ge(s["logits"], IMAGES + RING)
                    chain(nc.vector.reduce_max(row[:, :], by_token(logits_ps), AX_X))
                    nc.vector.tensor_tensor(by_token(prob), by_token(logits_ps), over_e(row[:, :]), ALU.subtract).then_inc(s["shifted"], 1)
                    dve.wait_ge(s["exp"], 1)
                    chain(nc.vector.reduce_sum(row[:, :], by_token(work), AX_X))
                    chain(nc.vector.reciprocal(row[:, :], row[:, :]))
                    chain(nc.vector.tensor_tensor(by_token(prob), by_token(work), over_e(row[:, :]), ALU.mult))
                    for k in range(2):
                        chain(nc.vector.reduce_max(top[k][:, :], by_token(prob), AX_X))
                        chain(nc.vector.tensor_tensor(by_token(work), by_token(prob), over_e(top[k][:, :]), ALU.is_equal))
                        chain(nc.vector.tensor_tensor(by_token(work), by_token(work), over_j(K("first_wins")), ALU.mult))
                        chain(nc.vector.reduce_max(row[:, :], by_token(work), AX_X))
                        chain(nc.vector.tensor_tensor(by_token(one_hot[k]), by_token(work), over_e(row[:, :]), ALU.is_equal))
                        if k == 0:
                            chain(nc.vector.scalar_tensor_tensor(out=prob[:, :], in0=one_hot[0][:, :], scalar=-2.0, in1=prob[:, :],
                                                                 op0=ALU.mult, op1=ALU.add))
                    chain(nc.vector.tensor_tensor(row[:, :], top[0][:, :], top[1][:, :], ALU.add))
                    chain(nc.vector.reciprocal(row[:, :], row[:, :]))
                    for k in range(2):
                        chain(nc.vector.tensor_tensor(w_top[:, k * TILES:(k + 1) * TILES], top[k][:, :], row[:, :], ALU.mult))
                    chain(nc.vector.tensor_tensor(chosen[:, :], one_hot[0][:, :], one_hot[1][:, :], ALU.add))
                    for e in range(E):
                        last = nc.vector.tensor_tensor_scan(count[:, e * TILES:(e + 1) * TILES], zeros[:, 0:TILES],
                                                            by_token(chosen)[:, :, e], 0.0, ALU.add, ALU.add)
                    last.then_inc(s["totals"], 1)
                    dve.wait_ge(s["bases"], 1)
                    chain(nc.vector.tensor_scalar(tiles_of[:, :], sums_ps[:, E:2 * E], 1.0 / P, (P - 1) / P - 0.5 + 0.5 / P, ALU.mult, ALU.add))
                    chain(nc.vector.tensor_scalar(tiles_of[:, :], tiles_of[:, :], ROUND, None, ALU.add))
                    chain(nc.vector.tensor_scalar(tiles_of[:, :], tiles_of[:, :], -ROUND, None, ALU.add))
                    chain(nc.vector.tensor_tensor_scan(ends[:, :], zeros[:, 0:E], tiles_of[:, :], 0.0, ALU.add, ALU.add))
                    chain(nc.vector.tensor_tensor(offset[:, :], ends[:, :], tiles_of[:, :], ALU.subtract))
                    chain(nc.vector.tensor_scalar(offset[:, :], offset[:, :], float(P), -1.0, ALU.mult, ALU.add))
                    chain(nc.vector.tensor_tensor(offset[:, :], offset[:, :], sums_ps[:, 0:E], ALU.add))
                    chain(nc.vector.tensor_tensor(by_token(chosen), count[:, :].rearrange("p (e j) -> p j e", e=E),
                                                  over_j(offset[:, :]), ALU.add))
                    for k in range(2):
                        chain(nc.vector.tensor_tensor(work[:, :], one_hot[k][:, :], chosen[:, :], ALU.mult))
                        chain(nc.vector.reduce_sum(pos[:, k * TILES:(k + 1) * TILES], by_token(work), AX_X))
                    nc.vector.tensor_copy(pos_i[:, :], pos[:, :])
                    chain(nc.vector.tensor_scalar(slot_tile[:, :], pos[:, :], 1.0 / P, -0.5 + 0.5 / P, ALU.mult, ALU.add))
                    chain(nc.vector.tensor_scalar(slot_tile[:, :], slot_tile[:, :], ROUND, None, ALU.add))
                    chain(nc.vector.tensor_scalar(slot_tile[:, :], slot_tile[:, :], -ROUND, None, ALU.add))
                    chain(nc.vector.scalar_tensor_tensor(out=slot_row[:, :], in0=slot_tile[:, :], scalar=-float(P), in1=pos[:, :],
                                                         op0=ALU.mult, op1=ALU.add))
                    pe3 = past[:, :].rearrange("p (s e) -> p s e", e=E)
                    chain(nc.vector.tensor_tensor(pe3, K("ramp", 1)[:, 0:SLOT_TILES].unsqueeze(2).broadcast_to([1, SLOT_TILES, E]),
                                                  ends[0:1, :].unsqueeze(1).broadcast_to([1, SLOT_TILES, E]), ALU.is_ge))
                    chain(nc.vector.reduce_sum(etile[:, :], pe3, AX_X))
                    chain(nc.vector.tensor_scalar(etile_i[:, :], etile[:, :], float(E - 1), None, ALU.min))
                    chain(nc.vector.tensor_scalar(token[:, :], K("tile_base"), K("column"), None, ALU.add))
                    with dve.Fori(0, TILES) as j:
                        for k in range(2):
                            dve.wait_ge(s["spread"], j * 2 + k + 1)
                            nc.vector.tensor_scalar(at_row[k][:, :], K("ramp"), slot_row[:, bass.ds(j + k * TILES, 1)], None, ALU.is_equal)
                            nc.vector.tensor_scalar(at_tile[k][:, :], K("ramp")[:, 0:SLOT_TILES], slot_tile[:, bass.ds(j + k * TILES, 1)],
                                                    token[:, bass.ds(j, 1)], ALU.is_equal, ALU.mult).then_inc(s["one_hot"], 1)
                    dve.wait_ge(s["filled"], 1)
                    chain(nc.vector.tensor_copy(ids_i[:, :], ids_ps[:, :]))

        def mlp(tag, n_tiles, hidden, up, down, gate=None, load=(), experts=True):
            KI = hidden // P
            DEPTH = 4
            first = gate if gate is not None else up
            on = ExitStack()
            with on:
                s = {n: sem(f"{tag}_{n}") for n in ("h_turned", "h_copied", "gated", "up", "act", "a", "a_turned", "a_copied", "down", "y_copied")}
                s_rows = [sem(f"{tag}_rows{g}") for g in range(DEPTH)]
                s_stored = [sem(f"{tag}_stored{b}") for b in range(RING)]
                rows = [sb(f"{tag}_rows_sb{g}", [P, C], on=on) for g in range(DEPTH)]
                hT = [sb(f"{tag}_hT{b}", [P, C], on=on) for b in range(RING)]
                act_sb = [sb(f"{tag}_act_sb{b}", [P, hidden], on=on) for b in range(RING)]
                a_sb = [sb(f"{tag}_a_sb{b}", [P, hidden], on=on) for b in range(RING)]
                aT = [sb(f"{tag}_aT{b}", [P, hidden], on=on) for b in range(RING)]
                y_sb = [sb(f"{tag}_y_sb{b}", [P, C], on=on) for b in range(RING)]
                bankH = pb(f"{tag}_bankH", 512, on=on)
                bankA = pb(f"{tag}_bankA", 512, on=on)
                bankG = [pb(f"{tag}_bankG{b}", 512, on=on) for b in range(RING)]
                bankU = [pb(f"{tag}_bankU{b}", 512, on=on) for b in range(RING)] if gate is not None else bankG
                bankY = [pb(f"{tag}_bankY{b}", 512, on=on) for b in range(RING)]
                block = on.enter_context(nc.Block())

                if experts:
                    @block.gpsimd
                    def _(pool):
                        for t in range(n_tiles):
                            if t >= DEPTH:
                                pool.wait_ge(s["h_turned"], t - DEPTH + 1)
                            nc.gpsimd.indirect_dma_start(rows[t % DEPTH][:, :], None, h_dram,
                                                         bass.IndirectOffsetOnAxis(ap=ids_i[:, t:t + 1], axis=0)).then_inc(s_rows[t % DEPTH], 16)

                @block.sync
                def _(sp):
                    if not experts:
                        for g in range(DEPTH):
                            sp.dma_start(rows[g][:, :], h_dram[g * P:(g + 1) * P, :]).then_inc(s_rows[g], 16)
                        with sp.Fori(1, n_tiles // DEPTH) as q:
                            for g in range(DEPTH):
                                sp.wait_ge(s["h_turned"], (q - 1) * DEPTH + g + 1)
                                sp.dma_start(rows[g][:, :], h_dram[bass.ds((q * DEPTH + g) * P, P), :]).then_inc(s_rows[g], 16)
                    else:
                        for b in range(RING):
                            sp.sem_inc(s_stored[b], 16)
                        with sp.Fori(0, n_tiles // RING) as q:
                            for b in range(RING):
                                sp.wait_ge(s["y_copied"], q * RING + b + 1 + RING)
                                sp.dma_start(y_dram[bass.ds((q * RING + b) * P, P), :], y_sb[b][:, :]).then_inc(s_stored[b], 16)
                        for b in range(RING):
                            sp.wait_ge(s_stored[b], n_tiles // RING * 16 + 16)

                @block.tensor
                def _(pe):
                    pe.sem_inc(s["up"], RING)
                    pe.sem_inc(s["a_turned"], RING)
                    pe.sem_inc(s["down"], RING)
                    for name, value in load:
                        pe.wait_ge(loads[name], value)

                    def turn_h(t, i):
                        pe.wait_ge(s_rows[i % DEPTH], (t - i) * (16 // DEPTH) + (i // DEPTH + 1) * 16)
                        pe.wait_ge(s["h_copied"], t + 1)
                        for kc in range(KC):
                            last = nc.tensor.transpose(bankH[:, kc * P:(kc + 1) * P], rows[i % DEPTH][:, kc * P:(kc + 1) * P], K("ident"))
                        last.then_inc(s["h_turned"], 1)

                    def turn_a(t, i):
                        pe.wait_ge(s["a"], t + 1 + RING)
                        pe.wait_ge(s["a_copied"], t + 1)
                        for k in range(KI):
                            last = nc.tensor.transpose(bankA[:, k * P:(k + 1) * P], a_sb[i % RING][:, k * P:(k + 1) * P], K("ident"))
                        last.then_inc(s["a_turned"], 1)

                    def expert(t):
                        return pe.value_load(etile_i[0:1, bass.ds(t, 1)], min_val=0, max_val=E - 1) if experts else 0

                    def project(t, i):
                        e = expert(t)
                        pe.wait_ge(s["h_copied"], t + 2)
                        pe.wait_ge(s["a"], t + 1)
                        for w, bank, done in ((gate, bankG, "gated"), (up, bankU, "up")):
                            if w is None:
                                continue
                            for kc in range(KC):
                                last = nc.tensor.matmul(bank[i % RING][:, 0:hidden], hT[i % RING][:, kc * P:(kc + 1) * P],
                                                        w[:, bass.ds((e * KC + kc) * hidden, hidden)], start=(kc == 0), stop=(kc == KC - 1))
                            last.then_inc(s[done], 1)

                    def project_back(t, i):
                        e = expert(t)
                        pe.wait_ge(s["a_copied"], t + 2)
                        pe.wait_ge(s["y_copied"], t + 1)
                        for k in range(KI):
                            last = nc.tensor.matmul(bankY[i % RING][:, 0:C], aT[i % RING][:, k * P:(k + 1) * P],
                                                    down[:, bass.ds((e * KI + k) * C, C)], start=(k == 0), stop=(k == KI - 1))
                        last.then_inc(s["down"], 1)

                    turn_h(0, 0)
                    project(0, 0)
                    turn_h(1, 1)
                    turn_a(0, 0)
                    rounds = (n_tiles - 2) // DEPTH

                    def step(t, i, last=False):
                        project(t, i)
                        if not last:
                            turn_h(t + 1, i + 1)
                        project_back(t - 1, i - 1)
                        turn_a(t, i)
                    with pe.Fori(0, rounds) as q:
                        for i in range(1, DEPTH + 1):
                            step(q * DEPTH + i, i)
                    for t in range(rounds * DEPTH + 1, n_tiles):
                        step(t, t, t == n_tiles - 1)
                    project_back(n_tiles - 1, n_tiles - 1)

                @block.scalar
                def _(act):
                    act.sem_inc(s["h_copied"], 1)
                    act.sem_inc(s["y_copied"], RING)

                    def copy_h(t, i):
                        act.wait_ge(s["h_turned"], t + 1)
                        act.wait_ge(s["up"], t + 1)
                        nc.scalar.activation(hT[i % RING][:, :], bankH[:, 0:C], ACT.Copy).then_inc(s["h_copied"], 1)

                    def activate(t, i):
                        if gate is not None:
                            act.wait_ge(s["gated"], t + 1)
                        else:
                            act.wait_ge(s["up"], t + 1 + RING)
                        act.wait_ge(s["a"], t + 1)
                        nc.scalar.activation(act_sb[i % RING][:, :], bankG[i % RING][:, 0:hidden],
                                             ACT.Silu if gate is not None else ACT.Relu).then_inc(s["act"], 1)

                    def copy_y(t, i):
                        act.wait_ge(s["down"], t + 1 + RING)
                        act.wait_ge(s_stored[i % RING], (t - i) * (16 // RING) + i // RING * 16 + 16)
                        nc.scalar.activation(y_sb[i % RING][:, :], bankY[i % RING][:, 0:C], ACT.Copy).then_inc(s["y_copied"], 1)

                    copy_h(0, 0)
                    activate(0, 0)
                    copy_h(1, 1)
                    rounds = (n_tiles - 2) // DEPTH

                    def step(t, i, last=False):
                        activate(t, i)
                        if not last:
                            copy_h(t + 1, i + 1)
                        if experts:
                            copy_y(t - 1, i - 1)
                    with act.Fori(0, rounds) as q:
                        for i in range(1, DEPTH + 1):
                            step(q * DEPTH + i, i)
                    for t in range(rounds * DEPTH + 1, n_tiles):
                        step(t, t, t == n_tiles - 1)
                    if experts:
                        copy_y(n_tiles - 1, n_tiles - 1)

                @block.vector
                def _(dve):
                    dve.sem_inc(s["a"], RING)
                    dve.sem_inc(s["a_copied"], 1)

                    def multiply(t, i):
                        dve.wait_ge(s["act"], t + 1)
                        dve.wait_ge(s["up"], t + 1 + RING)
                        dve.wait_ge(s["a_turned"], t + 1)
                        nc.vector.tensor_tensor(a_sb[i % RING][:, :], act_sb[i % RING][:, :], bankU[i % RING][:, 0:hidden],
                                                ALU.mult).then_inc(s["a"], 1)

                    def copy_a(t, i):
                        dve.wait_ge(s["a_turned"], t + 1 + RING)
                        dve.wait_ge(s["down"], t + 1)
                        nc.vector.tensor_copy(aT[i % RING][:, :], bankA[:, 0:hidden]).then_inc(s["a_copied"], 1)

                    def add_y(t, i):
                        dve.wait_ge(s["down"], t + 1 + RING)
                        nc.vector.tensor_tensor(x_tile(t), x_tile(t), bankY[i % RING][:, 0:C], ALU.add).then_inc(s["y_copied"], 1)

                    multiply(0, 0)
                    copy_a(0, 0)
                    rounds = (n_tiles - 2) // DEPTH

                    def step(t, i):
                        multiply(t, i)
                        if not experts:
                            add_y(t - 1, i - 1)
                        copy_a(t, i)
                    with dve.Fori(0, rounds) as q:
                        for i in range(1, DEPTH + 1):
                            step(q * DEPTH + i, i)
                    for t in range(rounds * DEPTH + 1, n_tiles):
                        step(t, t)
                    if not experts:
                        add_y(n_tiles - 1, n_tiles - 1)

        def combine(tag):
            on = ExitStack()
            with on:
                DEPTH = 4
                s_in = [sem(f"{tag}_in{g}") for g in range(DEPTH)]
                s_used = sem(f"{tag}_used")
                s_chain = sem(f"{tag}_chain")
                y_in = [sb(f"{tag}_y{g}", [P, C], on=on) for g in range(DEPTH)]
                block = on.enter_context(nc.Block())

                @block.gpsimd
                def _(pool):
                    for j in range(TILES):
                        for k in range(2):
                            u = j * 2 + k
                            if u >= DEPTH:
                                pool.wait_ge(s_used, u - DEPTH + 2)
                            nc.gpsimd.indirect_dma_start(
                                y_in[u % DEPTH][:, :], None, y_dram,
                                bass.IndirectOffsetOnAxis(ap=pos_i[:, j + k * TILES:j + k * TILES + 1], axis=0)).then_inc(s_in[u % DEPTH], 16)

                @block.vector
                def _(dve):
                    dve.sem_inc(s_used, 1)
                    with dve.Fori(0, TILES // RING) as q:
                        for b in range(RING):
                            for k in range(2):
                                j = q * RING + b
                                dve.wait_ge(s_in[b * 2 + k], q * 16 + 16)
                                dve.wait_ge(s_used, q * 4 + b * 2 + k + 1)
                                nc.vector.scalar_tensor_tensor(out=x_tile(j), in0=y_in[b * 2 + k][:, :],
                                                               scalar=w_top[:, bass.ds(j + k * TILES, 1)], in1=x_tile(j),
                                                               op0=ALU.mult, op1=ALU.add).then_inc(s_used, 1)

        def entry_convolution():
            on = ExitStack()
            with on:
                W2 = COLS + 2
                IMG = (ROWS + 2) * W2
                s = {n: sem(f"conv_{n}") for n in ("var", "sqrt", "xn", "transposed", "copied", "border", "chain", "conv", "feat", "pooled")}
                bankT = [pb(f"conv_bankT{b}", 512, on=on) for b in range(RING)]
                bankC = [pb(f"conv_bankC{b}", 512, on=on) for b in range(RING)]
                pool_ps = pb("conv_pool", KC * IMAGES, on=on)
                padded = sb("conv_padded", [P, KC * IMAGES * IMG], on=on)
                block = on.enter_context(nc.Block())

                @block.gpsimd
                def _(pool):
                    nc.gpsimd.memset(padded[:, :], 0.0).then_inc(s["border"], 1)

                @block.scalar
                def _(act):
                    act.sem_inc(s["copied"], RING)
                    act.sem_inc(s["feat"], 1)
                    act.wait_ge(s["border"], 1)

                    def copy(n, b):
                        act.wait_ge(s["transposed"], n + 1 + RING)
                        for kc in range(KC):
                            inner = padded[:, bass.ds(kc * IMAGES * IMG + n * IMG, IMG)].rearrange("p (r c) -> p r c", c=W2)
                            last = nc.scalar.activation(inner[:, 1:ROWS + 1, 1:COLS + 1],
                                                        bankT[b][:, kc * 256:(kc + 1) * 256].rearrange("p (r c) -> p r c", c=COLS), ACT.Copy)
                        last.then_inc(s["copied"], 1)

                    def relu(g, b):
                        act.wait_ge(s["conv"], g + 1)
                        nc.scalar.activation(feat[:, bass.ds(g * 512, 512)], bankC[b][:, :], ACT.Relu,
                                             bias=entry_sb[:, 1:2], scale=entry_sb[:, 0:1]).then_inc(s["feat"], 1)

                    def chunk(c, first=False, last=False):
                        copy(c * 4, 0)
                        copy(c * 4 + 1, 1)
                        if not first:
                            relu(c * 2 - 1, 1)
                        copy(c * 4 + 2, 0)
                        copy(c * 4 + 3, 1)
                        if not last:
                            layer_norm_sqrt(act, s, c + 1)
                        relu(c * 2, 0)
                    layer_norm_sqrt(act, s, 0)
                    chunk(0, first=True)
                    with act.Fori(1, CHUNKS - 1) as c:
                        chunk(c)
                    chunk(CHUNKS - 1, last=True)
                    relu(CHUNKS * 2 - 1, 1)

                @block.vector
                def _(dve):
                    chain = Chain(dve, s["chain"])
                    layer_norm(dve, chain, s, 1e-6)
                    dve.wait_ge(s["pooled"], IMAGES)
                    chain(nc.vector.tensor_scalar(pooled[:, :], pool_ps[:, :], 1.0 / (ROWS * COLS), None, ALU.mult))

                @block.tensor
                def _(pe):
                    pe.sem_inc(s["transposed"], RING)
                    pe.wait_ge(loads["conv"], 16 * 2)

                    def turn(n, b):
                        pe.wait_ge(s["xn"], n + 1)
                        for kc in range(KC):
                            for h in range(HALVES):
                                last = nc.tensor.matmul(pool_ps[:, bass.ds(kc * IMAGES + n, 1)], xn[b][:, h * C + kc * P:h * C + (kc + 1) * P],
                                                        K("ones")[:, 0:1], start=(h == 0), stop=(h == HALVES - 1))
                        last.then_inc(s["pooled"], 1)
                        transpose_image(pe, s, n, b, bankT[b])

                    def convolve(g, b):
                        pe.wait_ge(s["copied"], g * 2 + 2 + RING)
                        pe.wait_ge(s["feat"], g)
                        step = 0
                        for kc in range(KC):
                            pair = padded[:, bass.ds(kc * IMAGES * IMG + g * 2 * IMG, 2 * IMG)].rearrange("p (n r c) -> p n r c", n=2, c=W2)
                            for dr in range(3):
                                for dc in range(3):
                                    last = nc.tensor.matmul(bankC[b][:, :], conv_w[:, ((dr * 3 + dc) * KC + kc) * F:((dr * 3 + dc) * KC + kc + 1) * F],
                                                            pair[:, :, dr:dr + ROWS, dc:dc + COLS], start=(step == 0), stop=(step == 17))
                                    step += 1
                        last.then_inc(s["conv"], 1)
                    turn(0, 0)
                    turn(1, 1)
                    turn(2, 0)
                    turn(3, 1)
                    convolve(0, 0)
                    with pe.Fori(0, (IMAGES // 2 - 2) // 2) as r:
                        for b in range(2):
                            g = r * 2 + b + 1
                            turn(g * 2 + 2, 0)
                            turn(g * 2 + 3, 1)
                            convolve(g, 1 - b)
                    convolve(IMAGES // 2 - 1, 1)

        def axial_scores():
            on = ExitStack()
            with on:
                STEPS = IMAGES // 2
                names = ("projected", "queries", "values_t", "values", "chain", "att")
                s = {n: sem(f"axial_{n}") for n in names}
                for ax in ("down", "along"):
                    for n in ("scores", "max", "exp", "soft", "turned", "turned_sb"):
                        s[n, ax] = sem(f"axial_{n}_{ax}")
                s["att_sb"] = sem("axial_att_sb")
                bankQ, bankF, bankV, bankO = (pb(f"axial_{n}", 512, on=on) for n in ("bankQ", "bankF", "bankV", "bankO"))
                bankS = {ax: pb(f"axial_bankS_{ax}", 512, on=on) for ax in ("down", "along")}
                bankP = {ax: pb(f"axial_bankP_{ax}", 512, on=on) for ax in ("down", "along")}
                q = {ax: [sb(f"axial_q_{ax}{b}", [G, 512], on=on) for b in range(RING)] for ax in ("down", "along")}
                val_t = [sb(f"axial_val_t{b}", [F, 512], on=on) for b in range(RING)]
                val = [sb(f"axial_val{b}", [P, 512], on=on) for b in range(RING)]
                expo = {ax: [sb(f"axial_exp_{ax}{b}", [P, 512], on=on) for b in range(RING)] for ax in ("down", "along")}
                nmax = {ax: sb(f"axial_nmax_{ax}", [P, 4], on=on) for ax in ("down", "along")}
                total = {ax: sb(f"axial_total_{ax}", [P, 4], on=on) for ax in ("down", "along")}
                att_down = sb("axial_att_down", [P, 512], on=on)
                mask = {"down": "same_col", "along": "same_row"}
                block = on.enter_context(nc.Block())

                def by_column(image):
                    return image.rearrange("p (y h z) -> p h y z", y=ROWS, h=2)

                def steps(eng, step):
                    step(0, 0, first=True)
                    with eng.Fori(0, (STEPS - 2) // 2) as r:
                        step(r * 2 + 1, 1)
                        step(r * 2 + 2, 0)
                    step(STEPS - 1, (STEPS - 1) % 2, last=True)

                @block.tensor
                def _(pe):
                    pe.sem_inc(s["values_t"], RING)
                    pe.wait_ge(loads["attn"], ATTN_LOADS * 16)

                    def project(g):
                        pe.wait_ge(s["queries"], g)
                        nc.tensor.matmul(bankQ[0:64, :], qk_w[:, :], feat[:, bass.ds(g * 512, 512)], start=True, stop=True)
                        nc.tensor.matmul(bankF[:, :], val_w[:, :], feat[:, bass.ds(g * 512, 512)],
                                         start=True, stop=True).then_inc(s["projected"], 1)

                    def scores(g, b):
                        pe.wait_ge(s["queries"], g + 1)
                        for ax in ("down", "along"):
                            pe.wait_ge(s["exp", ax], g)
                            for t in range(4):
                                qt = q[ax][b][:, t * P:(t + 1) * P]
                                nc.tensor.matmul(bankS[ax][:, t * P:(t + 1) * P], K(mask[ax] + "_l", 9), K(mask[ax] + "_r", 9), start=True, stop=False)
                                last = nc.tensor.matmul(bankS[ax][:, t * P:(t + 1) * P], qt, qt, start=False, stop=True)
                            last.then_inc(s["scores", ax], 1)
                        pe.wait_ge(s["values"], g)
                        for t in range(4):
                            last = nc.tensor.transpose(bankV[:, t * P:(t + 1) * P], val_t[b][:, t * P:(t + 1) * P], K("ident"))
                        last.then_inc(s["values_t"], 1)

                    def attend(g, b):
                        for ax in ("down", "along"):
                            pe.wait_ge(s["soft", ax], g + 1)
                            pe.wait_ge(s["turned_sb", ax], g)
                            for t in range(4):
                                last = nc.tensor.transpose(bankP[ax][:, t * P:(t + 1) * P], expo[ax][b][:, t * P:(t + 1) * P], K("ident"))
                            last.then_inc(s["turned", ax], 1)
                        pe.wait_ge(s["turned_sb", "down"], g + 1)
                        pe.wait_ge(s["values"], g + 1)
                        pe.wait_ge(s["att_sb"], g)
                        for t in range(4):
                            last = nc.tensor.matmul(bankO[:, t * P:(t + 1) * P], val[b][:, t * P:(t + 1) * P],
                                                    att_down[:, t * P:(t + 1) * P], start=True, stop=True)
                        last.then_inc(s["att"], 1)

                    def step(g, b, first=False, last=False):
                        scores(g, b)
                        if not first:
                            attend(g - 1, 1 - b)
                        if not last:
                            project(g + 1)
                    project(0)
                    steps(pe, step)
                    attend(STEPS - 1, (STEPS - 1) % 2)

                @block.scalar
                def _(act):
                    def queries(g, b):
                        act.wait_ge(s["projected"], g + 1)
                        act.wait_ge(s["values_t"], g + 1)
                        for n in range(2):
                            part = slice(n * 256, (n + 1) * 256)
                            nc.scalar.activation(q["down"][b][:, part].rearrange("p (h y z) -> p h y z", h=2, y=ROWS),
                                                 by_column(bankQ[0:G, part]), ACT.Relu, bias=qk_sb[0:G, 1:2], scale=qk_sb[0:G, 0:1])
                            nc.scalar.activation(val_t[b][:, part].rearrange("p (h y z) -> p h y z", h=2, y=ROWS),
                                                 by_column(bankF[:, part]), ACT.Relu, bias=val_sb[:, 1:2], scale=val_sb[:, 0:1])
                        nc.scalar.activation(q["along"][b][:, :], bankQ[32:32 + G, :], ACT.Relu, bias=qk_sb[32:32 + G, 1:2],
                                             scale=qk_sb[32:32 + G, 0:1]).then_inc(s["queries"], 1)

                    def exponentials(g, b):
                        for ax in ("down", "along"):
                            act.wait_ge(s["max", ax], g + 1)
                            for t in range(4):
                                last = nc.scalar.activation(expo[ax][b][:, t * P:(t + 1) * P], bankS[ax][:, t * P:(t + 1) * P], ACT.Exp,
                                                            bias=nmax[ax][:, t:t + 1], accum_out=total[ax][:, t:t + 1])
                            last.then_inc(s["exp", ax], 1)

                    def step(g, b, first=False, last=False):
                        exponentials(g, b)
                        if not last:
                            queries(g + 1, 1 - b)
                    act.wait_ge(loads["attn"], ATTN_LOADS * 16)
                    queries(0, 0)
                    steps(act, step)

                @block.vector
                def _(dve):
                    chain = Chain(dve, s["chain"])

                    def copies(g, b):
                        dve.wait_ge(s["turned", "down"], g + 1)
                        nc.vector.tensor_copy(att_down[:, :], bankP["down"][:, :]).then_inc(s["turned_sb", "down"], 1)
                        dve.wait_ge(s["turned", "along"], g + 1)
                        nc.vector.tensor_copy(att_along[:, bass.ds(g * 512, 512)], bankP["along"][:, :]).then_inc(s["turned_sb", "along"], 1)
                        dve.wait_ge(s["att"], g + 1)
                        for n in range(2):
                            last = nc.vector.tensor_copy(by_column(att_t[:, bass.ds(g * 512 + n * 256, 256)]),
                                                         bankO[:, n * 256:(n + 1) * 256].rearrange("p (h y z) -> p h y z", h=2, y=ROWS))
                        last.then_inc(s["att_sb"], 1)

                    def step(g, b, first=False, last=False):
                        for ax in ("down", "along"):
                            dve.wait_ge(s["scores", ax], g + 1)
                            nc.vector.tensor_reduce(nmax[ax][:, :], bankS[ax][:, :].rearrange("p (t j) -> p t j", t=4), AX_X, ALU.max,
                                                    negate=True).then_inc(s["max", ax], 1)
                        dve.wait_ge(s["values_t"], g + 1 + RING)
                        nc.vector.tensor_copy(val[b][:, :], bankV[:, :]).then_inc(s["values"], 1)
                        if not first:
                            copies(g - 1, 1 - b)
                        for n, ax in enumerate(("down", "along")):
                            dve.wait_ge(s["exp", ax], g + 1)
                            chain.n = g * 2 + n
                            chain(nc.vector.reciprocal(total[ax][:, :], total[ax][:, :]))
                            e3 = expo[ax][b][:, :].rearrange("p (t j) -> p t j", t=4)
                            nc.vector.tensor_tensor(e3, e3, total[ax][:, :].unsqueeze(2).broadcast_to([P, 4, P]),
                                                    ALU.mult).then_inc(s["soft", ax], 1)
                    steps(dve, step)
                    copies(STEPS - 1, (STEPS - 1) % 2)

        def gate_network(on, tag, s, in_ps, sums, w0, wh, we, gate):
            hidden = [sb(f"{tag}_hidden{b}", [HID, IMAGES * 16], on=on) for b in range(2)]
            small = sb(f"{tag}_small", [HID, IMAGES * 16], on=on)
            LAYERS = 5

            def tensor(pe):
                pe.wait_ge(s["sums"], 1)
                for n in range(LAYERS):
                    w = w0 if n == 0 else wh[:, (n - 1) * HID:n * HID]
                    if n:
                        pe.wait_ge(s["leaky"], n)
                    nc.tensor.matmul(in_ps[0:HID, 0:256], w, sums[:, :] if n == 0 else hidden[(n - 1) % 2][:, :],
                                     start=True, stop=True).then_inc(s["layer"], 1)
                pe.wait_ge(s["leaky"], LAYERS)
                nc.tensor.matmul(in_ps[:, 0:256], we, hidden[(LAYERS - 1) % 2][:, :], start=True, stop=True).then_inc(s["layer"], 1)

            def vector(dve, chain):
                for n in range(LAYERS):
                    dve.wait_ge(s["layer"], n + 1)
                    chain(nc.vector.tensor_scalar(small[:, :], in_ps[0:HID, 0:256], 0.2, None, ALU.mult))
                    nc.vector.tensor_tensor(hidden[n % 2][:, :], small[:, :], in_ps[0:HID, 0:256], ALU.max).then_inc(s["leaky"], 1)

            def scalar(act):
                act.wait_ge(s["layer"], LAYERS + 1)
                nc.scalar.activation(gate[:, :], in_ps[:, 0:256], ACT.Sigmoid).then_inc(s["gate"], 1)
            return tensor, vector, scalar

        def axial_along():
            on = ExitStack()
            with on:
                s = {n: sem(f"rows_{n}") for n in ("sums", "layer", "leaky", "gate", "chain", "gated", "turned", "turned_sb", "att", "att_sb")}
                sums = sb("rows_sums", [F, 256], on=on)
                gate = sb("rows_gate", [F, 256], on=on)
                gated = [sb(f"rows_gated{b}", [F, 512], on=on) for b in range(RING)]
                val = [sb(f"rows_val{b}", [P, 512], on=on) for b in range(RING)]
                bankG = pb("rows_bankG", 512, on=on)
                bankX = [pb(f"rows_bankX{b}", 512, on=on) for b in range(RING)]
                bankO = [pb(f"rows_bankO{b}", 512, on=on) for b in range(RING)]
                g_tensor, g_vector, g_scalar = gate_network(on, "rows", s, bankG, sums, gates_w[:, 0:HID], gates_wh[:, 0:4 * HID],
                                                            gates_we[:, 0:F], gate)
                block = on.enter_context(nc.Block())

                @block.tensor
                def _(pe):
                    pe.sem_inc(s["turned"], RING)
                    pe.sem_inc(s["att"], RING)
                    g_tensor(pe)

                    def turn(g, b):
                        pe.wait_ge(s["gated"], g + 1)
                        pe.wait_ge(s["turned_sb"], g + 1)
                        for t in range(4):
                            last = nc.tensor.transpose(bankX[b][:, t * P:(t + 1) * P], gated[b][:, t * P:(t + 1) * P], K("ident"))
                        last.then_inc(s["turned"], 1)

                    def attend(g, b):
                        pe.wait_ge(s["turned_sb"], g + 1 + RING)
                        pe.wait_ge(s["att_sb"], g + 1)
                        for t in range(4):
                            last = nc.tensor.matmul(bankO[b][:, t * P:(t + 1) * P], val[b][:, t * P:(t + 1) * P],
                                                    att_along[:, bass.ds((g * 4 + t) * P, P)], start=True, stop=True)
                        last.then_inc(s["att"], 1)
                    with pe.Fori(0, IMAGES // 4) as r:
                        for b in range(2):
                            turn(r * 2 + b, b)
                        for b in range(2):
                            attend(r * 2 + b, b)

                @block.scalar
                def _(act):
                    act.sem_inc(s["turned_sb"], RING)
                    act.sem_inc(s["att_sb"], RING)
                    g_scalar(act)
                    with act.Fori(0, IMAGES // 4) as r:
                        for b in range(2):
                            g = r * 2 + b
                            act.wait_ge(s["turned"], g + 1 + RING)
                            act.wait_ge(s["att"], g + 1)
                            nc.scalar.activation(val[b][:, :], bankX[b][:, :], ACT.Copy).then_inc(s["turned_sb"], 1)
                        for b in range(2):
                            g = r * 2 + b
                            act.wait_ge(s["att"], g + 1 + RING)
                            nc.scalar.activation(feat[:, bass.ds(g * 512, 512)], bankO[b][:, :], ACT.Copy).then_inc(s["att_sb"], 1)

                @block.vector
                def _(dve):
                    chain = Chain(dve, s["chain"])
                    chain(nc.vector.reduce_sum(sums[:, :], att_t[:, :].rearrange("p (r c) -> p r c", c=COLS), AX_X))
                    nc.vector.tensor_scalar(sums[:, :], sums[:, :], 1.0 / (ROWS * COLS), None, ALU.mult).then_inc(s["sums"], 1)
                    g_vector(dve, chain)
                    dve.wait_ge(s["gate"], 1)
                    with dve.Fori(0, IMAGES // 4) as r:
                        for b in range(2):
                            g = r * 2 + b
                            dve.wait_ge(s["turned"], g + 1)
                            nc.vector.tensor_tensor(gated[b][:, :].rearrange("p (r c) -> p r c", c=COLS),
                                                    att_t[:, bass.ds(g * 512, 512)].rearrange("p (r c) -> p r c", c=COLS),
                                                    gate[:, bass.ds(g * 32, 32)].unsqueeze(2).broadcast_to([F, 32, COLS]),
                                                    ALU.mult).then_inc(s["gated"], 1)

        def attention_output():
            on = ExitStack()
            with on:
                s = {n: sem(f"cols_{n}") for n in ("sums", "layer", "leaky", "gate", "chain", "gated", "out", "added", "weights", "branch", "branch_sb")}
                sums = sb("cols_sums", [F, 256], on=on)
                gate = sb("cols_gate", [F, 256], on=on)
                gated = [sb(f"cols_gated{b}", [F, 512], on=on) for b in range(RING)]
                branch = sb("cols_branch", [IMAGES, F], on=on)
                picked = [sb(f"cols_picked{b}", [IMAGES, 2 * P], on=on) for b in range(RING)]
                bankG = pb("cols_bankG", 512, on=on)
                bankI = pb("cols_bankI", 512, on=on)
                bankO = [pb(f"cols_bankO{b}", 512, on=on) for b in range(RING)]
                bankB = [pb(f"cols_bankB{b}", 512, on=on) for b in range(RING)]
                g_tensor, g_vector, g_scalar = gate_network(on, "cols", s, bankG, sums, gates_w[:, HID:2 * HID],
                                                            gates_wh[:, 4 * HID:8 * HID], gates_we[:, F:2 * F], gate)
                block = on.enter_context(nc.Block())

                @block.tensor
                def _(pe):
                    pe.sem_inc(s["out"], RING)
                    pe.wait_ge(s["weights"], 3)
                    nc.tensor.matmul(bankI[0:IMAGES, 0:F], K("ones", 1)[:, 0:IMAGES], out_rows[:, 3 * F:4 * F], start=True, stop=False)
                    for kc in range(KC):
                        last = nc.tensor.matmul(bankI[0:IMAGES, 0:F], pooled[:, kc * IMAGES:(kc + 1) * IMAGES], il_w[:, kc * F:(kc + 1) * F],
                                                start=False, stop=(kc == KC - 1))
                    last.then_inc(s["branch"], 1)
                    g_tensor(pe)
                    pe.wait_ge(s["branch_sb"], 1)
                    with pe.Fori(0, IMAGES // 4) as r:
                        for b in range(2):
                            g = r * 2 + b
                            pe.wait_ge(s["gated"], g + 1)
                            pe.wait_ge(s["added"], g + 1)
                            for n in range(2):
                                nc.tensor.matmul(bankB[b][:, n * F:(n + 1) * F], picked[b][:, n * P:(n + 1) * P], branch[:, :],
                                                 start=True, stop=True)
                            for t in range(4):
                                nc.tensor.matmul(bankO[b][:, t * P:(t + 1) * P], K("ones", 1), out_rows[:, 2 * F:3 * F], start=True, stop=False)
                                last = nc.tensor.matmul(bankO[b][:, t * P:(t + 1) * P], gated[b][:, t * P:(t + 1) * P], end_w[:, :],
                                                        start=False, stop=True)
                            last.then_inc(s["out"], 1)

                @block.scalar
                def _(act):
                    act.wait_ge(s["branch"], 1)
                    nc.scalar.activation(branch[:, :], bankI[0:IMAGES, 0:F], ACT.Relu).then_inc(s["branch_sb"], 1)
                    g_scalar(act)

                @block.vector
                def _(dve):
                    chain = Chain(dve, s["chain"])
                    dve.sem_inc(s["added"], RING)
                    nc.vector.tensor_tensor(end_w[:, :], end_w[:, :], scales_b[:, 0:F], ALU.mult).then_inc(s["weights"], 1)
                    for kc in range(KC):
                        nc.vector.tensor_tensor(il_w[:, kc * F:(kc + 1) * F], il_w[:, kc * F:(kc + 1) * F], scales_b[:, F:2 * F],
                                                ALU.mult).then_inc(s["weights"], 1)
                    chain(nc.vector.reduce_sum(sums[:, :].rearrange("p (n c) -> p n c", c=COLS),
                                               feat[:, :].rearrange("p (n r c) -> p n c r", n=IMAGES, c=COLS), AX_X))
                    nc.vector.tensor_scalar(sums[:, :], sums[:, :], 1.0 / (ROWS * COLS), None, ALU.mult).then_inc(s["sums"], 1)
                    g_vector(dve, chain)
                    dve.wait_ge(s["gate"], 1)

                    def apply_gate(g, b):
                        dve.wait_ge(s["out"], g + 1)
                        for n in range(2):
                            nc.vector.tensor_tensor(gated[b][:, n * 256:(n + 1) * 256].rearrange("p (r c) -> p r c", c=COLS),
                                                    feat[:, bass.ds(g * 512 + n * 256, 256)].rearrange("p (r c) -> p r c", c=COLS),
                                                    gate[:, bass.ds(g * 32 + n * 16, 16)].unsqueeze(1).broadcast_to([F, ROWS, COLS]), ALU.mult)
                        nc.vector.tensor_scalar(picked[b][:, :], K("pick", IMAGES)[:, bass.ds(g * 2 * P, 2 * P)], 1.0, None,
                                                ALU.mult).then_inc(s["gated"], 1)

                    def add(g, b):
                        dve.wait_ge(s["out"], g + 1 + RING)
                        x4 = x_res[:, bass.ds(g * 4 * C, 4 * C)].rearrange("p (t c) -> p t c", c=C)
                        nc.vector.scalar_tensor_tensor(out=x4[:, :, 0:F], in0=bankO[b][:, :].rearrange("p (t c) -> p t c", c=F), scalar=0.0,
                                                       in1=x4[:, :, 0:F], op0=ALU.max, op1=ALU.add)
                        x22 = x_res[:, bass.ds(g * 4 * C, 4 * C)].rearrange("p (n h c) -> p n h c", n=2, c=C)
                        nc.vector.tensor_tensor(x22[:, :, :, F:2 * F], x22[:, :, :, F:2 * F],
                                                bankB[b][:, 0:2 * F].rearrange("p (n c) -> p n c", n=2).unsqueeze(2).broadcast_to([P, 2, 2, F]),
                                                ALU.add).then_inc(s["added"], 1)
                    with dve.Fori(0, IMAGES // 4) as r:
                        for b in range(2):
                            apply_gate(r * 2 + b, b)
                        for b in range(2):
                            add(r * 2 + b, b)

        with ExitStack() as on:
            s = {n: sem(f"mix_{n}") for n in ("var", "sqrt", "xn", "transposed", "copied", "dft", "chain", "chain_act",
                                              "arg", "sin", "emb", "theta", "magnitude2", "magnitude", "block_diag",
                                              "spectrum", "mixed", "norm", "scaled", "turned", "turned_sb", "row", "added")}
            xT = [sb(f"mix_xT{b}", [P, KC * HALVES * P], on=on) for b in range(RING)]
            bankT = [pb(f"mix_bankT{b}", 512, on=on) for b in range(RING)]
            spec_ps = pb("mix_spec", TILES * 2 * MODES, on=on)
            mix_ps = pb("mix_mix", MODES * 2 * TILES, on=on)
            small_ps = pb("mix_small", 512, on=on)
            t_b = sb("mix_t", [2 * MODES, ROWS], on=on)
            w_rep = sb("mix_w", [P, COLS * MODES * 2], on=on)
            w_abs = sb("mix_wabs", [P, COLS * MODES], on=on)
            w_sq = sb("mix_wsq", [P, COLS * MODES], on=on)
            ke = sb("mix_ke", [2 * MODES, 2 * MODES], on=on)
            bias_b = sb("mix_bias", [P, 2 * MODES], on=on)
            arg = sb("mix_arg", [2 * MODES, ROWS], on=on)
            turns = sb("mix_turns", [2 * MODES, ROWS], on=on)
            emb = sb("mix_emb", [2 * MODES, ROWS], on=on)
            emb_x = sb("mix_embx", [2 * MODES, ROWS * COLS], on=on)
            theta = sb("mix_theta", [P, HALVES * 2 * MODES], on=on)
            theta_sq = sb("mix_theta_sq", [P, HALVES * MODES], on=on)
            theta_abs = sb("mix_theta_abs", [P, HALVES * MODES], on=on)
            bd = [sb(f"mix_bd{r}", [P, MODES * P], on=on) for r in range(3)]
            spec = sb("mix_spec_sb", [P, MODES * 3 * TILES], on=on)
            tmp = [sb(f"mix_tmp{b}", [P, IMAGES * MODES], on=on) for b in range(2)]
            rnorm = sb("mix_rnorm", [P, HALVES * MODES], on=on)
            scaled = sb("mix_scaled", [P, TILES * 2 * MODES], on=on)
            def inverse_bank(n):
                return (spec_ps, mix_ps)[n // 2 % 2][:, n % 2 * 512:(n % 2 + 1) * 512], 8 * (n // 4) + n % 4

            turned = sb("mix_turned", [P, 8 * P], on=on)

            block = on.enter_context(nc.Block())

            @block.sync
            def _(sp):
                sp.dma_start(konst[:, :], A["konst"]).then_inc(loads["konst"], 16)
                x_rows = A["x"].rearrange("(j p) c -> p j c", p=P)
                for c in range(CHUNKS):
                    dst = x_res[:, c * CHUNK_T * C:(c + 1) * CHUNK_T * C].rearrange("p (j c) -> p j c", c=C)
                    sp.dma_start(dst, x_rows[:, c * CHUNK_T:(c + 1) * CHUNK_T, :]).then_inc(loads["x"], 16)
                sp.dma_start(router0[:, :], A["L0_ffn_router_w"]).then_inc(loads["router0"], 16)
                for dst, name in ((gate0, "gate"), (up0, "up"), (down0, "down")):
                    sp.dma_start(dst[:, :], A[f"L0_ffn_{name}_w"], max_dma_last_dim=32768).then_inc(loads["w0"], 16)

            @block.scalar
            def _(act):
                act.dma_start(t_b[:, :], A["L0_conv_t"].unsqueeze(0).broadcast_to([2 * MODES, ROWS])).then_inc(loads["spectral"], 16)
                act.dma_start(ke[:, :], A["L0_conv_ke_weights"]).then_inc(loads["spectral"], 16)
                act.dma_start(bias_b[:, :], A["L0_conv_ke_bias"].broadcast_to([P, 2 * MODES])).then_inc(loads["spectral"], 16)
                for r in range(ROWS_T):
                    act.dma_start(w_rep[r * COLS:(r + 1) * COLS, :], A["L0_conv_weights1"]).then_inc(loads["spectral"], 16)
                act.wait_ge(s["arg"], 1)
                nc.scalar.activation(emb[:, :], arg[:, :], ACT.Sin).then_inc(s["sin"], 1)
                act.wait_ge(s["magnitude2"], 2)
                nc.scalar.activation(theta_abs[:, :], theta_sq[:, :], ACT.Sqrt).then_inc(s["magnitude"], 1)
                nc.scalar.activation(w_abs[:, :], w_sq[:, :], ACT.Sqrt).then_inc(s["magnitude"], 1)
                act.sem_inc(s["copied"], RING)
                with act.Fori(0, CHUNKS) as c:
                    layer_norm_sqrt(act, s, c)
                    for i in range(CHUNK_T // HALVES):
                        n = c * (CHUNK_T // HALVES) + i
                        act.wait_ge(s["transposed"], n + 1 + RING)
                        act.wait_ge(s["dft"], n + 1)
                        nc.scalar.activation(xT[i % RING][:, :], bankT[i % RING][:, :], ACT.Copy).then_inc(s["copied"], 1)
                for g in range(2):
                    act.wait_ge(s["turned"], g + 1)
                    nc.scalar.activation(turned[:, g * 512:(g + 1) * 512], bankT[g][:, :], ACT.Copy).then_inc(s["turned_sb"], 1)

            @block.gpsimd
            def _(pool):
                pool.wait_ge(loads["konst"], 16)
                pool.wait_ge(loads["spectral"], (3 + ROWS_T) * 16)
                shape = [P, MODES, ROWS_T, COLS]
                w4 = w_rep[:, :].rearrange("p (o m r) -> p m o r", m=MODES, r=2)
                rows = K("row_of").unsqueeze(1).unsqueeze(3)
                for r in range(2):
                    for m in range(MODES):
                        last = nc.gpsimd.tensor_tensor(
                            bd[r][:, m * P:(m + 1) * P].rearrange("p (t o) -> p t o", o=COLS),
                            w4[:, m, :, r].unsqueeze(1).broadcast_to([P, ROWS_T, COLS]),
                            K("row_of").unsqueeze(2).broadcast_to([P, ROWS_T, COLS]), ALU.mult)
                    last.then_inc(s["block_diag"], 1)
                pool.wait_ge(s["magnitude"], 2)
                wa = w_abs[:, :].rearrange("p (o m) -> p m o", m=MODES)
                for m in range(MODES):
                    last = nc.gpsimd.tensor_tensor(
                        bd[2][:, m * P:(m + 1) * P].rearrange("p (t o) -> p t o", o=COLS),
                        wa[:, m, :].unsqueeze(1).broadcast_to([P, ROWS_T, COLS]),
                        K("row_of").unsqueeze(2).broadcast_to([P, ROWS_T, COLS]), ALU.mult)
                last.then_inc(s["block_diag"], 1)

            @block.vector
            def _(dve):
                chain = Chain(dve, s["chain"])
                dve.wait_ge(loads["konst"], 16)
                dve.wait_ge(loads["spectral"], (3 + ROWS_T) * 16)
                freq, phase = K("freq", 2 * MODES), K("phase", 2 * MODES)
                chain(nc.vector.tensor_scalar(arg[:, :], t_b[:, :], freq, None, ALU.mult))
                chain(nc.vector.tensor_scalar(turns[:, :], arg[:, :], phase, 1.0 / TWO_PI, ALU.add, ALU.mult))
                chain(nc.vector.tensor_scalar(turns[:, :], turns[:, :], ROUND, None, ALU.add))
                chain(nc.vector.tensor_scalar(turns[:, :], turns[:, :], -ROUND, None, ALU.add))
                p1 = 6.28125
                p2 = float(np.round((TWO_PI - p1) * 2 ** 21) / 2 ** 21)
                for part in (p1, p2, TWO_PI - p1 - p2):
                    chain(nc.vector.scalar_tensor_tensor(out=arg[:, :], in0=turns[:, :], scalar=-part, in1=arg[:, :],
                                                         op0=ALU.mult, op1=ALU.add))
                chain(nc.vector.tensor_scalar(arg[:, :], arg[:, :], phase, None, ALU.add))
                pi = float(np.nextafter(np.float32(np.pi), np.float32(0)))
                nc.vector.tensor_scalar(arg[:, :], arg[:, :], pi, -pi, ALU.min, ALU.max).then_inc(s["arg"], 1)
                dve.wait_ge(s["sin"], 1)
                nc.vector.tensor_tensor(emb_x[:, :].rearrange("j (t i) -> j t i", i=COLS),
                                        emb[:, :].unsqueeze(2).broadcast_to([2 * MODES, ROWS, COLS]),
                                        K("head", 2 * MODES).unsqueeze(1).broadcast_to([2 * MODES, ROWS, COLS]),
                                        ALU.mult).then_inc(s["emb"], 1)
                dve.wait_ge(s["theta"], 1)
                chain(nc.vector.tensor_tensor(
                    theta[:, :].rearrange("p (h r m) -> p h m r", h=HALVES, r=2),
                    small_ps[:, 0:HALVES * 2 * MODES].rearrange("p (h m r) -> p h m r", h=HALVES, r=2),
                    bias_b[:, :].rearrange("p (m r) -> p m r", r=2).unsqueeze(1).broadcast_to([P, HALVES, MODES, 2]),
                    ALU.add))
                th = theta[:, :].rearrange("p (h r m) -> p h r m", h=HALVES, r=2)
                ths = theta_sq[:, :].rearrange("p (h m) -> p h m", h=HALVES)
                t0 = tmp[0][:, 0:HALVES * MODES].rearrange("p (h m) -> p h m", h=HALVES)
                t1 = tmp[1][:, 0:HALVES * MODES].rearrange("p (h m) -> p h m", h=HALVES)
                chain(nc.vector.tensor_tensor(t0, th[:, :, 0, :], th[:, :, 0, :], ALU.mult))
                chain(nc.vector.tensor_tensor(t1, th[:, :, 1, :], th[:, :, 1, :], ALU.mult))
                chain(nc.vector.tensor_tensor(ths, t0, t1, ALU.add))
                nc.vector.tensor_scalar(ths, ths, 2.0 ** -116, None, ALU.max).then_inc(s["magnitude2"], 1)
                w3 = w_rep[:, :].rearrange("p (om r) -> p om r", r=2)
                chain(nc.vector.tensor_tensor(tmp[0][:, :], w3[:, :, 0], w3[:, :, 0], ALU.mult))
                chain(nc.vector.tensor_tensor(tmp[1][:, :], w3[:, :, 1], w3[:, :, 1], ALU.mult))
                chain(nc.vector.tensor_tensor(w_sq[:, :], tmp[0][:, :], tmp[1][:, :], ALU.add))
                nc.vector.tensor_scalar(w_sq[:, :], w_sq[:, :], 2.0 ** -116, None, ALU.max).then_inc(s["magnitude2"], 1)

                dve.wait_ge(loads["x"], CHUNKS * 16)
                layer_norm(dve, chain, s, 1e-6)

                dve.wait_ge(s["dft"], IMAGES + RING)
                sp5 = spec_ps[:, :].rearrange("p (b h r m) -> p h r b m", h=HALVES, r=2, m=MODES)
                so5 = spec[:, :].rearrange("p (m v b h) -> p h v b m", v=3, b=IMAGES, h=HALVES)
                v0 = tmp[0][:, :].rearrange("p (b m) -> p b m", m=MODES)
                v1 = tmp[1][:, :].rearrange("p (b m) -> p b m", m=MODES)
                for h in range(HALVES):
                    def wt(r):
                        return th[:, h, r, :].unsqueeze(1).broadcast_to([P, IMAGES, MODES])
                    nc.vector.tensor_tensor(v0, sp5[:, h, 0], wt(0), ALU.mult)
                    chain(nc.vector.tensor_tensor(v1, sp5[:, h, 1], wt(1), ALU.mult))
                    chain(nc.vector.tensor_tensor(so5[:, h, 1], v0, v1, ALU.subtract))
                    nc.vector.tensor_tensor(v0, sp5[:, h, 0], wt(1), ALU.mult)
                    chain(nc.vector.tensor_tensor(v1, sp5[:, h, 1], wt(0), ALU.mult))
                    chain(nc.vector.tensor_tensor(so5[:, h, 2], v0, v1, ALU.add))
                    nc.vector.tensor_scalar(so5[:, h, 0], so5[:, h, 2], -1.0, None, ALU.mult).then_inc(s["spectrum"], 1)
                dve.wait_ge(s["norm"], 1)
                nrm = small_ps[:, 128:128 + HALVES * MODES].rearrange("p (m h) -> p h m", h=HALVES)
                rn = rnorm[:, :].rearrange("p (h m) -> p h m", h=HALVES)
                chain(nc.vector.tensor_scalar(rn, nrm, 1e-12, -1.0, ALU.add, ALU.add))
                chain(nc.vector.tensor_scalar(rn, rn, 0.0, 1.0, ALU.max, ALU.add))
                chain(nc.vector.reciprocal(rn, rn))
                dve.wait_ge(s["mixed"], 1)
                mp = mix_ps[:, :].rearrange("p (m r b h) -> p h r b m", r=2, b=IMAGES, h=HALVES)
                sc = scaled[:, :].rearrange("p (b h r m) -> p h r b m", h=HALVES, r=2, m=MODES)
                for h in range(HALVES):
                    for r in range(2):
                        nc.vector.tensor_tensor(sc[:, h, r], mp[:, h, r],
                                                rn[:, h, :].unsqueeze(1).broadcast_to([P, IMAGES, MODES]),
                                                ALU.mult).then_inc(s["scaled"], 1)
                for n in range(IMAGES):
                    dve.wait_ge(s["row"], n + 1)
                    bank, j = inverse_bank(n)
                    xi = x_res[:, 8 * (n // 4) * C:8 * (n // 4 + 1) * C].rearrange("p (h r c) -> p r h c", h=2, c=C)[:, j % 4]
                    nc.vector.tensor_tensor(xi, xi, bank.rearrange("p (h c) -> p h c", h=2), ALU.add).then_inc(s["added"], 1)

            @block.tensor
            def _(pe):
                pe.sem_inc(s["transposed"], RING)
                pe.sem_inc(s["dft"], RING)
                pe.wait_ge(loads["konst"], 16)
                pe.wait_ge(loads["spectral"], (3 + ROWS_T) * 16)
                pe.wait_ge(s["emb"], 1)
                for h in range(HALVES):
                    last = nc.tensor.matmul(small_ps[:, h * 32:(h + 1) * 32], emb_x[:, h * P:(h + 1) * P], ke[:, :],
                                            start=True, stop=True)
                last.then_inc(s["theta"], 1)
                dft = K("dft").rearrange("p (k f) -> p k f", k=KC)
                with pe.Fori(0, IMAGES // RING) as q:
                    for b in range(RING):
                        transpose_image(pe, s, q * RING + b, b, bankT[b])
                    for b in range(RING):
                        n = q * RING + b
                        pe.wait_ge(s["copied"], n + 1 + RING)
                        for h in range(HALVES):
                            for kc in range(KC):
                                last = nc.tensor.matmul(spec_ps[:, bass.ds((n * HALVES + h) * 32, 32)],
                                                        xT[b][:, (kc * HALVES + h) * P:(kc * HALVES + h + 1) * P],
                                                        dft[:, kc, :], start=(kc == 0), stop=(kc == KC - 1))
                        last.then_inc(s["dft"], 1)
                pe.wait_ge(s["block_diag"], 3)
                ta = theta_abs[:, :].rearrange("p (h m) -> p m h", h=HALVES)
                pe.wait_ge(s["magnitude"], 2)
                for m in range(MODES):
                    last = nc.tensor.matmul(small_ps[:, 128 + m * HALVES:128 + (m + 1) * HALVES], bd[2][:, m * P:(m + 1) * P],
                                            ta[:, m, :], start=True, stop=True)
                last.then_inc(s["norm"], 1)
                pe.wait_ge(s["spectrum"], HALVES)
                for m in range(MODES):
                    dst = mix_ps[:, m * 64:(m + 1) * 64]
                    nc.tensor.matmul(dst, bd[0][:, m * P:(m + 1) * P], spec[:, m * 96 + 32:m * 96 + 96], start=True, stop=False)
                    last = nc.tensor.matmul(dst, bd[1][:, m * P:(m + 1) * P], spec[:, m * 96:m * 96 + 64], start=False, stop=True)
                last.then_inc(s["mixed"], 1)
                pe.wait_ge(s["scaled"], 2 * HALVES)
                for g in range(8):
                    last = nc.tensor.transpose(bankT[g // 4][:, g % 4 * P:(g % 4 + 1) * P], scaled[:, g * P:(g + 1) * P],
                                               K("ident"))
                    if g % 4 == 3:
                        last.then_inc(s["turned"], 1)
                for n in range(IMAGES):
                    pe.wait_ge(s["turned_sb"], n // 8 + 1)
                    if n >= 4:
                        pe.wait_ge(s["added"], n - 3)
                    bank, j0 = inverse_bank(n)
                    for h in range(2):
                        j = j0 + 4 * h
                        r = j % 4 * 32
                        last = nc.tensor.matmul(bank[:, h * C:(h + 1) * C], turned[r:r + 32, j // 4 * P:(j // 4 + 1) * P],
                                                K("idft")[r:r + 32, :], start=True, stop=True)
                    last.then_inc(s["row"], 1)

        if upto >= 2:
            router("moe0", router0, "router0")
            mlp("experts0", SLOT_TILES, I0, up0, down0, gate0, (("w0", 48),))
            combine("combine0")
        moe0.close()
        clear_semaphores()
        if upto >= 3:
            attention = ExitStack()
            with attention as on3:
                conv_w = sb("conv_w", [P, 9 * KC * F], on=on3)
                entry_sb = sb("entry_sb", [P, 2], on=on3)
                qk_w = sb("qk_w", [F, 64], on=on3)
                qk_sb = sb("qk_sb", [64, 2], on=on3)
                val_w = sb("val_w", [F, F], on=on3)
                val_sb = sb("val_sb", [F, 2], on=on3)
                gates_w = sb("gates_w", [F, 2 * HID], on=on3)
                gates_wh = sb("gates_wh", [HID, 8 * HID], on=on3)
                gates_we = sb("gates_we", [HID, 2 * F], on=on3)
                end_w = sb("end_w", [F, F], on=on3)
                il_w = sb("il_w", [P, KC * F], on=on3)
                out_rows = sb("out_rows", [1, 4 * F], on=on3)
                scales_b = sb("scales_b", [P, 2 * F], on=on3)
                feat = sb("feat", [F, TOKENS], on=on3)
                pooled = sb("pooled", [P, KC * IMAGES], on=on3)
                ATTN_LOADS = 11
                with nc.Block() as block:
                    @block.sync
                    def _(sp):
                        sp.dma_start(conv_w[:, :], A["conv_w"]).then_inc(loads["conv"], 16)
                        sp.dma_start(entry_sb[:, :], A["entry_sb"]).then_inc(loads["conv"], 16)
                        for dst, name in ((qk_w, "qk_w"), (qk_sb, "qk_sb"), (val_w, "val_w"), (val_sb, "val_sb"), (gates_w, "gates_w"),
                                          (gates_wh, "gates_wh"), (gates_we, "gates_we"), (end_w, "end_w"), (il_w, "il_w"), (out_rows, "out_rows")):
                            sp.dma_start(dst[:, :], A[name]).then_inc(loads["attn"], 16)
                        sp.dma_start(scales_b[:, :], A["out_rows"][:, 0:2 * F].broadcast_to([P, 2 * F])).then_inc(loads["attn"], 16)
                entry_convolution()
                with ExitStack() as on4:
                    att_t = sb("att_t", [F, TOKENS], on=on4)
                    att_along = sb("att_along", [P, TILES * P], on=on4)
                    axial_scores()
                    axial_along()
                    attention_output()
        if upto >= 4:
            with ExitStack() as moe1:
                router1 = sb("router1_sb", [P, KC * E], on=moe1)
                up1 = sb("up1", [P, E * KC * I1], on=moe1)
                down1 = sb("down1", [P, E * (I1 // P) * C], on=moe1)
                ws1 = sb("ws1_sb", [P, KC * IS], on=moe1)
                ws2 = sb("ws2_sb", [P, IS // P * C], on=moe1)
                with nc.Block() as block:
                    @block.sync
                    def _(sp):
                        sp.dma_start(router1[:, :], A["L1_ffn_w_router"]).then_inc(loads["router1"], 16)
                        sp.dma_start(ws1[:, :], A["L1_ffn_ws1"]).then_inc(loads["ws"], 16)
                        sp.dma_start(ws2[:, :], A["L1_ffn_ws2"]).then_inc(loads["ws"], 16)
                        sp.dma_start(up1[:, :], A["L1_ffn_w1_stack"]).then_inc(loads["w1"], 16)
                        sp.dma_start(down1[:, :], A["L1_ffn_w2_stack"]).then_inc(loads["w1"], 16)
                router("moe1", router1, "router1")
                mlp("shared", TILES, IS, ws1, ws2, load=(("ws", 32),), experts=False)
                mlp("experts1", SLOT_TILES, I1, up1, down1, load=(("w1", 32),))
                combine("combine1")

        with ExitStack() as on:
            stored = sem("out_stored")
            block = on.enter_context(nc.Block())

            @block.sync
            def _(sp):
                sp.dma_start(out.rearrange("(j p) c -> p j c", p=P), x_res[:, :].rearrange("p (j c) -> p j c", c=C)).then_inc(stored, 16)
                sp.wait_ge(stored, 16)


def padded_pair(v, h, axis):
    pad = [(0, 0), (0, 0)]
    pad[axis] = (0, 32 - G)
    return np.ascontiguousarray(np.concatenate([np.pad(v, pad), np.pad(h, pad)], axis))


def by_contracted_row(w):
    e, o, c = w.shape
    return np.ascontiguousarray(w.reshape(e, o, c // P, P).transpose(3, 0, 2, 1).reshape(P, -1))


def layouts(inputs):
    a = {k: np.asarray(v) for k, v in inputs.items()}
    t = np.ascontiguousarray
    return {
        "konst": constants()[0],
        "x": t(a["x"].reshape(TOKENS, C)),
        "L0_conv_t": t(a["L0_conv_t"]),
        "L0_conv_weights1": t(a["L0_conv_weights1"].reshape(COLS, -1)),
        "L0_conv_ke_weights": t(a["L0_conv_ke_weights"].reshape(2 * MODES, 2 * MODES)),
        "L0_conv_ke_bias": t(a["L0_conv_ke_bias"].reshape(1, 2 * MODES)),
        "conv_w": t(a["L1_conv_entry_w"].reshape(9, KC, P, F).transpose(2, 0, 1, 3).reshape(P, -1)),
        "entry_sb": t(np.stack([a["L1_conv_entry_s"], a["L1_conv_entry_b"]], 1)),
        "qk_w": padded_pair(a["L1_conv_vqk_w"], a["L1_conv_hqk_w"], 1),
        "qk_sb": padded_pair(np.stack([a["L1_conv_vqk_s"], a["L1_conv_vqk_b"]], 1), np.stack([a["L1_conv_hqk_s"], a["L1_conv_hqk_b"]], 1), 0),
        "val_w": a["L1_conv_val_w"],
        "val_sb": t(np.stack([a["L1_conv_val_s"], a["L1_conv_val_b"]], 1)),
        "gates_w": t(np.concatenate([a["L1_conv_vca_w0"], a["L1_conv_hca_w0"]], 1)),
        "gates_wh": t(np.concatenate([a["L1_conv_vca_wh"], a["L1_conv_hca_wh"]], 0).transpose(1, 0, 2).reshape(HID, -1)),
        "gates_we": t(np.concatenate([a["L1_conv_vca_we"], a["L1_conv_hca_we"]], 1)),
        "end_w": a["L1_conv_end_w"],
        "il_w": t(a["L1_conv_il_w"].reshape(KC, P, F).transpose(1, 0, 2).reshape(P, -1)),
        "out_rows": t(np.concatenate([a[f"L1_conv_{n}"] for n in ("end_s", "il_s", "end_b", "il_b")])[None]),
        "L1_ffn_w_router": by_contracted_row(a["L1_ffn_w_router"][None]),
        "L1_ffn_ws1": by_contracted_row(a["L1_ffn_ws1"][None]),
        "L1_ffn_ws2": by_contracted_row(a["L1_ffn_ws2"][None]),
        "L1_ffn_w1_stack": by_contracted_row(a["L1_ffn_w1_stack"]),
        "L1_ffn_w2_stack": by_contracted_row(a["L1_ffn_w2_stack"]),
        "L0_ffn_router_w": by_contracted_row(a["L0_ffn_router_w"][None]),
        "L0_ffn_gate_w": by_contracted_row(a["L0_ffn_gate_w"]),
        "L0_ffn_up_w": by_contracted_row(a["L0_ffn_up_w"]),
        "L0_ffn_down_w": by_contracted_row(a["L0_ffn_down_w"]),
    }


def kernel(**inputs):
    import concourse.bacc as bacc
    from concourse.bass_utils import run_bass_kernel_spmd

    nc = bacc.Bacc("TRN2", target_bir_lowering=False, num_devices=1)
    arrays = layouts(inputs)
    ins = {n: nc.dram_tensor("in_" + n, a.shape, mybir.dt.from_np(a.dtype), kind="ExternalInput").ap() for n, a in arrays.items()}
    out = nc.dram_tensor("out", (TOKENS, C), F32, kind="ExternalOutput").ap()
    build(nc, ins, out)
    r = run_bass_kernel_spmd(nc, [{"in_" + n: a for n, a in arrays.items()}], core_ids=[0])
    return r.results[0]["out"].reshape(IMAGES, ROWS, COLS, C)
```

```python
from contextlib import ExitStack

import numpy as np

import concourse.bass as bass
from concourse import mybir

ALU = mybir.AluOpType
ACT = mybir.ActivationFunctionType
AX_X = mybir.AxisListType.X
F32 = mybir.dt.float32
I32 = mybir.dt.int32
HALF = mybir.dt.float32r

P = 128
IMAGES, ROWS, COLS, C = 16, 16, 16, 256
TOKENS = IMAGES * ROWS * COLS
TILES = TOKENS // P
KC = C // P
HALVES = TILES // IMAGES
ROWS_T = ROWS // HALVES
MODES = 16
E = 8
I0, I1, IS = 512, 256, 512
F = 128
G = 16
HID = 32
SLOT_TILES = (2 * TOKENS // P + E - 1 + 3) // 4 * 4
CHUNKS, CHUNK_T = 4, 8
RING = 2
ROUND = 1.5 * 2.0 ** 23
BIG = 2.0 ** 100
TWO_PI = 2.0 * np.pi


def constants():
    parts = {}
    c = np.arange(C)[:, None]
    m = np.arange(MODES)[None, :]
    angle = 2 * np.pi * c * m / C
    dft = np.concatenate([np.cos(angle), -np.sin(angle)], 1)
    parts["dft"] = dft.reshape(KC, P, 2 * MODES).transpose(1, 0, 2).reshape(P, -1)
    twice = np.where(m == 0, 1.0, 2.0)
    idft = np.concatenate([twice * np.cos(angle), -twice * np.sin(angle) * (m > 0)], 1).T / C
    parts["idft"] = np.tile(idft, (4, 1))
    parts["ident"] = np.eye(P)
    parts["ramp"] = np.tile(np.arange(P)[None, :], (P, 1))
    parts["column"] = np.arange(P)[:, None]
    parts["tile_base"] = np.tile(P * np.arange(TILES)[None, :], (P, 1))
    parts["first_wins"] = np.tile(E - np.arange(E)[None, :], (P, 1))
    parts["row_of"] = (np.arange(P)[:, None] // COLS == np.arange(ROWS_T)[None, :])
    parts["before"] = (np.arange(P)[:, None] < np.arange(P)[None, :])
    parts["ones"] = np.ones((P, P))
    j = np.arange(2 * MODES)
    freq = np.exp(-np.log(10000.0).astype(np.float32) * (j % MODES).astype(np.float32) / np.float32(MODES))
    parts["freq"] = np.pad(freq[:, None], ((0, P - 2 * MODES), (0, 0)))
    parts["phase"] = np.pad(np.where(j >= MODES, np.pi / 2, 0.0)[:, None], ((0, P - 2 * MODES), (0, 0)))
    head = (np.arange(COLS)[None, :] % 4 == j[:, None] // 8)
    parts["head"] = np.pad(head, ((0, P - 2 * MODES), (0, 0)))
    for name, group in (("same_col", np.arange(P) % 8), ("same_row", np.arange(P) // COLS)):
        member = (group[None, :] == np.arange(8)[:, None]).astype(np.float64)
        left = np.concatenate([np.ones((1, P)), member])
        right = np.concatenate([-BIG * np.ones((1, P)), BIG * member])
        parts[name + "_l"] = np.pad(left, ((0, P - 9), (0, 0)))
        parts[name + "_r"] = np.pad(right, ((0, P - 9), (0, 0)))
    arrays, where = {}, {}
    for name, a in parts.items():
        a = np.asarray(a, np.float32)
        kind = "konst_mix" if name in ("dft", "idft", "freq", "phase", "head", "row_of") else "konst_attn" if name[:5] == "same_" else "konst"
        at = sum(other.shape[1] for other in arrays.get(kind, []))
        where[name] = (kind, at, a.shape[1])
        arrays.setdefault(kind, []).append(a)
    return {kind: np.ascontiguousarray(np.concatenate(a, 1)) for kind, a in arrays.items()}, where


class Chain:

    def __init__(self, eng, sem):
        self.eng, self.sem, self.n = eng, sem, 0

    def __call__(self, ins):
        ins.then_inc(self.sem, 1)
        self.n = self.n + 1
        self.eng.wait_ge(self.sem, self.n)


def build(nc, A, out, upto=4):
    _, where = constants()
    ctx = ExitStack()
    with ctx:
        live = []

        def sem(name):
            live.append(nc.alloc_semaphore(name=name))
            return live[-1]

        def clear_semaphores():
            nc.clear_and_free_semaphores(live)
            live.clear()
            nc.all_engine_barrier()

        def sb(name, shape, dt=F32, on=ctx):
            return on.enter_context(nc.sbuf_tensor(name, shape, dt))

        def pb(name, width, on=ctx):
            return on.enter_context(nc.psum_tensor(name, [P, width], F32))

        konst = {}

        def place_tables(kind, on=ctx):
            konst[kind] = sb(f"{kind}_sb", [P, sum(w for k, _, w in where.values() if k == kind)], on=on)
        place_tables("konst")

        def K(name, parts=P):
            kind, at, w = where[name]
            return konst[kind][0:parts, at:at + w]

        x_res = sb("x_res", [P, TILES * C])
        h_dram = nc.dram_tensor("h_rows", (TOKENS, C), F32, kind="Internal").ap()
        y_dram = nc.dram_tensor("y_rows", (SLOT_TILES * P, C), F32, kind="Internal").ap()

        router0 = sb("router0_sb", [P, KC * E])
        stats = sb("stats", [P, CHUNK_T * 6])
        mean = sb("mean", [P, CHUNK_T])
        var_eps = sb("var_eps", [P, CHUNK_T])
        sqrt_v = sb("sqrt_v", [P, CHUNK_T])
        rstd = sb("rstd", [P, CHUNK_T])
        newton = sb("newton", [P, CHUNK_T])
        xn = [sb(f"xn{b}", [P, HALVES * C]) for b in range(RING)]

        w_top = sb("w_top", [P, 2 * TILES])
        pos_i = sb("pos_i", [P, 2 * TILES], I32)
        ids_i = sb("ids_i", [P, SLOT_TILES], I32)
        etile_i = sb("etile_i", [1, SLOT_TILES], I32)

        moe0 = ExitStack()
        gate0 = sb("gate0", [P, E * KC * I0], on=moe0)
        up0 = sb("up0", [P, E * KC * I0], on=moe0)

        loads = {n: nc.alloc_semaphore(name=f"loaded_{n}") for n in ("konst", "x", "spectral", "router0", "w0", "router1", "conv", "attn")}

        def x_tile(j, width=C, n=1):
            return x_res[:, bass.ds(j * C, n * C)]

        def product(out, left, right, start, stop):
            if len(left) == 1:
                return nc.tensor.matmul(out, left[0], right[0], start=start, stop=stop)
            nc.tensor.matmul(out, left[0], right[0], start=start, stop=False)
            nc.tensor.matmul(out, left[0], right[1], start=False, stop=False)
            return nc.tensor.matmul(out, left[1], right[0], start=False, stop=stop)

        def low_half(eng, low, whole, high):
            return eng.tensor_tensor(low, whole, high.bitcast(F32), ALU.subtract)

        def split_weights(tag, on, parts, step):
            stage = [sb(f"{tag}_stage{b}", [P, step], on=on) for b in range(RING)]
            s_in = [sem(f"{tag}_stage_in{b}") for b in range(RING)]
            s_high, s_low = sem(f"{tag}_high"), sem(f"{tag}_low")
            pieces = [(src, high, low, slice(at, at + step)) for src, high, low in parts for at in range(0, high.shape[1], step)]

            def split(pool):
                def load(n):
                    src, _, _, cols = pieces[n]
                    pool.dma_start(stage[n % RING][:, :], src[:, cols]).then_inc(s_in[n % RING], 16)

                for n in range(RING):
                    load(n)
                for n, (_, high, low, cols) in enumerate(pieces):
                    pool.wait_ge(s_in[n % RING], (n // RING + 1) * 16)
                    nc.gpsimd.tensor_copy(high[:, cols], stage[n % RING][:, :]).then_inc(s_high, 1)
                    pool.wait_ge(s_high, n + 1)
                    low_half(nc.gpsimd, low[:, cols], stage[n % RING][:, :], high[:, cols]).then_inc(s_low, 1)
                    pool.wait_ge(s_low, n + 1)
                    if n + RING < len(pieces):
                        load(n + RING)
            return split

        def layer_norm(dve, chain, s, eps, before=None, after=None):
            at = chain.n
            per = 8
            st = stats[:, :].rearrange("p (t f) -> p t f", f=6)
            with dve.Fori(0, CHUNKS) as c:
                chain.n = c * per + at
                if before is not None:
                    before(c)
                for t in range(CHUNK_T):
                    last = nc.vector.bn_stats(stats[:, 6 * t:6 * t + 6], x_tile(c * CHUNK_T + t))
                chain(last)
                nc.vector.tensor_tensor(mean[:, :], st[:, :, 1], st[:, :, 4], ALU.add)
                nc.vector.tensor_tensor(newton[:, :], st[:, :, 1], st[:, :, 4], ALU.subtract)
                chain(nc.vector.tensor_tensor(var_eps[:, :], st[:, :, 2], st[:, :, 5], ALU.add))
                nc.vector.tensor_scalar(mean[:, :], mean[:, :], 0.5, None, ALU.mult)
                nc.vector.tensor_scalar(var_eps[:, :], var_eps[:, :], 1.0 / C, eps, ALU.mult, ALU.add)
                chain(nc.vector.scalar_tensor_tensor(out=newton[:, :], in0=newton[:, :], scalar=0.25, in1=newton[:, :],
                                                     op0=ALU.mult, op1=ALU.mult))
                nc.vector.tensor_tensor(var_eps[:, :], var_eps[:, :], newton[:, :], ALU.add).then_inc(s["var"], 1)
                dve.wait_ge(s["sqrt"], c + 1)
                chain(nc.vector.reciprocal(rstd[:, :], sqrt_v[:, :]))
                chain(nc.vector.tensor_tensor(newton[:, :], var_eps[:, :], rstd[:, :], ALU.mult))
                chain(nc.vector.tensor_tensor(newton[:, :], newton[:, :], rstd[:, :], ALU.mult))
                chain(nc.vector.tensor_scalar(newton[:, :], newton[:, :], -0.5, 1.5, ALU.mult, ALU.add))
                chain(nc.vector.tensor_tensor(rstd[:, :], rstd[:, :], newton[:, :], ALU.mult))
                for i in range(CHUNK_T // HALVES):
                    n = c * (CHUNK_T // HALVES) + i
                    dve.wait_ge(s["transposed"], n + 1)
                    if "stored" in s:
                        dve.wait_ge(s["stored"][i % RING], (c * (CHUNK_T // HALVES // RING) + i // RING + 1) * 16)
                    for h in range(HALVES):
                        t = i * HALVES + h
                        last = nc.vector.tensor_scalar(
                            xn[i % RING][:, h * C:(h + 1) * C], x_tile(n * HALVES + h),
                            mean[:, t:t + 1], rstd[:, t:t + 1], ALU.subtract, ALU.mult)
                    last.then_inc(s["xn"], 1)
                    if after is not None and i:
                        after(n - 1, (i - 1) % RING)
                if after is not None:
                    after(n, i % RING)
            chain.n = at + CHUNKS * per

        def layer_norm_sqrt(act, s, c):
            act.wait_ge(s["var"], c + 1)
            nc.scalar.activation(sqrt_v[:, :], var_eps[:, :], ACT.Sqrt).then_inc(s["sqrt"], 1)

        def transpose_image(pe, s, n, b, bank):
            pe.wait_ge(s["xn"], n + 1)
            pe.wait_ge(s["copied"], n + 1)
            for kc in range(KC):
                for h in range(HALVES):
                    last = nc.tensor.transpose(bank[:, (kc * HALVES + h) * P:(kc * HALVES + h + 1) * P],
                                               xn[b][:, h * C + kc * P:h * C + (kc + 1) * P], K("ident"))
            last.then_inc(s["transposed"], 1)

        def router(tag, w_router, load, split=None):
            on = ExitStack()
            with on:
                s = {n: sem(f"{tag}_{n}") for n in ("var", "sqrt", "xn", "transposed", "copied", "logits", "chain", "shifted",
                                                    "exp", "totals", "bases", "one_hot", "spread", "filled")}
                s["stored"] = [sem(f"{tag}_stored{b}") for b in range(RING)]
                xT = [sb(f"{tag}_xT{b}", [P, KC * HALVES * P], on=on) for b in range(RING)]
                bankT = [pb(f"{tag}_bankT{b}", 512, on=on) for b in range(RING)]
                logits_ps = pb(f"{tag}_logits", TILES * E, on=on)
                sums_ps = pb(f"{tag}_sums", 2 * E, on=on)
                ids_ps = pb(f"{tag}_ids", SLOT_TILES, on=on)
                prob, work, *one_hot = [x[:, h * TILES * E:(h + 1) * TILES * E] for x in xT for h in range(2)]
                chosen = xn[0][:, 0:TILES * E]
                count = xn[0][:, TILES * E:2 * TILES * E]
                zeros = sb(f"{tag}_zeros", [P, SLOT_TILES], on=on)
                top = [sb(f"{tag}_top{k}", [P, TILES], on=on) for k in range(2)]
                row = sb(f"{tag}_row", [P, TILES], on=on)
                tiles_of = sb(f"{tag}_tiles_of", [P, E], on=on)
                ends = sb(f"{tag}_ends", [P, E], on=on)
                offset = sb(f"{tag}_offset", [P, E], on=on)
                pos = sb(f"{tag}_pos", [P, 2 * TILES], on=on)
                slot_tile = sb(f"{tag}_slot_tile", [P, 2 * TILES], on=on)
                slot_row = sb(f"{tag}_slot_row", [P, 2 * TILES], on=on)
                token = sb(f"{tag}_token", [P, TILES], on=on)
                past = xn[1][0:1, 0:SLOT_TILES // 2 * E]
                etile = sb(f"{tag}_etile", [1, SLOT_TILES], on=on)
                at_row = [xn[1][:, k * P:(k + 1) * P] for k in range(2)]
                at_tile = [sb(f"{tag}_at_tile{k}", [P, SLOT_TILES], on=on) for k in range(2)]
                block = on.enter_context(nc.Block())

                @block.sync
                def _(sp):
                    rows = h_dram.rearrange("(j p) c -> p j c", p=P)
                    for b in range(RING):
                        sp.sem_inc(s["stored"][b], 16)
                    with sp.Fori(0, IMAGES // RING) as q:
                        for b in range(RING):
                            n = q * RING + b
                            sp.wait_ge(s["xn"], n + 1)
                            sp.dma_start(rows[:, bass.ds(n * HALVES, HALVES), :],
                                         xn[b][:, :].rearrange("p (h c) -> p h c", c=C)).then_inc(s["stored"][b], 16)
                    for b in range(RING):
                        sp.wait_ge(s["stored"][b], IMAGES // RING * 16 + 16)

                if split is not None:
                    @block.gpsimd
                    def _(pool):
                        split(pool)

                @block.scalar
                def _(act):
                    act.sem_inc(s["copied"], RING)
                    with act.Fori(0, CHUNKS) as c:
                        layer_norm_sqrt(act, s, c)
                        for i in range(CHUNK_T // HALVES):
                            n = c * (CHUNK_T // HALVES) + i
                            act.wait_ge(s["transposed"], n + 1 + RING)
                            act.wait_ge(s["logits"], n + 1)
                            nc.scalar.activation(xT[i % RING][:, :], bankT[i % RING][:, :], ACT.Copy).then_inc(s["copied"], 1)
                    act.wait_ge(s["shifted"], 1)
                    nc.scalar.activation(work[:, :], prob[:, :], ACT.Exp).then_inc(s["exp"], 1)

                @block.tensor
                def _(pe):
                    pe.sem_inc(s["transposed"], RING)
                    pe.sem_inc(s["logits"], RING)
                    pe.sem_inc(s["spread"], RING)
                    pe.wait_ge(loads[load], 16)
                    with pe.Fori(0, IMAGES // RING) as q:
                        for b in range(RING):
                            transpose_image(pe, s, q * RING + b, b, bankT[b])
                        for b in range(RING):
                            n = q * RING + b
                            pe.wait_ge(s["copied"], n + 1 + RING)
                            for h in range(HALVES):
                                for kc in range(KC):
                                    last = nc.tensor.matmul(logits_ps[:, bass.ds((n * HALVES + h) * E, E)],
                                                            xT[b][:, (kc * HALVES + h) * P:(kc * HALVES + h + 1) * P],
                                                            w_router[:, kc * E:(kc + 1) * E], start=(kc == 0), stop=(kc == KC - 1))
                            last.then_inc(s["logits"], 1)
                    pe.wait_ge(s["totals"], 1)
                    totals = count[:, :].rearrange("p (e j) -> p e j", e=E)[:, :, TILES - 1]
                    nc.tensor.matmul(sums_ps[:, 0:E], K("before"), totals, start=True, stop=True)
                    nc.tensor.matmul(sums_ps[:, E:2 * E], K("ones"), totals, start=True, stop=True).then_inc(s["bases"], 1)
                    nc.tensor.matmul(ids_ps[:, :], K("ident"), zeros[:, :], start=True, stop=False)
                    with pe.Fori(0, TILES) as j:
                        for k in range(2):
                            pe.wait_ge(s["one_hot"], j * 2 + k + 1)
                            nc.tensor.matmul(ids_ps[:, :], at_row[k][:, :], at_tile[k][:, :],
                                             start=False, stop=False).then_inc(s["spread"], 1)
                    nc.tensor.matmul(ids_ps[:, :], K("ident"), zeros[:, :], start=False, stop=True).then_inc(s["filled"], 1)

                @block.vector
                def _(dve):
                    chain = Chain(dve, s["chain"])
                    chain(nc.vector.memset(zeros[:, :], 0.0))
                    layer_norm(dve, chain, s, 1e-5)

                    def by_token(t):
                        return t[:, :].rearrange("p (j e) -> p j e", e=E)

                    def over_e(t):
                        return t.unsqueeze(2).broadcast_to([P, TILES, E])

                    def over_j(t):
                        return t.unsqueeze(1).broadcast_to([P, TILES, E])
                    dve.wait_ge(s["logits"], IMAGES + RING)
                    chain(nc.vector.reduce_max(row[:, :], by_token(logits_ps), AX_X))
                    nc.vector.tensor_tensor(by_token(prob), by_token(logits_ps), over_e(row[:, :]), ALU.subtract).then_inc(s["shifted"], 1)
                    dve.wait_ge(s["exp"], 1)
                    chain(nc.vector.reduce_sum(row[:, :], by_token(work), AX_X))
                    chain(nc.vector.reciprocal(row[:, :], row[:, :]))
                    chain(nc.vector.tensor_tensor(by_token(prob), by_token(work), over_e(row[:, :]), ALU.mult))
                    for k in range(2):
                        chain(nc.vector.reduce_max(top[k][:, :], by_token(prob), AX_X))
                        chain(nc.vector.tensor_tensor(by_token(work), by_token(prob), over_e(top[k][:, :]), ALU.is_equal))
                        chain(nc.vector.tensor_tensor(by_token(work), by_token(work), over_j(K("first_wins")), ALU.mult))
                        chain(nc.vector.reduce_max(row[:, :], by_token(work), AX_X))
                        chain(nc.vector.tensor_tensor(by_token(one_hot[k]), by_token(work), over_e(row[:, :]), ALU.is_equal))
                        if k == 0:
                            chain(nc.vector.scalar_tensor_tensor(out=prob[:, :], in0=one_hot[0][:, :], scalar=-2.0, in1=prob[:, :],
                                                                 op0=ALU.mult, op1=ALU.add))
                    chain(nc.vector.tensor_tensor(row[:, :], top[0][:, :], top[1][:, :], ALU.add))
                    chain(nc.vector.reciprocal(row[:, :], row[:, :]))
                    for k in range(2):
                        chain(nc.vector.tensor_tensor(w_top[:, k * TILES:(k + 1) * TILES], top[k][:, :], row[:, :], ALU.mult))
                    for b in range(RING):
                        dve.wait_ge(s["stored"][b], IMAGES // RING * 16 + 16)
                    chain(nc.vector.tensor_tensor(chosen[:, :], one_hot[0][:, :], one_hot[1][:, :], ALU.add))
                    for e in range(E):
                        last = nc.vector.tensor_tensor_scan(count[:, e * TILES:(e + 1) * TILES], zeros[:, 0:TILES],
                                                            by_token(chosen)[:, :, e], 0.0, ALU.add, ALU.add)
                    last.then_inc(s["totals"], 1)
                    dve.wait_ge(s["bases"], 1)
                    chain(nc.vector.tensor_scalar(tiles_of[:, :], sums_ps[:, E:2 * E], 1.0 / P, (P - 1) / P - 0.5 + 0.5 / P, ALU.mult, ALU.add))
                    chain(nc.vector.tensor_scalar(tiles_of[:, :], tiles_of[:, :], ROUND, None, ALU.add))
                    chain(nc.vector.tensor_scalar(tiles_of[:, :], tiles_of[:, :], -ROUND, None, ALU.add))
                    chain(nc.vector.tensor_tensor_scan(ends[:, :], zeros[:, 0:E], tiles_of[:, :], 0.0, ALU.add, ALU.add))
                    chain(nc.vector.tensor_tensor(offset[:, :], ends[:, :], tiles_of[:, :], ALU.subtract))
                    chain(nc.vector.tensor_scalar(offset[:, :], offset[:, :], float(P), -1.0, ALU.mult, ALU.add))
                    chain(nc.vector.tensor_tensor(offset[:, :], offset[:, :], sums_ps[:, 0:E], ALU.add))
                    chain(nc.vector.tensor_tensor(by_token(chosen), count[:, :].rearrange("p (e j) -> p j e", e=E),
                                                  over_j(offset[:, :]), ALU.add))
                    for k in range(2):
                        chain(nc.vector.tensor_tensor(work[:, :], one_hot[k][:, :], chosen[:, :], ALU.mult))
                        chain(nc.vector.reduce_sum(pos[:, k * TILES:(k + 1) * TILES], by_token(work), AX_X))
                    nc.vector.tensor_copy(pos_i[:, :], pos[:, :])
                    chain(nc.vector.tensor_scalar(slot_tile[:, :], pos[:, :], 1.0 / P, -0.5 + 0.5 / P, ALU.mult, ALU.add))
                    chain(nc.vector.tensor_scalar(slot_tile[:, :], slot_tile[:, :], ROUND, None, ALU.add))
                    chain(nc.vector.tensor_scalar(slot_tile[:, :], slot_tile[:, :], -ROUND, None, ALU.add))
                    chain(nc.vector.scalar_tensor_tensor(out=slot_row[:, :], in0=slot_tile[:, :], scalar=-float(P), in1=pos[:, :],
                                                         op0=ALU.mult, op1=ALU.add))
                    half = SLOT_TILES // 2
                    pe3 = past.rearrange("p (s e) -> p s e", e=E)
                    for h in range(2):
                        tiles = slice(h * half, (h + 1) * half)
                        chain(nc.vector.tensor_tensor(pe3, K("ramp", 1)[:, tiles].unsqueeze(2).broadcast_to([1, half, E]),
                                                      ends[0:1, :].unsqueeze(1).broadcast_to([1, half, E]), ALU.is_ge))
                        chain(nc.vector.reduce_sum(etile[:, tiles], pe3, AX_X))
                    chain(nc.vector.tensor_scalar(etile_i[:, :], etile[:, :], float(E - 1), None, ALU.min))
                    chain(nc.vector.tensor_scalar(token[:, :], K("tile_base"), K("column"), None, ALU.add))
                    with dve.Fori(0, TILES) as j:
                        for k in range(2):
                            dve.wait_ge(s["spread"], j * 2 + k + 1)
                            nc.vector.tensor_scalar(at_row[k][:, :], K("ramp"), slot_row[:, bass.ds(j + k * TILES, 1)], None, ALU.is_equal)
                            nc.vector.tensor_scalar(at_tile[k][:, :], K("ramp")[:, 0:SLOT_TILES], slot_tile[:, bass.ds(j + k * TILES, 1)],
                                                    token[:, bass.ds(j, 1)], ALU.is_equal, ALU.mult).then_inc(s["one_hot"], 1)
                    dve.wait_ge(s["filled"], 1)
                    chain(nc.vector.tensor_copy(ids_i[:, :], ids_ps[:, :]))

        def mlp(tag, n_tiles, hidden, up, down, gate=None, load=(), experts=True, sink=None):
            KI = hidden // P
            DEPTH = 4
            on = ExitStack()
            with on:
                s = {n: sem(f"{tag}_{n}") for n in ("h_turned", "h_high", "h_copied", "gated", "up", "act", "a", "a_turned", "a_high",
                                                    "a_copied", "down", "y_copied", "sum")}
                s_rows = [sem(f"{tag}_rows{g}") for g in range(DEPTH)]
                s_stored = [sem(f"{tag}_stored{b}") for b in range(RING)]
                s_routed = [sem(f"{tag}_routed{g}") for g in range(DEPTH)]

                def operand(name, width, w):
                    dt = F32 if len(w) == 1 else HALF
                    return [[sb(f"{tag}_{name}{b}_{part}", [P, width], dt, on=on) for part in range(len(w))] for b in range(RING)]
                rows = [sb(f"{tag}_rows_sb{g}", [P, C], on=on) for g in range(DEPTH)]
                routed = [sb(f"{tag}_routed_sb{g}", [P, C], on=on) for g in range(DEPTH)] if not experts else None
                hT = operand("hT", C, up)
                a_sb = [sb(f"{tag}_a_sb{b}", [P, hidden], on=on) for b in range(RING)]
                aT = operand("aT", hidden, down)
                y_sb = [sb(f"{tag}_y_sb{b}", [P, C], on=on) for b in range(RING)] if experts else None
                bankH = pb(f"{tag}_bankH", 512, on=on)
                bankA = pb(f"{tag}_bankA", 512, on=on)
                bankG = [pb(f"{tag}_bankG{b}", 512, on=on) for b in range(RING)]
                bankU = [pb(f"{tag}_bankU{b}", 512, on=on) for b in range(RING)] if gate is not None else bankG
                bankY = [pb(f"{tag}_bankY{b}", 512, on=on) for b in range(RING)]
                block = on.enter_context(nc.Block())

                def steps(eng, step, prepare=lambda first, n: None):
                    rounds = (n_tiles - 2 - 2) // DEPTH
                    with eng.Fori(0, rounds) as q:
                        prepare(q * DEPTH, DEPTH + 2)
                        for i in range(2, DEPTH + 2):
                            step(q * DEPTH + i, i)
                    first = rounds * DEPTH
                    prepare(first, n_tiles - first)
                    for i in range(2, n_tiles - first):
                        step(first + i, i, ahead=first + i + 2 < n_tiles)

                @block.gpsimd
                def _(pool):
                    if experts:
                        for t in range(n_tiles):
                            if t >= DEPTH:
                                pool.wait_ge(s["h_turned"], t - DEPTH + 1)
                            nc.gpsimd.indirect_dma_start(rows[t % DEPTH][:, :], None, h_dram,
                                                         bass.IndirectOffsetOnAxis(ap=ids_i[:, t:t + 1], axis=0)).then_inc(s_rows[t % DEPTH], 16)
                    else:
                        for j in range(n_tiles):
                            for k in range(2):
                                u = j * 2 + k
                                if u >= DEPTH:
                                    pool.wait_ge(s["sum"], u - DEPTH + 1)
                                nc.gpsimd.indirect_dma_start(
                                    routed[u % DEPTH][:, :], None, y_dram,
                                    bass.IndirectOffsetOnAxis(ap=pos_i[:, j + k * TILES:j + k * TILES + 1], axis=0)).then_inc(s_routed[u % DEPTH], 16)

                @block.sync
                def _(sp):
                    if not experts:
                        def store(t):
                            sp.wait_ge(s["sum"], t * 2 + 2)
                            sp.dma_start(sink[bass.ds(t * P, P), :], x_tile(t)).then_inc(s_stored[0], 16)
                        for g in range(DEPTH):
                            sp.dma_start(rows[g][:, :], h_dram[g * P:(g + 1) * P, :]).then_inc(s_rows[g], 16)
                        with sp.Fori(1, n_tiles // DEPTH) as q:
                            for g in range(DEPTH):
                                sp.wait_ge(s["h_turned"], (q - 1) * DEPTH + g + 1)
                                sp.dma_start(rows[g][:, :], h_dram[bass.ds((q * DEPTH + g) * P, P), :]).then_inc(s_rows[g], 16)
                            for g in range(DEPTH):
                                store((q - 1) * DEPTH + g)
                        for t in range(n_tiles - DEPTH, n_tiles):
                            store(t)
                        sp.wait_ge(s_stored[0], n_tiles * 16)
                    else:
                        for b in range(RING):
                            sp.sem_inc(s_stored[b], 16)
                        with sp.Fori(0, n_tiles // RING) as q:
                            for b in range(RING):
                                sp.wait_ge(s["y_copied"], q * RING + b + 1 + RING)
                                sp.dma_start(y_dram[bass.ds((q * RING + b) * P, P), :], y_sb[b][:, :]).then_inc(s_stored[b], 16)
                        for b in range(RING):
                            sp.wait_ge(s_stored[b], n_tiles // RING * 16 + 16)

                @block.tensor
                def _(pe):
                    pe.sem_inc(s["up"], RING)
                    pe.sem_inc(s["a_turned"], RING)
                    pe.sem_inc(s["down"], RING)
                    for name, value in load:
                        pe.wait_ge(loads[name], value)

                    def turn_h(t, i):
                        pe.wait_ge(s_rows[i % DEPTH], (t - i) * (16 // DEPTH) + (i // DEPTH + 1) * 16)
                        pe.wait_ge(s["h_copied"], t + 1)
                        for kc in range(KC):
                            last = nc.tensor.transpose(bankH[:, kc * P:(kc + 1) * P], rows[i % DEPTH][:, kc * P:(kc + 1) * P], K("ident"))
                        last.then_inc(s["h_turned"], 1)

                    def turn_a(t, i):
                        pe.wait_ge(s["a"], t + 1 + RING)
                        pe.wait_ge(s["a_copied"], t + 1)
                        for k in range(KI):
                            last = nc.tensor.transpose(bankA[:, k * P:(k + 1) * P], a_sb[i % RING][:, k * P:(k + 1) * P], K("ident"))
                        last.then_inc(s["a_turned"], 1)

                    expert = []

                    def load_experts(first, n):
                        if not experts:
                            expert[:] = [0] * n
                            return
                        _, values = nc.values_load_multi_w_load_instructions(etile_i[0:1, bass.ds(first, n)], engines=[mybir.EngineType.PE],
                                                                             min_val=0, max_val=E - 1)
                        expert[:] = values

                    def project(t, i):
                        e = expert[i]
                        pe.wait_ge(s["h_copied"], t + 2)
                        pe.wait_ge(s["a"], t + 1)
                        for w, bank, done in ((gate, bankG, "gated"), (up, bankU, "up")):
                            if w is None:
                                continue
                            for kc in range(KC):
                                last = product(bank[i % RING][:, 0:hidden], [x[:, kc * P:(kc + 1) * P] for x in hT[i % RING]],
                                               [x[:, bass.ds((e * KC + kc) * hidden, hidden)] for x in w], kc == 0, kc == KC - 1)
                            last.then_inc(s[done], 1)

                    def project_back(t, i):
                        e = expert[i]
                        pe.wait_ge(s["a_copied"], t + 2)
                        pe.wait_ge(s["y_copied"], t + 1)
                        for k in range(KI):
                            last = product(bankY[i % RING][:, 0:C], [x[:, k * P:(k + 1) * P] for x in aT[i % RING]],
                                           [x[:, bass.ds((e * KI + k) * C, C)] for x in down], k == 0, k == KI - 1)
                        last.then_inc(s["down"], 1)

                    turn_h(0, 0)
                    turn_h(1, 1)
                    load_experts(0, 2)
                    project(0, 0)
                    turn_h(2, 2)
                    project(1, 1)
                    turn_h(3, 3)
                    turn_a(0, 0)

                    def step(t, i, ahead=True):
                        project(t, i)
                        if ahead:
                            turn_h(t + 2, i + 2)
                        turn_a(t - 1, i - 1)
                        project_back(t - 2, i - 2)
                    steps(pe, step, load_experts)
                    end = len(expert)
                    turn_a(n_tiles - 1, end - 1)
                    project_back(n_tiles - 2, end - 2)
                    project_back(n_tiles - 1, end - 1)

                @block.scalar
                def _(act):
                    act.sem_inc(s["h_copied"], 1)
                    act.sem_inc(s["y_copied"], RING)

                    def copy_h(t, i):
                        act.wait_ge(s["h_turned"], t + 1)
                        act.wait_ge(s["up"], t + 1)
                        nc.scalar.activation(hT[i % RING][0][:, :], bankH[:, 0:C], ACT.Copy) \
                            .then_inc(s["h_copied" if len(up) == 1 else "h_high"], 1)

                    def activate(t, i):
                        if gate is not None:
                            act.wait_ge(s["gated"], t + 1)
                        else:
                            act.wait_ge(s["up"], t + 1 + RING)
                        act.wait_ge(s["a_turned"], t + 1)
                        nc.scalar.activation(a_sb[i % RING][:, :], bankG[i % RING][:, 0:hidden],
                                             ACT.Silu if gate is not None else ACT.Relu).then_inc(s["act"], 1)

                    def copy_a(t, i):
                        act.wait_ge(s["a_turned"], t + 1 + RING)
                        act.wait_ge(s["down"], t + 1)
                        nc.scalar.activation(aT[i % RING][0][:, :], bankA[:, 0:hidden], ACT.Copy).then_inc(s["a_high"], 1)

                    def copy_y(t, i):
                        act.wait_ge(s["down"], t + 1 + RING)
                        act.wait_ge(s_stored[i % RING], (t - i) * (16 // RING) + i // RING * 16 + 16)
                        nc.scalar.activation(y_sb[i % RING][:, :], bankY[i % RING][:, 0:C], ACT.Copy).then_inc(s["y_copied"], 1)

                    def step(t, i, ahead=True):
                        activate(t, i)
                        if ahead:
                            copy_h(t + 2, i + 2)
                        if len(down) == 2 and i >= 1:
                            copy_a(t - 1, i - 1)
                        if experts and i >= 2:
                            copy_y(t - 2, i - 2)
                    copy_h(0, 0)
                    copy_h(1, 1)
                    step(0, 0)
                    step(1, 1)
                    steps(act, step)
                    if len(down) == 2:
                        copy_a(n_tiles - 1, n_tiles - 1)
                    if experts:
                        copy_y(n_tiles - 2, n_tiles - 2)
                        copy_y(n_tiles - 1, n_tiles - 1)

                @block.vector
                def _(dve):
                    dve.sem_inc(s["a"], RING)
                    dve.sem_inc(s["a_copied"], 1)

                    def low_h(t, i):
                        if len(up) == 2:
                            dve.wait_ge(s["h_high"], t + 1)
                            low_half(nc.vector, hT[i % RING][1][:, :], bankH[:, 0:C], hT[i % RING][0][:, :]).then_inc(s["h_copied"], 1)

                    def multiply(t, i):
                        dve.wait_ge(s["act"], t + 1)
                        dve.wait_ge(s["up"], t + 1 + RING)
                        nc.vector.tensor_tensor(a_sb[i % RING][:, :], a_sb[i % RING][:, :], bankU[i % RING][:, 0:hidden],
                                                ALU.mult).then_inc(s["a"], 1)

                    def copy_a(t, i):
                        if len(down) == 2:
                            dve.wait_ge(s["a_high"], t + 1)
                            low_half(nc.vector, aT[i % RING][1][:, :], bankA[:, 0:hidden], aT[i % RING][0][:, :]).then_inc(s["a_copied"], 1)
                            return
                        dve.wait_ge(s["a_turned"], t + 1 + RING)
                        dve.wait_ge(s["down"], t + 1)
                        nc.vector.tensor_copy(aT[i % RING][0][:, :], bankA[:, 0:hidden]).then_inc(s["a_copied"], 1)

                    def add_y(t, i):
                        dve.wait_ge(s["down"], t + 1 + RING)
                        nc.vector.tensor_tensor(x_tile(t), x_tile(t), bankY[i % RING][:, 0:C], ALU.add).then_inc(s["y_copied"], 1)
                        for k in range(2):
                            u = i * 2 + k
                            dve.wait_ge(s_routed[u % DEPTH], (t - i) * 8 + (u // DEPTH + 1) * 16)
                            if k == 0:
                                dve.wait_ge(s["y_copied"], t + 1 + RING)
                            else:
                                dve.wait_ge(s["sum"], t * 2 + 1)
                            nc.vector.scalar_tensor_tensor(out=x_tile(t), in0=routed[u % DEPTH][:, :],
                                                                 scalar=w_top[:, bass.ds(t + k * TILES, 1)], in1=x_tile(t),
                                                                 op0=ALU.mult, op1=ALU.add).then_inc(s["sum"], 1)

                    def step(t, i, ahead=True):
                        multiply(t, i)
                        if ahead:
                            low_h(t + 2, i + 2)
                        if i >= 1:
                            copy_a(t - 1, i - 1)
                        if not experts and i >= 2:
                            add_y(t - 2, i - 2)
                    low_h(0, 0)
                    low_h(1, 1)
                    step(0, 0)
                    step(1, 1)
                    steps(dve, step)
                    copy_a(n_tiles - 1, n_tiles - 1)
                    if not experts:
                        add_y(n_tiles - 2, n_tiles - 2)
                        add_y(n_tiles - 1, n_tiles - 1)

        def entry_convolution(on):
            W2 = COLS + 2
            IMG = (ROWS + 2) * W2
            DEPTH = 4
            s = {n: sem(f"conv_{n}") for n in ("var", "sqrt", "xn", "transposed", "high", "copied", "border", "chain", "conv", "feat", "pooled",
                                               "w_high", "w_low", "sum", "complete")}
            s_in = [sem(f"conv_in{g}") for g in range(DEPTH)]
            y_in = [sb(f"conv_y{g}", [P, C], on=on) for g in range(DEPTH)]
            w_raw = sb("conv_w_raw", [P, 9 * KC * F], on=on)
            w_half = [sb(f"conv_w_half{n}", [P, 9 * KC * F], HALF, on=on) for n in range(2)]
            bankT = [pb(f"conv_bankT{b}", 512, on=on) for b in range(RING)]
            bankC = [pb(f"conv_bankC{b}", 512, on=on) for b in range(RING)]
            pool_ps = pb("conv_pool", KC * IMAGES, on=on)
            padded = [sb(f"conv_padded{n}", [P, KC * IMAGES * IMG], HALF, on=on) for n in range(2)]
            block = on.enter_context(nc.Block())

            def image(part, kc, n):
                return padded[part][:, bass.ds(kc * IMAGES * IMG + n * IMG, IMG)].rearrange("p (y z) -> p y z", z=W2)[:, 1:ROWS + 1, 1:COLS + 1]

            def turned(b, kc):
                return bankT[b][:, kc * 256:(kc + 1) * 256].rearrange("p (y z) -> p y z", z=COLS)

            @block.sync
            def _(sp):
                sp.dma_start(w_raw[:, :], A["conv_w"]).then_inc(loads["conv"], 16)
                load_attention(sp)

            @block.gpsimd
            def _(pool):
                for j in range(TILES):
                    for k in range(2):
                        u = j * 2 + k
                        if u >= DEPTH:
                            pool.wait_ge(s["sum"], u - DEPTH + 1)
                        nc.gpsimd.indirect_dma_start(
                            y_in[u % DEPTH][:, :], None, y_dram,
                            bass.IndirectOffsetOnAxis(ap=pos_i[:, j + k * TILES:j + k * TILES + 1], axis=0)).then_inc(s_in[u % DEPTH], 16)

            @block.scalar
            def _(act):
                act.sem_inc(s["feat"], 1)
                act.wait_ge(loads["conv"], 16)
                nc.scalar.activation(w_half[0][:, :], w_raw[:, :], ACT.Copy).then_inc(s["w_high"], 1)
                act.wait_ge(loads["attn"], ATTN_LOADS * 16)
                act.wait_ge(s["border"], 1)

                def copy(n, b):
                    act.wait_ge(s["transposed"], n + 1 + RING)
                    for kc in range(KC):
                        last = nc.scalar.activation(image(0, kc, n), turned(b, kc), ACT.Copy)
                    last.then_inc(s["high"], 1)

                def relu(g, b):
                    act.wait_ge(s["conv"], g + 1)
                    nc.scalar.activation(feat[:, bass.ds(g * 512, 512)], bankC[b][:, :], ACT.Relu,
                                         bias=entry_sb[:, 1:2], scale=entry_sb[:, 0:1]).then_inc(s["feat"], 1)

                def chunk(c, first=False, last=False):
                    copy(c * 4, 0)
                    copy(c * 4 + 1, 1)
                    if not first:
                        relu(c * 2 - 1, 1)
                    copy(c * 4 + 2, 0)
                    copy(c * 4 + 3, 1)
                    if not last:
                        layer_norm_sqrt(act, s, c + 1)
                    relu(c * 2, 0)
                layer_norm_sqrt(act, s, 0)
                chunk(0, first=True)
                with act.Fori(1, CHUNKS - 1) as c:
                    chunk(c)
                chunk(CHUNKS - 1, last=True)
                relu(CHUNKS * 2 - 1, 1)

            @block.vector
            def _(dve):
                chain = Chain(dve, s["chain"])
                dve.sem_inc(s["copied"], RING)
                for part in range(2):
                    images = padded[part][:, :].bitcast(F32).rearrange("p (n i) -> p n i", i=IMG)
                    nc.vector.memset(images[:, :, 0:W2], 0.0)
                    nc.vector.memset(images[:, :, IMG - W2:IMG], 0.0)
                    by_row = images.rearrange("p n (y z) -> p n y z", z=W2)
                    nc.vector.memset(by_row[:, :, 1:ROWS + 1, 0:1], 0.0)
                    last = nc.vector.memset(by_row[:, :, 1:ROWS + 1, W2 - 1:W2], 0.0)
                last.then_inc(s["border"], 1)
                dve.wait_ge(s["w_high"], 1)
                low_half(nc.vector, w_half[1][:, :], w_raw[:, :], w_half[0][:, :]).then_inc(s["w_low"], 1)

                def add_routed(c):
                    for t in range(CHUNK_T):
                        for k in range(2):
                            j, u = c * CHUNK_T + t, t * 2 + k
                            dve.wait_ge(s_in[u % DEPTH], c * (CHUNK_T * 2 // DEPTH * 16) + (u // DEPTH + 1) * 16)
                            if k == 1:
                                dve.wait_ge(s["sum"], c * (CHUNK_T * 2) + u)
                            nc.vector.scalar_tensor_tensor(out=x_tile(j), in0=y_in[u % DEPTH][:, :], scalar=w_top[:, bass.ds(j + k * TILES, 1)],
                                                           in1=x_tile(j), op0=ALU.mult, op1=ALU.add).then_inc(s["sum"], 1)
                    dve.wait_ge(s["sum"], c * (CHUNK_T * 2) + CHUNK_T * 2)
                    dve.sem_inc(s["complete"], 1)

                def lows(n, b):
                    dve.wait_ge(s["high"], n + 1)
                    for kc in range(KC):
                        last = low_half(nc.vector, image(1, kc, n), turned(b, kc), image(0, kc, n))
                    last.then_inc(s["copied"], 1)
                layer_norm(dve, chain, s, 1e-6, before=add_routed, after=lows)
                dve.wait_ge(s["pooled"], IMAGES)
                chain(nc.vector.tensor_scalar(pooled[:, :], pool_ps[:, :], 1.0 / (ROWS * COLS), None, ALU.mult))

            @block.tensor
            def _(pe):
                pe.sem_inc(s["transposed"], RING)

                def turn(n, b):
                    pe.wait_ge(s["xn"], n + 1)
                    for kc in range(KC):
                        for h in range(HALVES):
                            last = nc.tensor.matmul(pool_ps[:, bass.ds(kc * IMAGES + n, 1)], xn[b][:, h * C + kc * P:h * C + (kc + 1) * P],
                                                    K("ones")[:, 0:1], start=(h == 0), stop=(h == HALVES - 1))
                    last.then_inc(s["pooled"], 1)
                    transpose_image(pe, s, n, b, bankT[b])

                def convolve(g, b):
                    pe.wait_ge(s["copied"], g * 2 + 2 + RING)
                    pe.wait_ge(s["feat"], g)
                    for step in range(9 * KC):
                        kc, dr, dc = step // 9, step % 9 // 3, step % 3
                        pair = [x[:, bass.ds(kc * IMAGES * IMG + g * 2 * IMG, 2 * IMG)].rearrange("p (n y z) -> p n y z", n=2, z=W2)
                                [:, :, dr:dr + ROWS, dc:dc + COLS] for x in padded]
                        at = ((dr * 3 + dc) * KC + kc) * F
                        last = product(bankC[b][:, :], [x[:, at:at + F] for x in w_half], pair, step == 0, step == 9 * KC - 1)
                    last.then_inc(s["conv"], 1)
                turn(0, 0)
                turn(1, 1)
                turn(2, 0)
                turn(3, 1)
                pe.wait_ge(s["w_low"], 1)
                convolve(0, 0)
                with pe.Fori(0, (IMAGES // 2 - 2) // 2) as q:
                    for b in range(2):
                        g = q * 2 + b + 1
                        turn(g * 2 + 2, 0)
                        turn(g * 2 + 3, 1)
                        convolve(g, 1 - b)
                convolve(IMAGES // 2 - 1, 1)

        def axial_scores(split):
            on = ExitStack()
            with on:
                STEPS = IMAGES // 2
                names = ("projected", "queries", "values_t", "values", "chain", "att")
                s = {n: sem(f"axial_{n}") for n in names}
                for ax in ("down", "along"):
                    for n in ("scores", "max", "exp", "soft", "turned", "turned_sb"):
                        s[n, ax] = sem(f"axial_{n}_{ax}")
                s["att_sb"] = sem("axial_att_sb")
                bankQ, bankF, bankV, bankO = (pb(f"axial_{n}", 512, on=on) for n in ("bankQ", "bankF", "bankV", "bankO"))
                bankS = {ax: pb(f"axial_bankS_{ax}", 512, on=on) for ax in ("down", "along")}
                bankP = {ax: pb(f"axial_bankP_{ax}", 512, on=on) for ax in ("down", "along")}
                q = {ax: [sb(f"axial_q_{ax}{b}", [G, 512], on=on) for b in range(RING)] for ax in ("down", "along")}
                val_t = [sb(f"axial_val_t{b}", [F, 512], on=on) for b in range(RING)]
                val = [sb(f"axial_val{b}", [P, 512], on=on) for b in range(RING)]
                expo = {ax: [sb(f"axial_exp_{ax}{b}", [P, 512], on=on) for b in range(RING)] for ax in ("down", "along")}
                nmax = {ax: sb(f"axial_nmax_{ax}", [P, 4], on=on) for ax in ("down", "along")}
                total = {ax: sb(f"axial_total_{ax}", [P, 4], on=on) for ax in ("down", "along")}
                att_down = sb("axial_att_down", [P, 512], on=on)
                mask = {"down": "same_col", "along": "same_row"}
                block = on.enter_context(nc.Block())

                def by_column(image):
                    return image.rearrange("p (y h z) -> p h y z", y=ROWS, h=2)

                def steps(eng, step):
                    step(0, 0, first=True)
                    with eng.Fori(0, (STEPS - 2) // 2) as r:
                        step(r * 2 + 1, 1)
                        step(r * 2 + 2, 0)
                    step(STEPS - 1, (STEPS - 1) % 2, last=True)

                @block.gpsimd
                def _(pool):
                    split(pool)

                @block.tensor
                def _(pe):
                    pe.sem_inc(s["values_t"], RING)
                    pe.wait_ge(loads["attn"], ATTN_LOADS * 16)

                    def project(g):
                        pe.wait_ge(s["queries"], g)
                        nc.tensor.matmul(bankQ[0:64, :], qk_w[:, :], feat[:, bass.ds(g * 512, 512)], start=True, stop=True)
                        nc.tensor.matmul(bankF[:, :], val_w[:, :], feat[:, bass.ds(g * 512, 512)],
                                         start=True, stop=True).then_inc(s["projected"], 1)

                    def scores(g, b):
                        pe.wait_ge(s["queries"], g + 1)
                        for ax in ("down", "along"):
                            pe.wait_ge(s["exp", ax], g)
                            for t in range(4):
                                qt = q[ax][b][:, t * P:(t + 1) * P]
                                nc.tensor.matmul(bankS[ax][:, t * P:(t + 1) * P], K(mask[ax] + "_l", 9), K(mask[ax] + "_r", 9), start=True, stop=False)
                                last = nc.tensor.matmul(bankS[ax][:, t * P:(t + 1) * P], qt, qt, start=False, stop=True)
                            last.then_inc(s["scores", ax], 1)
                        pe.wait_ge(s["values"], g)
                        for t in range(4):
                            last = nc.tensor.transpose(bankV[:, t * P:(t + 1) * P], val_t[b][:, t * P:(t + 1) * P], K("ident"))
                        last.then_inc(s["values_t"], 1)

                    def attend(g, b):
                        for ax in ("down", "along"):
                            pe.wait_ge(s["soft", ax], g + 1)
                            pe.wait_ge(s["turned_sb", ax], g)
                            for t in range(4):
                                last = nc.tensor.transpose(bankP[ax][:, t * P:(t + 1) * P], expo[ax][b][:, t * P:(t + 1) * P], K("ident"))
                            last.then_inc(s["turned", ax], 1)
                        pe.wait_ge(s["turned_sb", "down"], g + 1)
                        pe.wait_ge(s["values"], g + 1)
                        pe.wait_ge(s["att_sb"], g)
                        for t in range(4):
                            last = nc.tensor.matmul(bankO[:, t * P:(t + 1) * P], val[b][:, t * P:(t + 1) * P],
                                                    att_down[:, t * P:(t + 1) * P], start=True, stop=True)
                        last.then_inc(s["att"], 1)

                    def step(g, b, first=False, last=False):
                        scores(g, b)
                        if not first:
                            attend(g - 1, 1 - b)
                        if not last:
                            project(g + 1)
                    project(0)
                    steps(pe, step)
                    attend(STEPS - 1, (STEPS - 1) % 2)

                @block.scalar
                def _(act):
                    def queries(g, b):
                        act.wait_ge(s["projected"], g + 1)
                        act.wait_ge(s["values_t"], g + 1)
                        for n in range(2):
                            part = slice(n * 256, (n + 1) * 256)
                            nc.scalar.activation(q["down"][b][:, part].rearrange("p (h y z) -> p h y z", h=2, y=ROWS),
                                                 by_column(bankQ[0:G, part]), ACT.Relu, bias=qk_sb[0:G, 1:2], scale=qk_sb[0:G, 0:1])
                            nc.scalar.activation(val_t[b][:, part].rearrange("p (h y z) -> p h y z", h=2, y=ROWS),
                                                 by_column(bankF[:, part]), ACT.Relu, bias=val_sb[:, 1:2], scale=val_sb[:, 0:1])
                        nc.scalar.activation(q["along"][b][:, :], bankQ[32:32 + G, :], ACT.Relu, bias=qk_sb[32:32 + G, 1:2],
                                             scale=qk_sb[32:32 + G, 0:1]).then_inc(s["queries"], 1)

                    def exponentials(g, b):
                        for ax in ("down", "along"):
                            act.wait_ge(s["max", ax], g + 1)
                            for t in range(4):
                                last = nc.scalar.activation(expo[ax][b][:, t * P:(t + 1) * P], bankS[ax][:, t * P:(t + 1) * P], ACT.Exp,
                                                            bias=nmax[ax][:, t:t + 1], accum_out=total[ax][:, t:t + 1])
                            last.then_inc(s["exp", ax], 1)

                    def step(g, b, first=False, last=False):
                        exponentials(g, b)
                        if not last:
                            queries(g + 1, 1 - b)
                    act.wait_ge(loads["attn"], ATTN_LOADS * 16)
                    queries(0, 0)
                    steps(act, step)

                @block.vector
                def _(dve):
                    chain = Chain(dve, s["chain"])

                    def copies(g, b):
                        dve.wait_ge(s["turned", "down"], g + 1)
                        nc.vector.tensor_copy(att_down[:, :], bankP["down"][:, :]).then_inc(s["turned_sb", "down"], 1)
                        dve.wait_ge(s["turned", "along"], g + 1)
                        nc.vector.tensor_copy(att_along[:, bass.ds(g * 512, 512)], bankP["along"][:, :]).then_inc(s["turned_sb", "along"], 1)
                        dve.wait_ge(s["att"], g + 1)
                        for n in range(2):
                            last = nc.vector.tensor_copy(by_column(att_t[:, bass.ds(g * 512 + n * 256, 256)]),
                                                         bankO[:, n * 256:(n + 1) * 256].rearrange("p (h y z) -> p h y z", h=2, y=ROWS))
                        last.then_inc(s["att_sb"], 1)

                    def step(g, b, first=False, last=False):
                        for ax in ("down", "along"):
                            dve.wait_ge(s["scores", ax], g + 1)
                            nc.vector.tensor_reduce(nmax[ax][:, :], bankS[ax][:, :].rearrange("p (t j) -> p t j", t=4), AX_X, ALU.max,
                                                    negate=True).then_inc(s["max", ax], 1)
                        dve.wait_ge(s["values_t"], g + 1 + RING)
                        nc.vector.tensor_copy(val[b][:, :], bankV[:, :]).then_inc(s["values"], 1)
                        if not first:
                            copies(g - 1, 1 - b)
                        for n, ax in enumerate(("down", "along")):
                            dve.wait_ge(s["exp", ax], g + 1)
                            chain.n = g * 2 + n
                            chain(nc.vector.reciprocal(total[ax][:, :], total[ax][:, :]))
                            e3 = expo[ax][b][:, :].rearrange("p (t j) -> p t j", t=4)
                            nc.vector.tensor_tensor(e3, e3, total[ax][:, :].unsqueeze(2).broadcast_to([P, 4, P]),
                                                    ALU.mult).then_inc(s["soft", ax], 1)
                    steps(dve, step)
                    copies(STEPS - 1, (STEPS - 1) % 2)

        def gate_network(on, tag, s, in_ps, sums, w0, wh, we, gate):
            hidden = [sb(f"{tag}_hidden{b}", [HID, IMAGES * 16], on=on) for b in range(2)]
            small = sb(f"{tag}_small", [HID, IMAGES * 16], on=on)
            LAYERS = 5

            def tensor(pe):
                pe.wait_ge(s["sums"], 1)
                for n in range(LAYERS):
                    w = w0 if n == 0 else wh[:, (n - 1) * HID:n * HID]
                    if n:
                        pe.wait_ge(s["leaky"], n)
                    nc.tensor.matmul(in_ps[0:HID, 0:256], w, sums[:, :] if n == 0 else hidden[(n - 1) % 2][:, :],
                                     start=True, stop=True).then_inc(s["layer"], 1)
                pe.wait_ge(s["leaky"], LAYERS)
                nc.tensor.matmul(in_ps[:, 0:256], we, hidden[(LAYERS - 1) % 2][:, :], start=True, stop=True).then_inc(s["layer"], 1)

            def vector(dve, chain):
                for n in range(LAYERS):
                    dve.wait_ge(s["layer"], n + 1)
                    chain(nc.vector.tensor_scalar(small[:, :], in_ps[0:HID, 0:256], 0.2, None, ALU.mult))
                    nc.vector.tensor_tensor(hidden[n % 2][:, :], small[:, :], in_ps[0:HID, 0:256], ALU.max).then_inc(s["leaky"], 1)

            def scalar(act):
                act.wait_ge(s["layer"], LAYERS + 1)
                nc.scalar.activation(gate[:, :], in_ps[:, 0:256], ACT.Sigmoid).then_inc(s["gate"], 1)
            return tensor, vector, scalar

        def axial_along():
            on = ExitStack()
            with on:
                s = {n: sem(f"rows_{n}") for n in ("sums", "layer", "leaky", "gate", "chain", "gated", "turned", "turned_sb", "att", "att_sb")}
                sums = sb("rows_sums", [F, 256], on=on)
                gate = sb("rows_gate", [F, 256], on=on)
                gated = [sb(f"rows_gated{b}", [F, 512], on=on) for b in range(RING)]
                val = [sb(f"rows_val{b}", [P, 512], on=on) for b in range(RING)]
                bankG = pb("rows_bankG", 512, on=on)
                bankX = [pb(f"rows_bankX{b}", 512, on=on) for b in range(RING)]
                bankO = [pb(f"rows_bankO{b}", 512, on=on) for b in range(RING)]
                g_tensor, g_vector, g_scalar = gate_network(on, "rows", s, bankG, sums, gates_w[:, 0:HID], gates_wh[:, 0:4 * HID],
                                                            gates_we[:, 0:F], gate)
                block = on.enter_context(nc.Block())

                @block.tensor
                def _(pe):
                    pe.sem_inc(s["turned"], RING)
                    pe.sem_inc(s["att"], RING)
                    g_tensor(pe)

                    def turn(g, b):
                        pe.wait_ge(s["gated"], g + 1)
                        pe.wait_ge(s["turned_sb"], g + 1)
                        for t in range(4):
                            last = nc.tensor.transpose(bankX[b][:, t * P:(t + 1) * P], gated[b][:, t * P:(t + 1) * P], K("ident"))
                        last.then_inc(s["turned"], 1)

                    def attend(g, b):
                        pe.wait_ge(s["turned_sb"], g + 1 + RING)
                        pe.wait_ge(s["att_sb"], g + 1)
                        for t in range(4):
                            last = nc.tensor.matmul(bankO[b][:, t * P:(t + 1) * P], val[b][:, t * P:(t + 1) * P],
                                                    att_along[:, bass.ds((g * 4 + t) * P, P)], start=True, stop=True)
                        last.then_inc(s["att"], 1)
                    with pe.Fori(0, IMAGES // 4) as r:
                        for b in range(2):
                            turn(r * 2 + b, b)
                        for b in range(2):
                            attend(r * 2 + b, b)

                @block.scalar
                def _(act):
                    act.sem_inc(s["turned_sb"], RING)
                    act.sem_inc(s["att_sb"], RING)
                    g_scalar(act)
                    with act.Fori(0, IMAGES // 4) as r:
                        for b in range(2):
                            g = r * 2 + b
                            act.wait_ge(s["turned"], g + 1 + RING)
                            act.wait_ge(s["att"], g + 1)
                            nc.scalar.activation(val[b][:, :], bankX[b][:, :], ACT.Copy).then_inc(s["turned_sb"], 1)
                        for b in range(2):
                            g = r * 2 + b
                            act.wait_ge(s["att"], g + 1 + RING)
                            nc.scalar.activation(feat[:, bass.ds(g * 512, 512)], bankO[b][:, :], ACT.Copy).then_inc(s["att_sb"], 1)

                @block.vector
                def _(dve):
                    chain = Chain(dve, s["chain"])
                    chain(nc.vector.reduce_sum(sums[:, :], att_t[:, :].rearrange("p (r c) -> p r c", c=COLS), AX_X))
                    nc.vector.tensor_scalar(sums[:, :], sums[:, :], 1.0 / (ROWS * COLS), None, ALU.mult).then_inc(s["sums"], 1)
                    g_vector(dve, chain)
                    dve.wait_ge(s["gate"], 1)
                    with dve.Fori(0, IMAGES // 4) as r:
                        for b in range(2):
                            g = r * 2 + b
                            dve.wait_ge(s["turned"], g + 1)
                            nc.vector.tensor_tensor(gated[b][:, :].rearrange("p (r c) -> p r c", c=COLS),
                                                    att_t[:, bass.ds(g * 512, 512)].rearrange("p (r c) -> p r c", c=COLS),
                                                    gate[:, bass.ds(g * 32, 32)].unsqueeze(2).broadcast_to([F, 32, COLS]),
                                                    ALU.mult).then_inc(s["gated"], 1)

        def attention_output():
            on = ExitStack()
            with on:
                s = {n: sem(f"cols_{n}") for n in ("sums", "layer", "leaky", "gate", "chain", "gated", "out", "added", "weights", "branch", "branch_sb")}
                sums = sb("cols_sums", [F, 256], on=on)
                gate = sb("cols_gate", [F, 256], on=on)
                gated = [sb(f"cols_gated{b}", [F, 512], on=on) for b in range(RING)]
                branch = sb("cols_branch", [IMAGES, F], on=on)
                picked = [sb(f"cols_picked{b}", [IMAGES, 2 * P], on=on) for b in range(RING)]
                bankG = pb("cols_bankG", 512, on=on)
                bankI = pb("cols_bankI", 512, on=on)
                bankO = [pb(f"cols_bankO{b}", 512, on=on) for b in range(RING)]
                bankB = [pb(f"cols_bankB{b}", 512, on=on) for b in range(RING)]
                g_tensor, g_vector, g_scalar = gate_network(on, "cols", s, bankG, sums, gates_w[:, HID:2 * HID],
                                                            gates_wh[:, 4 * HID:8 * HID], gates_we[:, F:2 * F], gate)
                block = on.enter_context(nc.Block())

                @block.tensor
                def _(pe):
                    pe.sem_inc(s["out"], RING)
                    pe.wait_ge(s["weights"], 3)
                    nc.tensor.matmul(bankI[0:IMAGES, 0:F], K("ones", 1)[:, 0:IMAGES], out_rows[:, 3 * F:4 * F], start=True, stop=False)
                    for kc in range(KC):
                        last = nc.tensor.matmul(bankI[0:IMAGES, 0:F], pooled[:, kc * IMAGES:(kc + 1) * IMAGES], il_w[:, kc * F:(kc + 1) * F],
                                                start=False, stop=(kc == KC - 1))
                    last.then_inc(s["branch"], 1)
                    g_tensor(pe)
                    pe.wait_ge(s["branch_sb"], 1)
                    with pe.Fori(0, IMAGES // 4) as r:
                        for b in range(2):
                            g = r * 2 + b
                            pe.wait_ge(s["gated"], g + 1)
                            pe.wait_ge(s["added"], g + 1)
                            for n in range(2):
                                nc.tensor.matmul(bankB[b][:, n * F:(n + 1) * F], picked[b][:, n * P:(n + 1) * P], branch[:, :],
                                                 start=True, stop=True)
                            for t in range(4):
                                nc.tensor.matmul(bankO[b][:, t * P:(t + 1) * P], K("ones", 1), out_rows[:, 2 * F:3 * F], start=True, stop=False)
                                last = nc.tensor.matmul(bankO[b][:, t * P:(t + 1) * P], gated[b][:, t * P:(t + 1) * P], end_w[:, :],
                                                        start=False, stop=True)
                            last.then_inc(s["out"], 1)

                @block.scalar
                def _(act):
                    act.wait_ge(s["branch"], 1)
                    nc.scalar.activation(branch[:, :], bankI[0:IMAGES, 0:F], ACT.Relu).then_inc(s["branch_sb"], 1)
                    g_scalar(act)

                @block.vector
                def _(dve):
                    chain = Chain(dve, s["chain"])
                    dve.sem_inc(s["added"], RING)
                    nc.vector.tensor_tensor(end_w[:, :], end_w[:, :], scales_b[:, 0:F], ALU.mult).then_inc(s["weights"], 1)
                    for kc in range(KC):
                        nc.vector.tensor_tensor(il_w[:, kc * F:(kc + 1) * F], il_w[:, kc * F:(kc + 1) * F], scales_b[:, F:2 * F],
                                                ALU.mult).then_inc(s["weights"], 1)
                    chain(nc.vector.reduce_sum(sums[:, :].rearrange("p (n c) -> p n c", c=COLS),
                                               feat[:, :].rearrange("p (n r c) -> p n c r", n=IMAGES, c=COLS), AX_X))
                    nc.vector.tensor_scalar(sums[:, :], sums[:, :], 1.0 / (ROWS * COLS), None, ALU.mult).then_inc(s["sums"], 1)
                    g_vector(dve, chain)
                    dve.wait_ge(s["gate"], 1)

                    def apply_gate(g, b):
                        dve.wait_ge(s["out"], g + 1)
                        for n in range(2):
                            nc.vector.tensor_tensor(gated[b][:, n * 256:(n + 1) * 256].rearrange("p (r c) -> p r c", c=COLS),
                                                    feat[:, bass.ds(g * 512 + n * 256, 256)].rearrange("p (r c) -> p r c", c=COLS),
                                                    gate[:, bass.ds(g * 32 + n * 16, 16)].unsqueeze(1).broadcast_to([F, ROWS, COLS]), ALU.mult)
                        nc.vector.tensor_copy(picked[b][:, :].rearrange("p (n z) -> p n z", n=2),
                                              K("ident", IMAGES)[:, bass.ds(g * 2, 2)].unsqueeze(2).broadcast_to([IMAGES, 2, P])).then_inc(s["gated"], 1)

                    def add(g, b):
                        dve.wait_ge(s["out"], g + 1 + RING)
                        x4 = x_res[:, bass.ds(g * 4 * C, 4 * C)].rearrange("p (t c) -> p t c", c=C)
                        nc.vector.scalar_tensor_tensor(out=x4[:, :, 0:F], in0=bankO[b][:, :].rearrange("p (t c) -> p t c", c=F), scalar=0.0,
                                                       in1=x4[:, :, 0:F], op0=ALU.max, op1=ALU.add)
                        x22 = x_res[:, bass.ds(g * 4 * C, 4 * C)].rearrange("p (n h c) -> p n h c", n=2, c=C)
                        nc.vector.tensor_tensor(x22[:, :, :, F:2 * F], x22[:, :, :, F:2 * F],
                                                bankB[b][:, 0:2 * F].rearrange("p (n c) -> p n c", n=2).unsqueeze(2).broadcast_to([P, 2, 2, F]),
                                                ALU.add).then_inc(s["added"], 1)
                    with dve.Fori(0, IMAGES // 4) as r:
                        for b in range(2):
                            apply_gate(r * 2 + b, b)
                        for b in range(2):
                            add(r * 2 + b, b)

        with ExitStack() as on:
            s = {n: sem(f"mix_{n}") for n in ("var", "sqrt", "xn", "transposed", "copied", "dft", "chain", "chain_act",
                                              "arg", "sin", "emb", "theta", "magnitude2", "magnitude", "block_diag",
                                              "spectrum", "mixed", "norm", "scaled", "turned", "turned_sb", "row", "added")}
            place_tables("konst_mix", on)
            xT = [sb(f"mix_xT{b}", [P, KC * HALVES * P], on=on) for b in range(RING)]
            bankT = [pb(f"mix_bankT{b}", 512, on=on) for b in range(RING)]
            spec_ps = pb("mix_spec", TILES * 2 * MODES, on=on)
            mix_ps = pb("mix_mix", MODES * 2 * TILES, on=on)
            small_ps = pb("mix_small", 512, on=on)
            t_b = sb("mix_t", [2 * MODES, ROWS], on=on)
            w_rep = sb("mix_w", [P, COLS * MODES * 2], on=on)
            w_abs = sb("mix_wabs", [P, COLS * MODES], on=on)
            w_sq = sb("mix_wsq", [P, COLS * MODES], on=on)
            ke = sb("mix_ke", [2 * MODES, 2 * MODES], on=on)
            bias_b = sb("mix_bias", [P, 2 * MODES], on=on)
            arg = sb("mix_arg", [2 * MODES, ROWS], on=on)
            turns = sb("mix_turns", [2 * MODES, ROWS], on=on)
            emb = sb("mix_emb", [2 * MODES, ROWS], on=on)
            emb_x = sb("mix_embx", [2 * MODES, ROWS * COLS], on=on)
            theta = sb("mix_theta", [P, HALVES * 2 * MODES], on=on)
            theta_sq = sb("mix_theta_sq", [P, HALVES * MODES], on=on)
            theta_abs = sb("mix_theta_abs", [P, HALVES * MODES], on=on)
            bd = [sb(f"mix_bd{r}", [P, MODES * P], on=on) for r in range(3)]
            spec = sb("mix_spec_sb", [P, MODES * 3 * TILES], on=on)
            tmp = [sb(f"mix_tmp{b}", [P, IMAGES * MODES], on=on) for b in range(2)]
            rnorm = sb("mix_rnorm", [P, HALVES * MODES], on=on)
            scaled = sb("mix_scaled", [P, TILES * 2 * MODES], on=on)
            def inverse_bank(n):
                return (spec_ps, mix_ps)[n // 2 % 2][:, n % 2 * 512:(n % 2 + 1) * 512], 8 * (n // 4) + n % 4

            turned = sb("mix_turned", [P, 8 * P], on=on)

            block = on.enter_context(nc.Block())

            @block.sync
            def _(sp):
                for kind in ("konst", "konst_mix"):
                    sp.dma_start(konst[kind][:, :], A[kind]).then_inc(loads["konst"], 16)
                x_rows = A["x"].rearrange("(j p) c -> p j c", p=P)
                for c in range(CHUNKS):
                    dst = x_res[:, c * CHUNK_T * C:(c + 1) * CHUNK_T * C].rearrange("p (j c) -> p j c", c=C)
                    sp.dma_start(dst, x_rows[:, c * CHUNK_T:(c + 1) * CHUNK_T, :]).then_inc(loads["x"], 16)
                sp.dma_start(router0[:, :], A["L0_ffn_router_w"]).then_inc(loads["router0"], 16)
                sp.wait_ge(loads["x"], CHUNKS * 16)
                for dst, name in ((gate0, "gate"), (up0, "up")):
                    sp.dma_start(dst[:, :], A[f"L0_ffn_{name}_w"], max_dma_last_dim=32768).then_inc(loads["w0"], 16)

            @block.scalar
            def _(act):
                act.dma_start(t_b[:, :], A["L0_conv_t"].unsqueeze(0).broadcast_to([2 * MODES, ROWS])).then_inc(loads["spectral"], 16)
                act.dma_start(ke[:, :], A["L0_conv_ke_weights"]).then_inc(loads["spectral"], 16)
                act.dma_start(bias_b[:, :], A["L0_conv_ke_bias"].broadcast_to([P, 2 * MODES])).then_inc(loads["spectral"], 16)
                for r in range(ROWS_T):
                    act.dma_start(w_rep[r * COLS:(r + 1) * COLS, :], A["L0_conv_weights1"]).then_inc(loads["spectral"], 16)
                act.wait_ge(s["arg"], 1)
                nc.scalar.activation(emb[:, :], arg[:, :], ACT.Sin).then_inc(s["sin"], 1)
                act.wait_ge(s["magnitude2"], 2)
                nc.scalar.activation(theta_abs[:, :], theta_sq[:, :], ACT.Sqrt).then_inc(s["magnitude"], 1)
                nc.scalar.activation(w_abs[:, :], w_sq[:, :], ACT.Sqrt).then_inc(s["magnitude"], 1)
                act.sem_inc(s["copied"], RING)
                with act.Fori(0, CHUNKS) as c:
                    layer_norm_sqrt(act, s, c)
                    for i in range(CHUNK_T // HALVES):
                        n = c * (CHUNK_T // HALVES) + i
                        act.wait_ge(s["transposed"], n + 1 + RING)
                        act.wait_ge(s["dft"], n + 1)
                        nc.scalar.activation(xT[i % RING][:, :], bankT[i % RING][:, :], ACT.Copy).then_inc(s["copied"], 1)
                for g in range(2):
                    act.wait_ge(s["turned"], g + 1)
                    nc.scalar.activation(turned[:, g * 512:(g + 1) * 512], bankT[g][:, :], ACT.Copy).then_inc(s["turned_sb"], 1)

            @block.gpsimd
            def _(pool):
                pool.wait_ge(loads["konst"], 2 * 16)
                pool.wait_ge(loads["spectral"], (3 + ROWS_T) * 16)
                shape = [P, MODES, ROWS_T, COLS]
                w4 = w_rep[:, :].rearrange("p (o m r) -> p m o r", m=MODES, r=2)
                rows = K("row_of").unsqueeze(1).unsqueeze(3)
                for r in range(2):
                    for m in range(MODES):
                        last = nc.gpsimd.tensor_tensor(
                            bd[r][:, m * P:(m + 1) * P].rearrange("p (t o) -> p t o", o=COLS),
                            w4[:, m, :, r].unsqueeze(1).broadcast_to([P, ROWS_T, COLS]),
                            K("row_of").unsqueeze(2).broadcast_to([P, ROWS_T, COLS]), ALU.mult)
                    last.then_inc(s["block_diag"], 1)
                pool.wait_ge(s["magnitude"], 2)
                wa = w_abs[:, :].rearrange("p (o m) -> p m o", m=MODES)
                for m in range(MODES):
                    last = nc.gpsimd.tensor_tensor(
                        bd[2][:, m * P:(m + 1) * P].rearrange("p (t o) -> p t o", o=COLS),
                        wa[:, m, :].unsqueeze(1).broadcast_to([P, ROWS_T, COLS]),
                        K("row_of").unsqueeze(2).broadcast_to([P, ROWS_T, COLS]), ALU.mult)
                last.then_inc(s["block_diag"], 1)

            @block.vector
            def _(dve):
                chain = Chain(dve, s["chain"])
                dve.wait_ge(loads["konst"], 2 * 16)
                dve.wait_ge(loads["spectral"], (3 + ROWS_T) * 16)
                freq, phase = K("freq", 2 * MODES), K("phase", 2 * MODES)
                chain(nc.vector.tensor_scalar(arg[:, :], t_b[:, :], freq, None, ALU.mult))
                chain(nc.vector.tensor_scalar(turns[:, :], arg[:, :], phase, 1.0 / TWO_PI, ALU.add, ALU.mult))
                chain(nc.vector.tensor_scalar(turns[:, :], turns[:, :], ROUND, None, ALU.add))
                chain(nc.vector.tensor_scalar(turns[:, :], turns[:, :], -ROUND, None, ALU.add))
                p1 = 6.28125
                p2 = float(np.round((TWO_PI - p1) * 2 ** 21) / 2 ** 21)
                for part in (p1, p2, TWO_PI - p1 - p2):
                    chain(nc.vector.scalar_tensor_tensor(out=arg[:, :], in0=turns[:, :], scalar=-part, in1=arg[:, :],
                                                         op0=ALU.mult, op1=ALU.add))
                chain(nc.vector.tensor_scalar(arg[:, :], arg[:, :], phase, None, ALU.add))
                pi = float(np.nextafter(np.float32(np.pi), np.float32(0)))
                nc.vector.tensor_scalar(arg[:, :], arg[:, :], pi, -pi, ALU.min, ALU.max).then_inc(s["arg"], 1)
                dve.wait_ge(s["sin"], 1)
                nc.vector.tensor_tensor(emb_x[:, :].rearrange("j (t i) -> j t i", i=COLS),
                                        emb[:, :].unsqueeze(2).broadcast_to([2 * MODES, ROWS, COLS]),
                                        K("head", 2 * MODES).unsqueeze(1).broadcast_to([2 * MODES, ROWS, COLS]),
                                        ALU.mult).then_inc(s["emb"], 1)
                dve.wait_ge(s["theta"], 1)
                chain(nc.vector.tensor_tensor(
                    theta[:, :].rearrange("p (h r m) -> p h m r", h=HALVES, r=2),
                    small_ps[:, 0:HALVES * 2 * MODES].rearrange("p (h m r) -> p h m r", h=HALVES, r=2),
                    bias_b[:, :].rearrange("p (m r) -> p m r", r=2).unsqueeze(1).broadcast_to([P, HALVES, MODES, 2]),
                    ALU.add))
                th = theta[:, :].rearrange("p (h r m) -> p h r m", h=HALVES, r=2)
                ths = theta_sq[:, :].rearrange("p (h m) -> p h m", h=HALVES)
                t0 = tmp[0][:, 0:HALVES * MODES].rearrange("p (h m) -> p h m", h=HALVES)
                t1 = tmp[1][:, 0:HALVES * MODES].rearrange("p (h m) -> p h m", h=HALVES)
                chain(nc.vector.tensor_tensor(t0, th[:, :, 0, :], th[:, :, 0, :], ALU.mult))
                chain(nc.vector.tensor_tensor(t1, th[:, :, 1, :], th[:, :, 1, :], ALU.mult))
                chain(nc.vector.tensor_tensor(ths, t0, t1, ALU.add))
                nc.vector.tensor_scalar(ths, ths, 2.0 ** -116, None, ALU.max).then_inc(s["magnitude2"], 1)
                w3 = w_rep[:, :].rearrange("p (om r) -> p om r", r=2)
                chain(nc.vector.tensor_tensor(tmp[0][:, :], w3[:, :, 0], w3[:, :, 0], ALU.mult))
                chain(nc.vector.tensor_tensor(tmp[1][:, :], w3[:, :, 1], w3[:, :, 1], ALU.mult))
                chain(nc.vector.tensor_tensor(w_sq[:, :], tmp[0][:, :], tmp[1][:, :], ALU.add))
                nc.vector.tensor_scalar(w_sq[:, :], w_sq[:, :], 2.0 ** -116, None, ALU.max).then_inc(s["magnitude2"], 1)

                dve.wait_ge(loads["x"], CHUNKS * 16)
                layer_norm(dve, chain, s, 1e-6)

                dve.wait_ge(s["dft"], IMAGES + RING)
                sp5 = spec_ps[:, :].rearrange("p (b h r m) -> p h r b m", h=HALVES, r=2, m=MODES)
                so5 = spec[:, :].rearrange("p (m v b h) -> p h v b m", v=3, b=IMAGES, h=HALVES)
                v0 = tmp[0][:, :].rearrange("p (b m) -> p b m", m=MODES)
                v1 = tmp[1][:, :].rearrange("p (b m) -> p b m", m=MODES)
                for h in range(HALVES):
                    def wt(r):
                        return th[:, h, r, :].unsqueeze(1).broadcast_to([P, IMAGES, MODES])
                    nc.vector.tensor_tensor(v0, sp5[:, h, 0], wt(0), ALU.mult)
                    chain(nc.vector.tensor_tensor(v1, sp5[:, h, 1], wt(1), ALU.mult))
                    chain(nc.vector.tensor_tensor(so5[:, h, 1], v0, v1, ALU.subtract))
                    nc.vector.tensor_tensor(v0, sp5[:, h, 0], wt(1), ALU.mult)
                    chain(nc.vector.tensor_tensor(v1, sp5[:, h, 1], wt(0), ALU.mult))
                    chain(nc.vector.tensor_tensor(so5[:, h, 2], v0, v1, ALU.add))
                    nc.vector.tensor_scalar(so5[:, h, 0], so5[:, h, 2], -1.0, None, ALU.mult).then_inc(s["spectrum"], 1)
                dve.wait_ge(s["norm"], 1)
                nrm = small_ps[:, 128:128 + HALVES * MODES].rearrange("p (m h) -> p h m", h=HALVES)
                rn = rnorm[:, :].rearrange("p (h m) -> p h m", h=HALVES)
                chain(nc.vector.tensor_scalar(rn, nrm, 1e-12, -1.0, ALU.add, ALU.add))
                chain(nc.vector.tensor_scalar(rn, rn, 0.0, 1.0, ALU.max, ALU.add))
                chain(nc.vector.reciprocal(rn, rn))
                dve.wait_ge(s["mixed"], 1)
                mp = mix_ps[:, :].rearrange("p (m r b h) -> p h r b m", r=2, b=IMAGES, h=HALVES)
                sc = scaled[:, :].rearrange("p (b h r m) -> p h r b m", h=HALVES, r=2, m=MODES)
                for h in range(HALVES):
                    for r in range(2):
                        nc.vector.tensor_tensor(sc[:, h, r], mp[:, h, r],
                                                rn[:, h, :].unsqueeze(1).broadcast_to([P, IMAGES, MODES]),
                                                ALU.mult).then_inc(s["scaled"], 1)
                for n in range(IMAGES):
                    dve.wait_ge(s["row"], n + 1)
                    bank, j = inverse_bank(n)
                    xi = x_res[:, 8 * (n // 4) * C:8 * (n // 4 + 1) * C].rearrange("p (h r c) -> p r h c", h=2, c=C)[:, j % 4]
                    nc.vector.tensor_tensor(xi, xi, bank.rearrange("p (h c) -> p h c", h=2), ALU.add).then_inc(s["added"], 1)

            @block.tensor
            def _(pe):
                pe.sem_inc(s["transposed"], RING)
                pe.sem_inc(s["dft"], RING)
                pe.wait_ge(loads["konst"], 2 * 16)
                pe.wait_ge(loads["spectral"], (3 + ROWS_T) * 16)
                pe.wait_ge(s["emb"], 1)
                for h in range(HALVES):
                    last = nc.tensor.matmul(small_ps[:, h * 32:(h + 1) * 32], emb_x[:, h * P:(h + 1) * P], ke[:, :],
                                            start=True, stop=True)
                last.then_inc(s["theta"], 1)
                dft = K("dft").rearrange("p (k f) -> p k f", k=KC)
                with pe.Fori(0, IMAGES // RING) as q:
                    for b in range(RING):
                        transpose_image(pe, s, q * RING + b, b, bankT[b])
                    for b in range(RING):
                        n = q * RING + b
                        pe.wait_ge(s["copied"], n + 1 + RING)
                        for h in range(HALVES):
                            for kc in range(KC):
                                last = nc.tensor.matmul(spec_ps[:, bass.ds((n * HALVES + h) * 32, 32)],
                                                        xT[b][:, (kc * HALVES + h) * P:(kc * HALVES + h + 1) * P],
                                                        dft[:, kc, :], start=(kc == 0), stop=(kc == KC - 1))
                        last.then_inc(s["dft"], 1)
                pe.wait_ge(s["block_diag"], 3)
                ta = theta_abs[:, :].rearrange("p (h m) -> p m h", h=HALVES)
                pe.wait_ge(s["magnitude"], 2)
                for m in range(MODES):
                    last = nc.tensor.matmul(small_ps[:, 128 + m * HALVES:128 + (m + 1) * HALVES], bd[2][:, m * P:(m + 1) * P],
                                            ta[:, m, :], start=True, stop=True)
                last.then_inc(s["norm"], 1)
                pe.wait_ge(s["spectrum"], HALVES)
                for m in range(MODES):
                    dst = mix_ps[:, m * 64:(m + 1) * 64]
                    nc.tensor.matmul(dst, bd[0][:, m * P:(m + 1) * P], spec[:, m * 96 + 32:m * 96 + 96], start=True, stop=False)
                    last = nc.tensor.matmul(dst, bd[1][:, m * P:(m + 1) * P], spec[:, m * 96:m * 96 + 64], start=False, stop=True)
                last.then_inc(s["mixed"], 1)
                pe.wait_ge(s["scaled"], 2 * HALVES)
                for g in range(8):
                    last = nc.tensor.transpose(bankT[g // 4][:, g % 4 * P:(g % 4 + 1) * P], scaled[:, g * P:(g + 1) * P],
                                               K("ident"))
                    if g % 4 == 3:
                        last.then_inc(s["turned"], 1)
                for n in range(IMAGES):
                    pe.wait_ge(s["turned_sb"], n // 8 + 1)
                    if n >= 4:
                        pe.wait_ge(s["added"], n - 3)
                    bank, j0 = inverse_bank(n)
                    for h in range(2):
                        j = j0 + 4 * h
                        r = j % 4 * 32
                        last = nc.tensor.matmul(bank[:, h * C:(h + 1) * C], turned[r:r + 32, j // 4 * P:(j // 4 + 1) * P],
                                                K("idft")[r:r + 32, :], start=True, stop=True)
                    last.then_inc(s["row"], 1)

        if upto >= 2:
            down0 = [sb(f"down0_{n}", [P, E * (I0 // P) * C], HALF, on=moe0) for n in range(2)]
            with ExitStack() as staging:
                router("moe0", router0, "router0", split_weights("w0", staging, [(A["L0_ffn_down_w"], *down0)], 2048))
            mlp("experts0", SLOT_TILES, I0, [up0], down0, [gate0], (("w0", 2 * 16),))
        moe0.close()
        clear_semaphores()
        if upto >= 3:
            entry_sb = sb("entry_sb", [P, 2])
            qk_w = sb("qk_w", [F, 64])
            qk_sb = sb("qk_sb", [64, 2])
            val_w = sb("val_w", [F, F])
            val_sb = sb("val_sb", [F, 2])
            gates_w = sb("gates_w", [F, 2 * HID])
            gates_wh = sb("gates_wh", [HID, 8 * HID])
            gates_we = sb("gates_we", [HID, 2 * F])
            end_w = sb("end_w", [F, F])
            il_w = sb("il_w", [P, KC * F])
            out_rows = sb("out_rows", [1, 4 * F])
            scales_b = sb("scales_b", [P, 2 * F])
            feat = sb("feat", [F, TOKENS])
            pooled = sb("pooled", [P, KC * IMAGES])
            router1 = sb("router1_sb", [P, KC * E])
            place_tables("konst_attn")
            ATTN_LOADS = 13

            def load_attention(sp):
                for dst, name in ((entry_sb, "entry_sb"), (qk_w, "qk_w"), (qk_sb, "qk_sb"), (val_w, "val_w"), (val_sb, "val_sb"),
                                  (gates_w, "gates_w"), (gates_wh, "gates_wh"), (gates_we, "gates_we"), (end_w, "end_w"), (il_w, "il_w"),
                                  (out_rows, "out_rows")):
                    sp.dma_start(dst[:, :], A[name]).then_inc(loads["attn"], 16)
                sp.dma_start(konst["konst_attn"][:, :], A["konst_attn"]).then_inc(loads["attn"], 16)
                sp.dma_start(scales_b[:, :], A["out_rows"][:, 0:2 * F].broadcast_to([P, 2 * F])).then_inc(loads["attn"], 16)
                sp.dma_start(router1[:, :], A["L1_ffn_w_router"]).then_inc(loads["router1"], 16)

            with ExitStack() as on:
                entry_convolution(on)
            up1, down1, ws1, ws2 = ([sb(f"{name}_{n}", [P, width], HALF) for n in range(2)]
                                    for name, width in (("up1", E * KC * I1), ("down1", E * I1 // P * C), ("ws1", KC * IS), ("ws2", IS // P * C)))
            with ExitStack() as on:
                split1 = split_weights("w1", on, [(A["L1_ffn_w1_stack"], *up1), (A["L1_ffn_w2_stack"], *down1),
                                              (A["L1_ffn_ws1"], *ws1), (A["L1_ffn_ws2"], *ws2)], 512)
                att_t = sb("att_t", [F, TOKENS], on=on)
                att_along = sb("att_along", [P, TILES * P], on=on)
                axial_scores(split1)
                axial_along()
                attention_output()
        if upto >= 4:
            router("moe1", router1, "router1")
            mlp("experts1", SLOT_TILES, I1, up1, down1)
            mlp("shared", TILES, IS, ws1, ws2, experts=False, sink=out)
        else:
            with nc.Block() as block:
                @block.sync
                def _(sp):
                    stored = sem("out_stored")
                    sp.dma_start(out.rearrange("(j p) c -> p j c", p=P), x_res[:, :].rearrange("p (j c) -> p j c", c=C)).then_inc(stored, 16)
                    sp.wait_ge(stored, 16)


def padded_pair(v, h, axis):
    pad = [(0, 0), (0, 0)]
    pad[axis] = (0, 32 - G)
    return np.ascontiguousarray(np.concatenate([np.pad(v, pad), np.pad(h, pad)], axis))


def by_contracted_row(w):
    e, o, c = w.shape
    return np.ascontiguousarray(w.reshape(e, o, c // P, P).transpose(3, 0, 2, 1).reshape(P, -1))


def layouts(inputs):
    a = {k: np.asarray(v) for k, v in inputs.items()}
    t = np.ascontiguousarray
    return {
        **constants()[0],
        "x": t(a["x"].reshape(TOKENS, C)),
        "L0_conv_t": t(a["L0_conv_t"]),
        "L0_conv_weights1": t(a["L0_conv_weights1"].reshape(COLS, -1)),
        "L0_conv_ke_weights": t(a["L0_conv_ke_weights"].reshape(2 * MODES, 2 * MODES)),
        "L0_conv_ke_bias": t(a["L0_conv_ke_bias"].reshape(1, 2 * MODES)),
        "conv_w": t(a["L1_conv_entry_w"].reshape(9, KC, P, F).transpose(2, 0, 1, 3).reshape(P, -1)),
        "entry_sb": t(np.stack([a["L1_conv_entry_s"], a["L1_conv_entry_b"]], 1)),
        "qk_w": padded_pair(a["L1_conv_vqk_w"], a["L1_conv_hqk_w"], 1),
        "qk_sb": padded_pair(np.stack([a["L1_conv_vqk_s"], a["L1_conv_vqk_b"]], 1), np.stack([a["L1_conv_hqk_s"], a["L1_conv_hqk_b"]], 1), 0),
        "val_w": a["L1_conv_val_w"],
        "val_sb": t(np.stack([a["L1_conv_val_s"], a["L1_conv_val_b"]], 1)),
        "gates_w": t(np.concatenate([a["L1_conv_vca_w0"], a["L1_conv_hca_w0"]], 1)),
        "gates_wh": t(np.concatenate([a["L1_conv_vca_wh"], a["L1_conv_hca_wh"]], 0).transpose(1, 0, 2).reshape(HID, -1)),
        "gates_we": t(np.concatenate([a["L1_conv_vca_we"], a["L1_conv_hca_we"]], 1)),
        "end_w": a["L1_conv_end_w"],
        "il_w": t(a["L1_conv_il_w"].reshape(KC, P, F).transpose(1, 0, 2).reshape(P, -1)),
        "out_rows": t(np.concatenate([a[f"L1_conv_{n}"] for n in ("end_s", "il_s", "end_b", "il_b")])[None]),
        "L1_ffn_w_router": by_contracted_row(a["L1_ffn_w_router"][None]),
        "L1_ffn_ws1": by_contracted_row(a["L1_ffn_ws1"][None]),
        "L1_ffn_ws2": by_contracted_row(a["L1_ffn_ws2"][None]),
        "L1_ffn_w1_stack": by_contracted_row(a["L1_ffn_w1_stack"]),
        "L1_ffn_w2_stack": by_contracted_row(a["L1_ffn_w2_stack"]),
        "L0_ffn_router_w": by_contracted_row(a["L0_ffn_router_w"][None]),
        "L0_ffn_gate_w": by_contracted_row(a["L0_ffn_gate_w"]),
        "L0_ffn_up_w": by_contracted_row(a["L0_ffn_up_w"]),
        "L0_ffn_down_w": by_contracted_row(a["L0_ffn_down_w"]),
    }


def kernel(**inputs):
    import concourse.bacc as bacc
    from concourse.bass_utils import run_bass_kernel_spmd

    nc = bacc.Bacc("TRN2", target_bir_lowering=False, num_devices=1)
    arrays = layouts(inputs)
    ins = {n: nc.dram_tensor("in_" + n, a.shape, mybir.dt.from_np(a.dtype), kind="ExternalInput").ap() for n, a in arrays.items()}
    out = nc.dram_tensor("out", (TOKENS, C), F32, kind="ExternalOutput").ap()
    build(nc, ins, out)
    r = run_bass_kernel_spmd(nc, [{"in_" + n: a for n, a in arrays.items()}], core_ids=[0])
    return r.results[0]["out"].reshape(IMAGES, ROWS, COLS, C)
```

```python
from contextlib import ExitStack

import numpy as np

import concourse.bass as bass
from concourse import mybir

ALU = mybir.AluOpType
ACT = mybir.ActivationFunctionType
AX_X = mybir.AxisListType.X
F32 = mybir.dt.float32
I32 = mybir.dt.int32
HALF = mybir.dt.float32r

P = 128
IMAGES, ROWS, COLS, C = 16, 16, 16, 256
TOKENS = IMAGES * ROWS * COLS
TILES = TOKENS // P
KC = C // P
HALVES = TILES // IMAGES
ROWS_T = ROWS // HALVES
MODES = 16
E = 8
I0, I1, IS = 512, 256, 512
F = 128
G = 16
HID = 32
SLOT_TILES = (2 * TOKENS // P + E - 1 + 3) // 4 * 4
ROUND_T = 4
AHEAD = 2
CHUNKS, CHUNK_T = 4, 8
RING = 2
ROUND = 1.5 * 2.0 ** 23
BIG = 2.0 ** 100
TWO_PI = 2.0 * np.pi


def constants():
    parts = {}
    c = np.arange(C)[:, None]
    m = np.arange(MODES)[None, :]
    angle = 2 * np.pi * c * m / C
    dft = np.concatenate([np.cos(angle), -np.sin(angle)], 1)
    parts["dft"] = dft.reshape(KC, P, 2 * MODES).transpose(1, 0, 2).reshape(P, -1)
    twice = np.where(m == 0, 1.0, 2.0)
    idft = np.concatenate([twice * np.cos(angle), -twice * np.sin(angle) * (m > 0)], 1).T / C
    parts["idft"] = np.tile(idft, (4, 1))
    parts["ident"] = np.eye(P)
    parts["ramp"] = np.tile(np.arange(P)[None, :], (P, 1))
    parts["column"] = np.arange(P)[:, None]
    parts["tile_base"] = np.tile(P * np.arange(TILES)[None, :], (P, 1))
    parts["first_wins"] = np.tile(E - np.arange(E)[None, :], (P, 1))
    parts["row_of"] = (np.arange(P)[:, None] // COLS == np.arange(ROWS_T)[None, :])
    parts["before"] = (np.arange(P)[:, None] < np.arange(P)[None, :])
    parts["ones"] = np.ones((P, P))
    j = np.arange(2 * MODES)
    freq = np.exp(-np.log(10000.0).astype(np.float32) * (j % MODES).astype(np.float32) / np.float32(MODES))
    parts["freq"] = np.pad(freq[:, None], ((0, P - 2 * MODES), (0, 0)))
    parts["phase"] = np.pad(np.where(j >= MODES, np.pi / 2, 0.0)[:, None], ((0, P - 2 * MODES), (0, 0)))
    head = (np.arange(COLS)[None, :] % 4 == j[:, None] // 8)
    parts["head"] = np.pad(head, ((0, P - 2 * MODES), (0, 0)))
    for name, group in (("same_col", np.arange(P) % 8), ("same_row", np.arange(P) // COLS)):
        member = (group[None, :] == np.arange(8)[:, None]).astype(np.float64)
        left = np.concatenate([np.ones((1, P)), member])
        right = np.concatenate([-BIG * np.ones((1, P)), BIG * member])
        parts[name + "_l"] = np.pad(left, ((0, P - 9), (0, 0)))
        parts[name + "_r"] = np.pad(right, ((0, P - 9), (0, 0)))
    arrays, where = {}, {}
    for name, a in parts.items():
        a = np.asarray(a, np.float32)
        kind = "konst_mix" if name in ("dft", "idft", "freq", "phase", "head", "row_of") else "konst_attn" if name[:5] == "same_" else "konst"
        at = sum(other.shape[1] for other in arrays.get(kind, []))
        where[name] = (kind, at, a.shape[1])
        arrays.setdefault(kind, []).append(a)
    return {kind: np.ascontiguousarray(np.concatenate(a, 1)) for kind, a in arrays.items()}, where


class Chain:

    def __init__(self, eng, sem):
        self.eng, self.sem, self.n = eng, sem, 0

    def __call__(self, ins):
        ins.then_inc(self.sem, 1)
        self.n = self.n + 1
        self.eng.wait_ge(self.sem, self.n)


def build(nc, A, out, upto=4):
    _, where = constants()
    ctx = ExitStack()
    with ctx:
        live = []

        def sem(name):
            live.append(nc.alloc_semaphore(name=name))
            return live[-1]

        def clear_semaphores():
            nc.clear_and_free_semaphores(live)
            live.clear()
            nc.all_engine_barrier()

        def sb(name, shape, dt=F32, on=ctx):
            return on.enter_context(nc.sbuf_tensor(name, shape, dt))

        def pb(name, width, on=ctx):
            return on.enter_context(nc.psum_tensor(name, [P, width], F32))

        konst = {}

        def place_tables(kind, on=ctx):
            konst[kind] = sb(f"{kind}_sb", [P, sum(w for k, _, w in where.values() if k == kind)], on=on)
        place_tables("konst")

        def K(name, parts=P):
            kind, at, w = where[name]
            return konst[kind][0:parts, at:at + w]

        x_res = sb("x_res", [P, TILES * C])
        h_dram = nc.dram_tensor("h_rows", (TOKENS, C), F32, kind="Internal").ap()
        y_dram = nc.dram_tensor("y_rows", (SLOT_TILES * P, C), F32, kind="Internal").ap()

        router0 = sb("router0_sb", [P, KC * E])
        stats = sb("stats", [P, CHUNK_T * 6])
        means = sb("means", [P, TILES])
        rstds = sb("rstds", [P, TILES])
        twice_mean = sb("twice_mean", [P, CHUNK_T])
        var_eps = sb("var_eps", [P, CHUNK_T])
        sqrt_v = sb("sqrt_v", [P, CHUNK_T])
        rstd = sb("rstd", [P, CHUNK_T])
        newton = sb("newton", [P, CHUNK_T])
        xn = [sb(f"xn{b}", [P, HALVES * C]) for b in range(RING)]

        w_top = sb("w_top", [P, 2 * TILES])
        pos_i = sb("pos_i", [P, 2 * TILES], I32)
        ids_i = sb("ids_i", [P, SLOT_TILES], I32)
        experts_i = sb("experts_i", [1, SLOT_TILES // ROUND_T], I32)

        moe0 = ExitStack()
        gate0 = sb("gate0", [P, E * KC * I0], on=moe0)
        up0 = sb("up0", [P, E * KC * I0], on=moe0)

        loads = {n: nc.alloc_semaphore(name=f"loaded_{n}") for n in ("konst", "x_first", "x", "spectral", "router0", "w0", "router1", "conv", "attn")}

        def x_tile(j, width=C, n=1):
            return x_res[:, bass.ds(j * C, n * C)]

        def product(out, left, right, start, stop):
            if len(left) == 1:
                return nc.tensor.matmul(out, left[0], right[0], start=start, stop=stop)
            nc.tensor.matmul(out, left[0], right[0], start=start, stop=False)
            nc.tensor.matmul(out, left[0], right[1], start=False, stop=False)
            return nc.tensor.matmul(out, left[1], right[0], start=False, stop=stop)

        def low_half(eng, low, whole, high):
            return eng.tensor_tensor(low, whole, high.bitcast(F32), ALU.subtract)

        def split_weights(tag, stage, parts):
            step = stage[0].shape[1]
            s_in = [sem(f"{tag}_stage_in{b}") for b in range(RING)]
            s_high, s_low = sem(f"{tag}_high"), sem(f"{tag}_low")
            pieces = [(src, high, low, slice(at, at + step)) for src, high, low in parts for at in range(0, high.shape[1], step)]

            def split(pool):
                def load(n):
                    src, _, _, cols = pieces[n]
                    pool.dma_start(stage[n % RING][:, :], src[:, cols]).then_inc(s_in[n % RING], 16)

                for n in range(RING):
                    load(n)
                for n, (_, high, low, cols) in enumerate(pieces):
                    pool.wait_ge(s_in[n % RING], (n // RING + 1) * 16)
                    nc.gpsimd.tensor_copy(high[:, cols], stage[n % RING][:, :]).then_inc(s_high, 1)
                    pool.wait_ge(s_high, n + 1)
                    low_half(nc.gpsimd, low[:, cols], stage[n % RING][:, :], high[:, cols]).then_inc(s_low, 1)
                    pool.wait_ge(s_low, n + 1)
                    if n + RING < len(pieces):
                        load(n + RING)
            return split

        def layer_norm(dve, chain, s, eps, add=None, between=None, after=None):
            per = 8
            images = CHUNK_T // HALVES
            st = stats[:, :].rearrange("p (t f) -> p t f", f=6)

            def variances(c):
                for t in range(CHUNK_T):
                    if add is not None and isinstance(c, int):
                        add(c, (t,), complete=t + 1)
                    if add is not None and not isinstance(c, int) and t == 0:
                        add(c, (), complete=CHUNK_T)
                    last = nc.vector.bn_stats(stats[:, 6 * t:6 * t + 6], x_tile(c * CHUNK_T + t))
                chain(last)
                nc.vector.tensor_tensor(twice_mean[:, :], st[:, :, 1], st[:, :, 4], ALU.add)
                nc.vector.tensor_tensor(newton[:, :], st[:, :, 1], st[:, :, 4], ALU.subtract)
                chain(nc.vector.tensor_tensor(var_eps[:, :], st[:, :, 2], st[:, :, 5], ALU.add))
                nc.vector.tensor_scalar(means[:, bass.ds(c * CHUNK_T, CHUNK_T)], twice_mean[:, :], 0.5, None, ALU.mult)
                nc.vector.tensor_scalar(var_eps[:, :], var_eps[:, :], 1.0 / C, eps, ALU.mult, ALU.add)
                chain(nc.vector.scalar_tensor_tensor(out=newton[:, :], in0=newton[:, :], scalar=0.25, in1=newton[:, :],
                                                     op0=ALU.mult, op1=ALU.mult))
                nc.vector.tensor_tensor(var_eps[:, :], var_eps[:, :], newton[:, :], ALU.add).then_inc(s["var"], 1)

            def deviations(c):
                dve.wait_ge(s["sqrt"], c + 1)
                chain(nc.vector.reciprocal(rstd[:, :], sqrt_v[:, :]))
                chain(nc.vector.tensor_tensor(newton[:, :], var_eps[:, :], rstd[:, :], ALU.mult))
                chain(nc.vector.tensor_tensor(newton[:, :], newton[:, :], rstd[:, :], ALU.mult))
                chain(nc.vector.tensor_scalar(newton[:, :], newton[:, :], -0.5, 1.5, ALU.mult, ALU.add))
                chain(nc.vector.tensor_tensor(rstds[:, bass.ds(c * CHUNK_T, CHUNK_T)], rstd[:, :], newton[:, :], ALU.mult))

            def normalise(c, i):
                n = c * images + i
                dve.wait_ge(s["transposed"], n + 1)
                if "stored" in s:
                    dve.wait_ge(s["stored"][i % RING], (c * (images // RING) + i // RING + 1) * 16)
                for h in range(HALVES):
                    t = n * HALVES + h
                    last = nc.vector.tensor_scalar(xn[i % RING][:, h * C:(h + 1) * C], x_tile(t),
                                                   means[:, bass.ds(t, 1)], rstds[:, bass.ds(t, 1)], ALU.subtract, ALU.mult)
                last.then_inc(s["xn"], 1)
                if after is not None and i:
                    after(n - 1, (i - 1) % RING)
                if after is not None and i == images - 1:
                    after(n, i % RING)

            variances(0)
            deviations(0)
            if between is not None:
                between()
            at = chain.n
            with dve.Fori(0, CHUNKS - 1) as c:
                chain.n = c * per + at
                if add is None:
                    variances(c + 1)
                for i in range(images):
                    if add is None and i == images // 2:
                        deviations(c + 1)
                    normalise(c, i)
                    if add is not None:
                        add(c + 1, range(i * HALVES, (i + 1) * HALVES))
                if add is not None:
                    variances(c + 1)
                    deviations(c + 1)
            chain.n = at + (CHUNKS - 1) * per
            for i in range(images):
                normalise(CHUNKS - 1, i)

        def layer_norm_sqrt(act, s, c):
            act.wait_ge(s["var"], c + 1)
            nc.scalar.activation(sqrt_v[:, :], var_eps[:, :], ACT.Sqrt).then_inc(s["sqrt"], 1)

        def copy_transposes(act, s, xT, bankT, used):
            def copies(c):
                for i in range(CHUNK_T // HALVES):
                    n = c * (CHUNK_T // HALVES) + i
                    act.wait_ge(s["transposed"], n + 1 + RING)
                    act.wait_ge(s[used], n + 1)
                    nc.scalar.activation(xT[i % RING][:, :], bankT[i % RING][:, :], ACT.Copy).then_inc(s["copied"], 1)
            with act.Fori(0, CHUNKS - 1) as c:
                layer_norm_sqrt(act, s, c + 1)
                copies(c)
            copies(CHUNKS - 1)

        def transpose_image(pe, s, n, b, bank):
            pe.wait_ge(s["xn"], n + 1)
            pe.wait_ge(s["copied"], n + 1)
            for kc in range(KC):
                for h in range(HALVES):
                    last = nc.tensor.transpose(bank[:, (kc * HALVES + h) * P:(kc * HALVES + h + 1) * P],
                                               xn[b][:, h * C + kc * P:h * C + (kc + 1) * P], K("ident"))
            last.then_inc(s["transposed"], 1)

        def router(tag, w_router, load, split=None):
            on = ExitStack()
            with on:
                s = {n: sem(f"{tag}_{n}") for n in ("var", "sqrt", "xn", "transposed", "copied", "logits", "chain", "shifted",
                                                    "exp", "totals", "bases", "begun", "filled")}
                s_one_hot, s_spread, s_equal = ([sem(f"{tag}_{n}{k}") for k in range(2)] for n in ("one_hot", "spread", "equal"))
                s["stored"] = [sem(f"{tag}_stored{b}") for b in range(RING)]
                xT = [sb(f"{tag}_xT{b}", [P, KC * HALVES * P], on=on) for b in range(RING)]
                bankT = [pb(f"{tag}_bankT{b}", 512, on=on) for b in range(RING)]
                logits_ps = pb(f"{tag}_logits", TILES * E, on=on)
                sums_ps = pb(f"{tag}_sums", 2 * E, on=on)
                ids_ps = pb(f"{tag}_ids", SLOT_TILES, on=on)
                prob, work, *one_hot = [x[:, h * TILES * E:(h + 1) * TILES * E] for x in xT for h in range(2)]
                chosen = xn[0][:, 0:TILES * E]
                count = xn[0][:, TILES * E:2 * TILES * E]
                zeros = sb(f"{tag}_zeros", [P, SLOT_TILES], on=on)
                top = [sb(f"{tag}_top{k}", [P, TILES], on=on) for k in range(2)]
                row = sb(f"{tag}_row", [P, TILES], on=on)
                tiles_of = sb(f"{tag}_tiles_of", [P, E], on=on)
                ends = sb(f"{tag}_ends", [P, E], on=on)
                offset = sb(f"{tag}_offset", [P, E], on=on)
                pos = sb(f"{tag}_pos", [P, 2 * TILES], on=on)
                slot_tile = sb(f"{tag}_slot_tile", [P, 2 * TILES], on=on)
                slot_row = sb(f"{tag}_slot_row", [P, 2 * TILES], on=on)
                token = sb(f"{tag}_token", [P, TILES], on=on)
                past = xn[1][0:1, 0:SLOT_TILES // 2 * E]
                etile = sb(f"{tag}_etile", [1, SLOT_TILES + ROUND_T + AHEAD], on=on)
                packed = sb(f"{tag}_packed", [1, SLOT_TILES // ROUND_T], on=on)
                BATCH = 4
                at_row = [[sb(f"{tag}_at_row{k}{b}", [P, BATCH * P], HALF, on=on) for b in range(RING)] for k in range(2)]
                at_tile = [[sb(f"{tag}_at_tile{k}{b}", [P, BATCH * SLOT_TILES], HALF, on=on) for b in range(RING)] for k in range(2)]
                block = on.enter_context(nc.Block())

                @block.sync
                def _(sp):
                    rows = h_dram.rearrange("(j p) c -> p j c", p=P)
                    for b in range(RING):
                        sp.sem_inc(s["stored"][b], 16)
                    with sp.Fori(0, IMAGES // RING) as q:
                        for b in range(RING):
                            n = q * RING + b
                            sp.wait_ge(s["xn"], n + 1)
                            sp.dma_start(rows[:, bass.ds(n * HALVES, HALVES), :],
                                         xn[b][:, :].rearrange("p (h c) -> p h c", c=C)).then_inc(s["stored"][b], 16)
                    for b in range(RING):
                        sp.wait_ge(s["stored"][b], IMAGES // RING * 16 + 16)

                def tokens(t, at, width):
                    return t[:, bass.ds(at, BATCH)].unsqueeze(2).broadcast_to([P, BATCH, width])

                def table(t):
                    return t[:, :].rearrange("p (t i) -> p t i", t=BATCH)

                @block.gpsimd
                def _(pool):
                    if split is not None:
                        split(pool)
                    with pool.Fori(0, TILES // BATCH // RING) as q:
                        for b in range(RING):
                            n = q * RING + b
                            for k in range(2):
                                pool.wait_ge(s_equal[k], n + 1)
                                pool.sem_inc(s["begun"], 1)
                                nc.gpsimd.tensor_tensor(table(at_tile[k][b]), table(at_tile[k][b]).bitcast(F32), tokens(token, n * BATCH, SLOT_TILES),
                                                        ALU.mult).then_inc(s_one_hot[k], 1)

                @block.scalar
                def _(act):
                    act.sem_inc(s["copied"], RING)
                    layer_norm_sqrt(act, s, 0)
                    copy_transposes(act, s, xT, bankT, "logits")
                    act.wait_ge(s["shifted"], 1)
                    nc.scalar.activation(work[:, :], prob[:, :], ACT.Exp).then_inc(s["exp"], 1)

                @block.tensor
                def _(pe):
                    pe.sem_inc(s["transposed"], RING)
                    pe.sem_inc(s["logits"], RING)
                    for k in range(2):
                        pe.sem_inc(s_spread[k], RING)
                    pe.wait_ge(loads[load], 16)
                    with pe.Fori(0, IMAGES // RING) as q:
                        for b in range(RING):
                            transpose_image(pe, s, q * RING + b, b, bankT[b])
                        for b in range(RING):
                            n = q * RING + b
                            pe.wait_ge(s["copied"], n + 1 + RING)
                            for h in range(HALVES):
                                for kc in range(KC):
                                    last = nc.tensor.matmul(logits_ps[:, bass.ds((n * HALVES + h) * E, E)],
                                                            xT[b][:, (kc * HALVES + h) * P:(kc * HALVES + h + 1) * P],
                                                            w_router[:, kc * E:(kc + 1) * E], start=(kc == 0), stop=(kc == KC - 1))
                            last.then_inc(s["logits"], 1)
                    pe.wait_ge(s["totals"], 1)
                    totals = count[:, :].rearrange("p (e j) -> p e j", e=E)[:, :, TILES - 1]
                    nc.tensor.matmul(sums_ps[:, 0:E], K("before"), totals, start=True, stop=True)
                    nc.tensor.matmul(sums_ps[:, E:2 * E], K("ones"), totals, start=True, stop=True).then_inc(s["bases"], 1)
                    nc.tensor.matmul(ids_ps[:, :], K("ident"), zeros[:, :], start=True, stop=False)
                    with pe.Fori(0, TILES // BATCH // RING) as q:
                        for b in range(RING):
                            for k in range(2):
                                pe.wait_ge(s_one_hot[k], q * RING + b + 1)
                                for i in range(BATCH):
                                    last = nc.tensor.matmul(ids_ps[:, :], at_row[k][b][:, i * P:(i + 1) * P],
                                                            at_tile[k][b][:, i * SLOT_TILES:(i + 1) * SLOT_TILES], start=False, stop=False)
                                last.then_inc(s_spread[k], 1)
                    nc.tensor.matmul(ids_ps[:, :], K("ident"), zeros[:, :], start=False, stop=True).then_inc(s["filled"], 1)

                @block.vector
                def _(dve):
                    chain = Chain(dve, s["chain"])
                    nc.vector.memset(etile[:, :], 0.0)
                    chain(nc.vector.memset(zeros[:, :], 0.0))
                    layer_norm(dve, chain, s, 1e-5)

                    def by_token(t):
                        return t[:, :].rearrange("p (j e) -> p j e", e=E)

                    def over_e(t):
                        return t.unsqueeze(2).broadcast_to([P, TILES, E])

                    def over_j(t):
                        return t.unsqueeze(1).broadcast_to([P, TILES, E])
                    dve.wait_ge(s["logits"], IMAGES + RING)
                    chain(nc.vector.reduce_max(row[:, :], by_token(logits_ps), AX_X))
                    nc.vector.tensor_tensor(by_token(prob), by_token(logits_ps), over_e(row[:, :]), ALU.subtract).then_inc(s["shifted"], 1)
                    dve.wait_ge(s["exp"], 1)
                    chain(nc.vector.reduce_sum(row[:, :], by_token(work), AX_X))
                    chain(nc.vector.reciprocal(row[:, :], row[:, :]))
                    chain(nc.vector.tensor_tensor(by_token(prob), by_token(work), over_e(row[:, :]), ALU.mult))
                    for k in range(2):
                        chain(nc.vector.reduce_max(top[k][:, :], by_token(prob), AX_X))
                        chain(nc.vector.tensor_tensor(by_token(work), by_token(prob), over_e(top[k][:, :]), ALU.is_equal))
                        chain(nc.vector.tensor_tensor(by_token(work), by_token(work), over_j(K("first_wins")), ALU.mult))
                        chain(nc.vector.reduce_max(row[:, :], by_token(work), AX_X))
                        chain(nc.vector.tensor_tensor(by_token(one_hot[k]), by_token(work), over_e(row[:, :]), ALU.is_equal))
                        if k == 0:
                            chain(nc.vector.scalar_tensor_tensor(out=prob[:, :], in0=one_hot[0][:, :], scalar=-2.0, in1=prob[:, :],
                                                                 op0=ALU.mult, op1=ALU.add))
                    chain(nc.vector.tensor_tensor(row[:, :], top[0][:, :], top[1][:, :], ALU.add))
                    chain(nc.vector.reciprocal(row[:, :], row[:, :]))
                    for k in range(2):
                        chain(nc.vector.tensor_tensor(w_top[:, k * TILES:(k + 1) * TILES], top[k][:, :], row[:, :], ALU.mult))
                    for b in range(RING):
                        dve.wait_ge(s["stored"][b], IMAGES // RING * 16 + 16)
                    chain(nc.vector.tensor_tensor(chosen[:, :], one_hot[0][:, :], one_hot[1][:, :], ALU.add))
                    for e in range(E):
                        last = nc.vector.tensor_tensor_scan(count[:, e * TILES:(e + 1) * TILES], zeros[:, 0:TILES],
                                                            by_token(chosen)[:, :, e], 0.0, ALU.add, ALU.add)
                    last.then_inc(s["totals"], 1)
                    dve.wait_ge(s["bases"], 1)
                    chain(nc.vector.tensor_scalar(tiles_of[:, :], sums_ps[:, E:2 * E], 1.0 / P, (P - 1) / P - 0.5 + 0.5 / P, ALU.mult, ALU.add))
                    chain(nc.vector.tensor_scalar(tiles_of[:, :], tiles_of[:, :], ROUND, None, ALU.add))
                    chain(nc.vector.tensor_scalar(tiles_of[:, :], tiles_of[:, :], -ROUND, None, ALU.add))
                    chain(nc.vector.tensor_tensor_scan(ends[:, :], zeros[:, 0:E], tiles_of[:, :], 0.0, ALU.add, ALU.add))
                    chain(nc.vector.tensor_tensor(offset[:, :], ends[:, :], tiles_of[:, :], ALU.subtract))
                    chain(nc.vector.tensor_scalar(offset[:, :], offset[:, :], float(P), -1.0, ALU.mult, ALU.add))
                    chain(nc.vector.tensor_tensor(offset[:, :], offset[:, :], sums_ps[:, 0:E], ALU.add))
                    chain(nc.vector.tensor_tensor(by_token(chosen), count[:, :].rearrange("p (e j) -> p j e", e=E),
                                                  over_j(offset[:, :]), ALU.add))
                    for k in range(2):
                        chain(nc.vector.tensor_tensor(work[:, :], one_hot[k][:, :], chosen[:, :], ALU.mult))
                        chain(nc.vector.reduce_sum(pos[:, k * TILES:(k + 1) * TILES], by_token(work), AX_X))
                    nc.vector.tensor_copy(pos_i[:, :], pos[:, :])
                    chain(nc.vector.tensor_scalar(slot_tile[:, :], pos[:, :], 1.0 / P, -0.5 + 0.5 / P, ALU.mult, ALU.add))
                    chain(nc.vector.tensor_scalar(slot_tile[:, :], slot_tile[:, :], ROUND, None, ALU.add))
                    chain(nc.vector.tensor_scalar(slot_tile[:, :], slot_tile[:, :], -ROUND, None, ALU.add))
                    chain(nc.vector.scalar_tensor_tensor(out=slot_row[:, :], in0=slot_tile[:, :], scalar=-float(P), in1=pos[:, :],
                                                         op0=ALU.mult, op1=ALU.add))
                    half = SLOT_TILES // 2
                    pe3 = past.rearrange("p (s e) -> p s e", e=E)
                    for h in range(2):
                        tiles = slice(h * half, (h + 1) * half)
                        chain(nc.vector.tensor_tensor(pe3, K("ramp", 1)[:, tiles].unsqueeze(2).broadcast_to([1, half, E]),
                                                      ends[0:1, :].unsqueeze(1).broadcast_to([1, half, E]), ALU.is_ge))
                        chain(nc.vector.reduce_sum(etile[:, tiles], pe3, AX_X))
                    chain(nc.vector.tensor_scalar(etile[:, 0:SLOT_TILES], etile[:, 0:SLOT_TILES], float(E - 1), None, ALU.min))
                    for i in range(1, ROUND_T + AHEAD):
                        ith = etile[:, i:i + SLOT_TILES].rearrange("p (q f) -> p q f", f=ROUND_T)[:, :, 0]
                        before = etile[:, 0:SLOT_TILES].rearrange("p (q f) -> p q f", f=ROUND_T)[:, :, 0] if i == 1 else packed[:, :]
                        to = experts_i if i == ROUND_T + AHEAD - 1 else packed
                        chain(nc.vector.scalar_tensor_tensor(out=to[:, :], in0=ith, scalar=float(E ** i), in1=before, op0=ALU.mult, op1=ALU.add))
                    chain(nc.vector.tensor_scalar(token[:, :], K("tile_base"), K("column"), None, ALU.add))
                    with dve.Fori(0, TILES // BATCH // RING) as q:
                        for b in range(RING):
                            n = q * RING + b
                            for k in range(2):
                                at = n * BATCH + k * TILES
                                dve.wait_ge(s_spread[k], n + 1)
                                nc.vector.tensor_tensor(table(at_row[k][b]), K("ramp").unsqueeze(1).broadcast_to([P, BATCH, P]),
                                                        tokens(slot_row, at, P), ALU.is_equal)
                                nc.vector.tensor_tensor(table(at_tile[k][b]), K("ramp")[:, 0:SLOT_TILES].unsqueeze(1).broadcast_to([P, BATCH, SLOT_TILES]),
                                                        tokens(slot_tile, at, SLOT_TILES), ALU.is_equal).then_inc(s_equal[k], 1)
                    dve.wait_ge(s["filled"], 1)
                    chain(nc.vector.tensor_copy(ids_i[:, :], ids_ps[:, :]))

        def mlp(tag, n_tiles, hidden, up, down, gate=None, load=(), experts=True, sink=None):
            KI = hidden // P
            DEPTH = ROUND_T
            on = ExitStack()
            with on:
                s = {n: sem(f"{tag}_{n}") for n in ("h_turned", "h_high", "h_copied", "gated", "up", "act", "a", "a_turned", "a_high",
                                                    "a_copied", "down", "y_copied", "sum")}
                s_rows = [sem(f"{tag}_rows{g}") for g in range(DEPTH)]
                s_stored = [sem(f"{tag}_stored{b}") for b in range(RING)]
                s_routed = [sem(f"{tag}_routed{g}") for g in range(2 * DEPTH)]

                def operand(name, width, w):
                    dt = F32 if len(w) == 1 else HALF
                    return [[sb(f"{tag}_{name}{b}_{part}", [P, width], dt, on=on) for part in range(len(w))] for b in range(RING)]
                rows = [sb(f"{tag}_rows_sb{g}", [P, C], on=on) for g in range(DEPTH)]
                DEPTH_R = 2 * DEPTH
                routed = [sb(f"{tag}_routed_sb{g}", [P, C], on=on) for g in range(DEPTH_R)] if not experts else None
                hT = operand("hT", C, up)
                a_sb = [sb(f"{tag}_a_sb{b}", [P, hidden], on=on) for b in range(RING)]
                aT = operand("aT", hidden, down)
                y_sb = [sb(f"{tag}_y_sb{b}", [P, C], on=on) for b in range(RING)] if experts else None
                bankH = pb(f"{tag}_bankH", 512, on=on)
                bankA = pb(f"{tag}_bankA", 512, on=on)
                bankG = [pb(f"{tag}_bankG{b}", 512, on=on) for b in range(RING)]
                bankU = [pb(f"{tag}_bankU{b}", 512, on=on) for b in range(RING)] if gate is not None else bankG
                bankY = [pb(f"{tag}_bankY{b}", 512, on=on) for b in range(RING)]
                block = on.enter_context(nc.Block())

                rounds = (n_tiles - 2 * AHEAD) // DEPTH

                def steps(eng, step, prepare=lambda q: None):
                    with eng.Fori(0, rounds) as q:
                        prepare(q)
                        for i in range(AHEAD, DEPTH + AHEAD):
                            step(q * DEPTH + i, i)
                    prepare(rounds)
                    for t in range(rounds * DEPTH + AHEAD, n_tiles):
                        step(t, t - rounds * DEPTH, ahead=t + AHEAD < n_tiles)

                @block.gpsimd
                def _(pool):
                    if experts:
                        for t in range(n_tiles):
                            if t >= DEPTH:
                                pool.wait_ge(s["h_turned"], t - DEPTH + 1)
                            nc.gpsimd.indirect_dma_start(rows[t % DEPTH][:, :], None, h_dram,
                                                         bass.IndirectOffsetOnAxis(ap=ids_i[:, t:t + 1], axis=0)).then_inc(s_rows[t % DEPTH], 16)
                    else:
                        for j in range(n_tiles):
                            for k in range(2):
                                u = j * 2 + k
                                if u >= DEPTH_R:
                                    pool.wait_ge(s["sum"], u - DEPTH_R + 1)
                                nc.gpsimd.indirect_dma_start(
                                    routed[u % DEPTH_R][:, :], None, y_dram,
                                    bass.IndirectOffsetOnAxis(ap=pos_i[:, j + k * TILES:j + k * TILES + 1], axis=0)).then_inc(s_routed[u % DEPTH_R], 16)

                @block.sync
                def _(sp):
                    if not experts:
                        def store(t):
                            sp.wait_ge(s["sum"], t * 2 + 2)
                            sp.dma_start(sink[bass.ds(t * P, P), :], x_tile(t)).then_inc(s_stored[0], 16)
                        def load(t, g):
                            sp.dma_start(rows[g][:, :], h_dram[bass.ds(t * P, P), :]).then_inc(s_rows[g], 16)

                        for t in range(2 * DEPTH):
                            if t >= DEPTH:
                                sp.wait_ge(s["h_turned"], t - DEPTH + 1)
                            load(t, t % DEPTH)
                        with sp.Fori(2, n_tiles // DEPTH) as q:
                            for g in range(DEPTH):
                                sp.wait_ge(s["h_turned"], (q - 1) * DEPTH + g + 1)
                                load(q * DEPTH + g, g)
                                store((q - 2) * DEPTH + g)
                        for t in range(n_tiles - 2 * DEPTH, n_tiles):
                            store(t)
                        sp.wait_ge(s_stored[0], n_tiles * 16)
                    else:
                        for b in range(RING):
                            sp.sem_inc(s_stored[b], 16)
                        with sp.Fori(0, n_tiles // RING) as q:
                            for b in range(RING):
                                sp.wait_ge(s["y_copied"], q * RING + b + 1 + RING)
                                sp.dma_start(y_dram[bass.ds((q * RING + b) * P, P), :], y_sb[b][:, :]).then_inc(s_stored[b], 16)
                        for b in range(RING):
                            sp.wait_ge(s_stored[b], n_tiles // RING * 16 + 16)

                @block.tensor
                def _(pe):
                    pe.sem_inc(s["up"], RING)
                    pe.sem_inc(s["a_turned"], RING)
                    pe.sem_inc(s["down"], RING)
                    for name, value in load:
                        pe.wait_ge(loads[name], value)

                    def turn_h(t, i):
                        pe.wait_ge(s_rows[i % DEPTH], (t - i) * (16 // DEPTH) + (i // DEPTH + 1) * 16)
                        pe.wait_ge(s["h_copied"], t + 1)
                        for kc in range(KC):
                            last = nc.tensor.transpose(bankH[:, kc * P:(kc + 1) * P], rows[i % DEPTH][:, kc * P:(kc + 1) * P], K("ident"))
                        last.then_inc(s["h_turned"], 1)

                    def turn_a(t, i):
                        pe.wait_ge(s["a"], t + 1 + RING)
                        pe.wait_ge(s["a_copied"], t + 1)
                        for k in range(KI):
                            last = nc.tensor.transpose(bankA[:, k * P:(k + 1) * P], a_sb[i % RING][:, k * P:(k + 1) * P], K("ident"))
                        last.then_inc(s["a_turned"], 1)

                    expert = []

                    def load_experts(q):
                        if not experts:
                            expert[:] = [0] * (DEPTH + AHEAD)
                            return
                        word = pe.value_load(experts_i[0:1, bass.ds(q, 1)], min_val=0, max_val=E ** (DEPTH + AHEAD) - 1)
                        expert[:] = [(word >> (3 * i)) & (E - 1) for i in range(DEPTH + AHEAD)]

                    def project(t, i):
                        e = expert[i]
                        pe.wait_ge(s["h_copied"], t + 2)
                        pe.wait_ge(s["a"], t + 1)
                        for w, bank, done in ((gate, bankG, "gated"), (up, bankU, "up")):
                            if w is None:
                                continue
                            for kc in range(KC):
                                last = product(bank[i % RING][:, 0:hidden], [x[:, kc * P:(kc + 1) * P] for x in hT[i % RING]],
                                               [x[:, bass.ds((e * KC + kc) * hidden, hidden)] for x in w], kc == 0, kc == KC - 1)
                            last.then_inc(s[done], 1)

                    def project_back(t, i):
                        e = expert[i]
                        pe.wait_ge(s["a_copied"], t + 2)
                        pe.wait_ge(s["y_copied"], t + 1)
                        for k in range(KI):
                            last = product(bankY[i % RING][:, 0:C], [x[:, k * P:(k + 1) * P] for x in aT[i % RING]],
                                           [x[:, bass.ds((e * KI + k) * C, C)] for x in down], k == 0, k == KI - 1)
                        last.then_inc(s["down"], 1)

                    turn_h(0, 0)
                    turn_h(1, 1)
                    load_experts(0)
                    project(0, 0)
                    turn_h(2, 2)
                    project(1, 1)
                    turn_h(3, 3)
                    turn_a(0, 0)

                    def step(t, i, ahead=True):
                        project(t, i)
                        if ahead:
                            turn_h(t + 2, i + 2)
                        turn_a(t - 1, i - 1)
                        project_back(t - 2, i - 2)
                    steps(pe, step, load_experts)
                    end = n_tiles - rounds * DEPTH
                    turn_a(n_tiles - 1, end - 1)
                    project_back(n_tiles - 2, end - 2)
                    project_back(n_tiles - 1, end - 1)

                @block.scalar
                def _(act):
                    act.sem_inc(s["h_copied"], 1)
                    act.sem_inc(s["y_copied"], RING)

                    def copy_h(t, i):
                        act.wait_ge(s["h_turned"], t + 1)
                        act.wait_ge(s["up"], t + 1)
                        nc.scalar.activation(hT[i % RING][0][:, :], bankH[:, 0:C], ACT.Copy) \
                            .then_inc(s["h_copied" if len(up) == 1 else "h_high"], 1)

                    def activate(t, i):
                        if gate is not None:
                            act.wait_ge(s["gated"], t + 1)
                        else:
                            act.wait_ge(s["up"], t + 1 + RING)
                        act.wait_ge(s["a_turned"], t + 1)
                        nc.scalar.activation(a_sb[i % RING][:, :], bankG[i % RING][:, 0:hidden],
                                             ACT.Silu if gate is not None else ACT.Relu).then_inc(s["act"], 1)

                    def copy_a(t, i):
                        act.wait_ge(s["a_turned"], t + 1 + RING)
                        act.wait_ge(s["down"], t + 1)
                        nc.scalar.activation(aT[i % RING][0][:, :], bankA[:, 0:hidden], ACT.Copy).then_inc(s["a_high"], 1)

                    def copy_y(t, i):
                        act.wait_ge(s["down"], t + 1 + RING)
                        act.wait_ge(s_stored[i % RING], (t - i) * (16 // RING) + i // RING * 16 + 16)
                        nc.scalar.activation(y_sb[i % RING][:, :], bankY[i % RING][:, 0:C], ACT.Copy).then_inc(s["y_copied"], 1)

                    def step(t, i, ahead=True):
                        activate(t, i)
                        if ahead:
                            copy_h(t + 2, i + 2)
                        if len(down) == 2 and i >= 1:
                            copy_a(t - 1, i - 1)
                        if experts and i >= 2:
                            copy_y(t - 2, i - 2)
                    copy_h(0, 0)
                    copy_h(1, 1)
                    step(0, 0)
                    step(1, 1)
                    steps(act, step)
                    if len(down) == 2:
                        copy_a(n_tiles - 1, n_tiles - 1)
                    if experts:
                        copy_y(n_tiles - 2, n_tiles - 2)
                        copy_y(n_tiles - 1, n_tiles - 1)

                @block.vector
                def _(dve):
                    dve.sem_inc(s["a"], RING)
                    dve.sem_inc(s["a_copied"], 1)

                    def low_h(t, i):
                        if len(up) == 2:
                            dve.wait_ge(s["h_high"], t + 1)
                            low_half(nc.vector, hT[i % RING][1][:, :], bankH[:, 0:C], hT[i % RING][0][:, :]).then_inc(s["h_copied"], 1)

                    def multiply(t, i):
                        dve.wait_ge(s["act"], t + 1)
                        dve.wait_ge(s["up"], t + 1 + RING)
                        nc.vector.tensor_tensor(a_sb[i % RING][:, :], a_sb[i % RING][:, :], bankU[i % RING][:, 0:hidden],
                                                ALU.mult).then_inc(s["a"], 1)

                    def copy_a(t, i):
                        if len(down) == 2:
                            dve.wait_ge(s["a_high"], t + 1)
                            low_half(nc.vector, aT[i % RING][1][:, :], bankA[:, 0:hidden], aT[i % RING][0][:, :]).then_inc(s["a_copied"], 1)
                            return
                        dve.wait_ge(s["a_turned"], t + 1 + RING)
                        dve.wait_ge(s["down"], t + 1)
                        nc.vector.tensor_copy(aT[i % RING][0][:, :], bankA[:, 0:hidden]).then_inc(s["a_copied"], 1)

                    def add_y(t, i):
                        dve.wait_ge(s["down"], t + 1 + RING)
                        nc.vector.tensor_tensor(x_tile(t), x_tile(t), bankY[i % RING][:, 0:C], ALU.add).then_inc(s["y_copied"], 1)
                        for k in range(2):
                            u = i * 2 + k
                            dve.wait_ge(s_routed[u % DEPTH_R], (t - i) * (2 * 16 // DEPTH_R) + (u // DEPTH_R + 1) * 16)
                            if k == 0:
                                dve.wait_ge(s["y_copied"], t + 1 + RING)
                            else:
                                dve.wait_ge(s["sum"], t * 2 + 1)
                            nc.vector.scalar_tensor_tensor(out=x_tile(t), in0=routed[u % DEPTH_R][:, :],
                                                                 scalar=w_top[:, bass.ds(t + k * TILES, 1)], in1=x_tile(t),
                                                                 op0=ALU.mult, op1=ALU.add).then_inc(s["sum"], 1)

                    def step(t, i, ahead=True):
                        multiply(t, i)
                        if ahead:
                            low_h(t + 2, i + 2)
                        if i >= 1:
                            copy_a(t - 1, i - 1)
                        if not experts and i >= 2:
                            add_y(t - 2, i - 2)
                    low_h(0, 0)
                    low_h(1, 1)
                    step(0, 0)
                    step(1, 1)
                    steps(dve, step)
                    copy_a(n_tiles - 1, n_tiles - 1)
                    if not experts:
                        add_y(n_tiles - 2, n_tiles - 2)
                        add_y(n_tiles - 1, n_tiles - 1)

        def entry_convolution(on):
            W2 = COLS + 2
            IMG = (ROWS + 2) * W2
            DEPTH = 16
            s = {n: sem(f"conv_{n}") for n in ("var", "sqrt", "xn", "transposed", "high", "copied", "border", "chain", "conv", "feat",
                                               "w_high", "w_low", "sum", "complete")}
            s_in = [sem(f"conv_in{g}") for g in range(DEPTH)]
            y_in = [sb(f"conv_y{g}", [P, C], on=on) for g in range(DEPTH)]
            w_raw = sb("conv_w_raw", [P, 9 * KC * F], on=on)
            w_half = [sb(f"conv_w_half{n}", [P, 9 * KC * F], HALF, on=on) for n in range(2)]
            bankT = [pb(f"conv_bankT{b}", 512, on=on) for b in range(RING)]
            bankC = [pb(f"conv_bankC{b}", 512, on=on) for b in range(RING)]
            padded = [sb(f"conv_padded{n}", [P, KC * IMAGES * IMG], HALF, on=on) for n in range(2)]
            block = on.enter_context(nc.Block())

            def image(part, kc, n):
                return padded[part][:, bass.ds(kc * IMAGES * IMG + n * IMG, IMG)].rearrange("p (y z) -> p y z", z=W2)[:, 1:ROWS + 1, 1:COLS + 1]

            def turned(b, kc):
                return bankT[b][:, kc * 256:(kc + 1) * 256].rearrange("p (y z) -> p y z", z=COLS)

            @block.sync
            def _(sp):
                sp.dma_start(w_raw[:, :], A["conv_w"]).then_inc(loads["conv"], 16)
                load_attention(sp)

            @block.gpsimd
            def _(pool):
                for j in range(TILES):
                    for k in range(2):
                        u = j * 2 + k
                        if u >= DEPTH:
                            pool.wait_ge(s["sum"], u - DEPTH + 1)
                        nc.gpsimd.indirect_dma_start(
                            y_in[u % DEPTH][:, :], None, y_dram,
                            bass.IndirectOffsetOnAxis(ap=pos_i[:, j + k * TILES:j + k * TILES + 1], axis=0)).then_inc(s_in[u % DEPTH], 16)

            @block.scalar
            def _(act):
                act.sem_inc(s["feat"], 1)
                act.wait_ge(loads["conv"], 16)
                nc.scalar.activation(w_half[0][:, :], w_raw[:, :], ACT.Copy).then_inc(s["w_high"], 1)
                act.wait_ge(loads["attn"], ATTN_LOADS * 16)
                act.wait_ge(s["border"], 1)

                def copy(n, b):
                    act.wait_ge(s["transposed"], n + 1 + RING)
                    for kc in range(KC):
                        last = nc.scalar.activation(image(0, kc, n), turned(b, kc), ACT.Copy)
                    last.then_inc(s["high"], 1)

                def relu(g, b):
                    act.wait_ge(s["conv"], g + 1)
                    nc.scalar.activation(feat[:, bass.ds(g * 512, 512)], bankC[b][:, :], ACT.Relu,
                                         bias=entry_sb[:, 1:2], scale=entry_sb[:, 0:1]).then_inc(s["feat"], 1)

                def chunk(c, first=False, last=False):
                    copy(c * 4, 0)
                    copy(c * 4 + 1, 1)
                    if not first:
                        relu(c * 2 - 1, 1)
                    copy(c * 4 + 2, 0)
                    copy(c * 4 + 3, 1)
                    if not last:
                        layer_norm_sqrt(act, s, c + 1)
                    relu(c * 2, 0)
                layer_norm_sqrt(act, s, 0)
                chunk(0, first=True)
                with act.Fori(1, CHUNKS - 1) as c:
                    chunk(c)
                chunk(CHUNKS - 1, last=True)
                relu(CHUNKS * 2 - 1, 1)

            @block.vector
            def _(dve):
                chain = Chain(dve, s["chain"])
                dve.sem_inc(s["copied"], RING)
                for part in range(2):
                    images = padded[part][:, :].bitcast(F32).rearrange("p (n i) -> p n i", i=IMG)
                    nc.vector.memset(images[:, :, 0:W2], 0.0)
                    nc.vector.memset(images[:, :, IMG - W2:IMG], 0.0)
                    by_row = images.rearrange("p n (y z) -> p n y z", z=W2)
                    nc.vector.memset(by_row[:, :, 1:ROWS + 1, 0:1], 0.0)
                    last = nc.vector.memset(by_row[:, :, 1:ROWS + 1, W2 - 1:W2], 0.0)
                last.then_inc(s["border"], 1)

                def weights():
                    dve.wait_ge(s["w_high"], 1)
                    low_half(nc.vector, w_half[1][:, :], w_raw[:, :], w_half[0][:, :]).then_inc(s["w_low"], 1)

                def add_routed(c, tiles, complete=0):
                    for t in tiles:
                        for k in range(2):
                            j, u = c * CHUNK_T + t, t * 2 + k
                            dve.wait_ge(s_in[u % DEPTH], c * (CHUNK_T * 2 // DEPTH * 16) + (u // DEPTH + 1) * 16)
                            if k == 1:
                                dve.wait_ge(s["sum"], c * (CHUNK_T * 2) + u)
                            nc.vector.scalar_tensor_tensor(out=x_tile(j), in0=y_in[u % DEPTH][:, :], scalar=w_top[:, bass.ds(j + k * TILES, 1)],
                                                           in1=x_tile(j), op0=ALU.mult, op1=ALU.add).then_inc(s["sum"], 1)
                    if complete:
                        dve.wait_ge(s["sum"], c * (CHUNK_T * 2) + complete * 2)
                        dve.sem_inc(s["complete"], 1)

                sums = pooled[:, :].rearrange("p (k n) -> p k n", k=KC)

                def lows(n, b):
                    dve.wait_ge(s["high"], n + 1)
                    for kc in range(KC):
                        low_half(nc.vector, image(1, kc, n), turned(b, kc), image(0, kc, n))
                    nc.vector.reduce_sum(sums[:, :, bass.ds(n, 1)], bankT[b][:, :].rearrange("p (k t) -> p k t", k=KC), AX_X).then_inc(s["copied"], 1)
                layer_norm(dve, chain, s, 1e-6, add=add_routed, between=weights, after=lows)
                dve.wait_ge(s["copied"], IMAGES + RING)
                chain(nc.vector.tensor_scalar(pooled[:, :], pooled[:, :], 1.0 / (ROWS * COLS), None, ALU.mult))

            @block.tensor
            def _(pe):
                pe.sem_inc(s["transposed"], RING)

                def turn(n, b):
                    transpose_image(pe, s, n, b, bankT[b])

                def convolve(g, b):
                    pe.wait_ge(s["copied"], g * 2 + 2 + RING)
                    pe.wait_ge(s["feat"], g)
                    for step in range(9 * KC):
                        kc, dr, dc = step // 9, step % 9 // 3, step % 3
                        pair = [x[:, bass.ds(kc * IMAGES * IMG + g * 2 * IMG, 2 * IMG)].rearrange("p (n y z) -> p n y z", n=2, z=W2)
                                [:, :, dr:dr + ROWS, dc:dc + COLS] for x in padded]
                        at = ((dr * 3 + dc) * KC + kc) * F
                        last = product(bankC[b][:, :], [x[:, at:at + F] for x in w_half], pair, step == 0, step == 9 * KC - 1)
                    last.then_inc(s["conv"], 1)
                turn(0, 0)
                turn(1, 1)
                turn(2, 0)
                turn(3, 1)
                pe.wait_ge(s["w_low"], 1)
                convolve(0, 0)
                with pe.Fori(0, (IMAGES // 2 - 2) // 2) as q:
                    for b in range(2):
                        g = q * 2 + b + 1
                        turn(g * 2 + 2, 0)
                        turn(g * 2 + 3, 1)
                        convolve(g, 1 - b)
                convolve(IMAGES // 2 - 1, 1)

        def axial_scores(split):
            on = ExitStack()
            with on:
                STEPS = IMAGES // 2
                names = ("mask", "projected", "queries", "values_t", "values", "chain", "att")
                s = {n: sem(f"axial_{n}") for n in names}
                for ax in ("down", "along"):
                    for n in ("scores", "max", "exp", "soft", "turned", "turned_sb"):
                        s[n, ax] = sem(f"axial_{n}_{ax}")
                s["att_sb"], s["begun"] = sem("axial_att_sb"), sem("axial_begun")
                bankQ, bankF, bankV, bankO = (pb(f"axial_{n}", 512, on=on) for n in ("bankQ", "bankF", "bankV", "bankO"))
                bankS = {ax: pb(f"axial_bankS_{ax}", 512, on=on) for ax in ("down", "along")}
                bankP = {ax: pb(f"axial_bankP_{ax}", 512, on=on) for ax in ("down", "along")}
                q = {ax: [sb(f"axial_q_{ax}{b}", [G, 512], on=on) for b in range(RING)] for ax in ("down", "along")}
                val_t = [sb(f"axial_val_t{b}", [F, 512], on=on) for b in range(RING)]
                val = [sb(f"axial_val{b}", [P, 512], on=on) for b in range(RING)]
                expo = {ax: [sb(f"axial_exp_{ax}{b}", [P, 512], on=on) for b in range(RING)] for ax in ("down", "along")}
                nmax = {ax: sb(f"axial_nmax_{ax}", [P, 4], on=on) for ax in ("down", "along")}
                total = {ax: sb(f"axial_total_{ax}", [P, 4], on=on) for ax in ("down", "along")}
                att_down = sb("axial_att_down", [P, 512], on=on)
                mask = {ax: [sb(f"axial_mask_{ax}_{side}", [9, P], HALF, on=on) for side in "lr"] for ax in ("down", "along")}
                table = {"down": "same_col", "along": "same_row"}
                block = on.enter_context(nc.Block())

                def by_column(image):
                    return image.rearrange("p (y h z) -> p h y z", y=ROWS, h=2)

                def steps(eng, step):
                    step(0, 0, first=True)
                    with eng.Fori(0, (STEPS - 2) // 2) as r:
                        step(r * 2 + 1, 1)
                        step(r * 2 + 2, 0)
                    step(STEPS - 1, (STEPS - 1) % 2, last=True)

                @block.gpsimd
                def _(pool):
                    split(pool)

                @block.tensor
                def _(pe):
                    pe.sem_inc(s["values_t"], RING)
                    pe.wait_ge(s["mask"], 1)
                    pe.wait_ge(loads["attn"], ATTN_LOADS * 16)

                    def project(g):
                        pe.wait_ge(s["queries"], g)
                        nc.tensor.matmul(bankQ[0:64, :], qk_w[:, :], feat[:, bass.ds(g * 512, 512)], start=True, stop=True)
                        nc.tensor.matmul(bankF[:, :], val_w[:, :], feat[:, bass.ds(g * 512, 512)],
                                         start=True, stop=True).then_inc(s["projected"], 1)

                    def scores(g, b):
                        pe.wait_ge(s["queries"], g + 1)
                        for ax in ("down", "along"):
                            pe.wait_ge(s["exp", ax], g)
                            nc.tensor.matmul(bankS[ax][:, :], mask[ax][0][:, :], mask[ax][1][:, :].unsqueeze(1).broadcast_to([9, 4, P]),
                                             start=True, stop=False)
                            for t in range(4):
                                qt = q[ax][b][:, t * P:(t + 1) * P]
                                last = nc.tensor.matmul(bankS[ax][:, t * P:(t + 1) * P], qt, qt, start=False, stop=(t == 3))
                            last.then_inc(s["scores", ax], 1)
                        pe.wait_ge(s["values"], g)
                        for t in range(4):
                            last = nc.tensor.transpose(bankV[:, t * P:(t + 1) * P], val_t[b][:, t * P:(t + 1) * P], K("ident"))
                        last.then_inc(s["values_t"], 1)

                    def attend(g, b):
                        for ax in ("down", "along"):
                            pe.wait_ge(s["soft", ax], g + 1)
                            pe.wait_ge(s["turned_sb", ax], g)
                            for t in range(4):
                                last = nc.tensor.transpose(bankP[ax][:, t * P:(t + 1) * P], expo[ax][b][:, t * P:(t + 1) * P], K("ident"))
                            last.then_inc(s["turned", ax], 1)
                        pe.wait_ge(s["turned_sb", "down"], g + 1)
                        pe.wait_ge(s["values"], g + 1)
                        pe.wait_ge(s["att_sb"], g)
                        for t in range(4):
                            last = nc.tensor.matmul(bankO[:, t * P:(t + 1) * P], val[b][:, t * P:(t + 1) * P],
                                                    att_down[:, t * P:(t + 1) * P], start=True, stop=True)
                        last.then_inc(s["att"], 1)

                    def step(g, b, first=False, last=False):
                        scores(g, b)
                        if not last:
                            project(g + 1)
                        if not first:
                            attend(g - 1, 1 - b)
                    project(0)
                    steps(pe, step)
                    attend(STEPS - 1, (STEPS - 1) % 2)

                @block.scalar
                def _(act):
                    def queries(g, b):
                        act.wait_ge(s["projected"], g + 1)
                        act.wait_ge(s["values_t"], g + 1)
                        for n in range(2):
                            part = slice(n * 256, (n + 1) * 256)
                            nc.scalar.activation(q["down"][b][:, part].rearrange("p (h y z) -> p h y z", h=2, y=ROWS),
                                                 by_column(bankQ[0:G, part]), ACT.Relu, bias=qk_sb[0:G, 1:2], scale=qk_sb[0:G, 0:1])
                            nc.scalar.activation(val_t[b][:, part].rearrange("p (h y z) -> p h y z", h=2, y=ROWS),
                                                 by_column(bankF[:, part]), ACT.Relu, bias=val_sb[:, 1:2], scale=val_sb[:, 0:1])
                        nc.scalar.activation(q["along"][b][:, :], bankQ[32:32 + G, :], ACT.Relu, bias=qk_sb[32:32 + G, 1:2],
                                             scale=qk_sb[32:32 + G, 0:1]).then_inc(s["queries"], 1)

                    def exponentials(g, b):
                        for ax in ("down", "along"):
                            act.wait_ge(s["max", ax], g + 1)
                            for t in range(4):
                                last = nc.scalar.activation(expo[ax][b][:, t * P:(t + 1) * P], bankS[ax][:, t * P:(t + 1) * P], ACT.Exp,
                                                            bias=nmax[ax][:, t:t + 1], accum_out=total[ax][:, t:t + 1])
                            last.then_inc(s["exp", ax], 1)

                    def step(g, b, first=False, last=False):
                        if not last:
                            queries(g + 1, 1 - b)
                        exponentials(g, b)
                    act.wait_ge(loads["attn"], ATTN_LOADS * 16)
                    queries(0, 0)
                    steps(act, step)

                @block.vector
                def _(dve):
                    chain = Chain(dve, s["chain"])
                    dve.wait_ge(loads["attn"], ATTN_LOADS * 16)
                    for ax in ("down", "along"):
                        for side in range(2):
                            last = nc.vector.tensor_copy(mask[ax][side][:, :], K(f"{table[ax]}_{'lr'[side]}", 9))
                    last.then_inc(s["mask"], 1)

                    def copies(g, b):
                        dve.wait_ge(s["turned", "down"], g + 1)
                        nc.vector.tensor_copy(att_down[:, :], bankP["down"][:, :]).then_inc(s["turned_sb", "down"], 1)
                        dve.wait_ge(s["turned", "along"], g + 1)
                        nc.vector.tensor_copy(att_along[:, bass.ds(g * 512, 512)], bankP["along"][:, :]).then_inc(s["turned_sb", "along"], 1)
                        dve.wait_ge(s["att"], g + 1)
                        for n in range(2):
                            last = nc.vector.tensor_copy(by_column(att_t[:, bass.ds(g * 512 + n * 256, 256)]),
                                                         bankO[:, n * 256:(n + 1) * 256].rearrange("p (h y z) -> p h y z", h=2, y=ROWS))
                        last.then_inc(s["att_sb"], 1)

                    def sum_rows(g):
                        dve.wait_ge(s["att_sb"], g + 1)
                        dve.sem_inc(s["begun"], 1)
                        nc.vector.reduce_sum(row_sums[:, bass.ds(g * 2 * ROWS, 2 * ROWS)],
                                             att_t[:, bass.ds(g * 512, 512)].rearrange("p (r c) -> p r c", c=COLS), AX_X)

                    def step(g, b, first=False, last=False):
                        for ax in ("down", "along"):
                            dve.wait_ge(s["scores", ax], g + 1)
                            nc.vector.tensor_reduce(nmax[ax][:, :], bankS[ax][:, :].rearrange("p (t j) -> p t j", t=4), AX_X, ALU.max,
                                                    negate=True).then_inc(s["max", ax], 1)
                        dve.wait_ge(s["values_t"], g + 1 + RING)
                        nc.vector.tensor_copy(val[b][:, :], bankV[:, :]).then_inc(s["values"], 1)
                        if not first:
                            copies(g - 1, 1 - b)
                        for n, ax in enumerate(("down", "along")):
                            dve.wait_ge(s["exp", ax], g + 1)
                            chain.n = g * 2 + n
                            chain(nc.vector.reciprocal(total[ax][:, :], total[ax][:, :]))
                            e3 = expo[ax][b][:, :].rearrange("p (t j) -> p t j", t=4)
                            nc.vector.tensor_tensor(e3, e3, total[ax][:, :].unsqueeze(2).broadcast_to([P, 4, P]),
                                                    ALU.mult).then_inc(s["soft", ax], 1)
                        if not first:
                            sum_rows(g - 1)
                    steps(dve, step)
                    copies(STEPS - 1, (STEPS - 1) % 2)
                    sum_rows(STEPS - 1)

        def gate_network(on, tag, s, in_ps, sums, w0, wh, we, gate):
            hidden = [sb(f"{tag}_hidden{b}", [HID, IMAGES * 16], on=on) for b in range(2)]
            small = sb(f"{tag}_small", [HID, IMAGES * 16], on=on)
            LAYERS = 5

            def tensor(pe):
                pe.wait_ge(s["sums"], 1)
                for n in range(LAYERS):
                    w = w0 if n == 0 else wh[:, (n - 1) * HID:n * HID]
                    if n:
                        pe.wait_ge(s["leaky"], n)
                    nc.tensor.matmul(in_ps[0:HID, 0:256], w, sums[:, :] if n == 0 else hidden[(n - 1) % 2][:, :],
                                     start=True, stop=True).then_inc(s["layer"], 1)
                pe.wait_ge(s["leaky"], LAYERS)
                nc.tensor.matmul(in_ps[:, 0:256], we, hidden[(LAYERS - 1) % 2][:, :], start=True, stop=True).then_inc(s["layer"], 1)

            def vector(dve, chain):
                for n in range(LAYERS):
                    dve.wait_ge(s["layer"], n + 1)
                    chain(nc.vector.tensor_scalar(small[:, :], in_ps[0:HID, 0:256], 0.2, None, ALU.mult))
                    nc.vector.tensor_tensor(hidden[n % 2][:, :], small[:, :], in_ps[0:HID, 0:256], ALU.max).then_inc(s["leaky"], 1)

            def scalar(act):
                act.wait_ge(s["layer"], LAYERS + 1)
                nc.scalar.activation(gate[:, :], in_ps[:, 0:256], ACT.Sigmoid).then_inc(s["gate"], 1)
            return tensor, vector, scalar

        def axial_along():
            on = ExitStack()
            with on:
                s = {n: sem(f"rows_{n}") for n in ("sums", "layer", "leaky", "gate", "chain", "gated", "turned", "turned_sb", "att", "att_sb", "begun")}
                sums = sb("rows_sums", [F, 256], on=on)
                gate = sb("rows_gate", [F, 256], on=on)
                gated = [sb(f"rows_gated{b}", [F, 512], on=on) for b in range(RING)]
                val = [sb(f"rows_val{b}", [P, 512], on=on) for b in range(RING)]
                bankG = pb("rows_bankG", 512, on=on)
                bankX = [pb(f"rows_bankX{b}", 512, on=on) for b in range(RING)]
                bankO = [pb(f"rows_bankO{b}", 512, on=on) for b in range(RING)]
                g_tensor, g_vector, g_scalar = gate_network(on, "rows", s, bankG, sums, gates_w[:, 0:HID], gates_wh[:, 0:4 * HID],
                                                            gates_we[:, 0:F], gate)
                block = on.enter_context(nc.Block())

                @block.tensor
                def _(pe):
                    pe.sem_inc(s["turned"], RING)
                    pe.sem_inc(s["att"], RING)
                    g_tensor(pe)

                    def turn(g, b):
                        pe.wait_ge(s["gated"], g + 1)
                        pe.wait_ge(s["turned_sb"], g + 1)
                        for t in range(4):
                            last = nc.tensor.transpose(bankX[b][:, t * P:(t + 1) * P], gated[b][:, t * P:(t + 1) * P], K("ident"))
                        last.then_inc(s["turned"], 1)

                    def attend(g, b):
                        pe.wait_ge(s["turned_sb"], g + 1 + RING)
                        pe.wait_ge(s["att_sb"], g + 1)
                        for t in range(4):
                            last = nc.tensor.matmul(bankO[b][:, t * P:(t + 1) * P], val[b][:, t * P:(t + 1) * P],
                                                    att_along[:, bass.ds((g * 4 + t) * P, P)], start=True, stop=True)
                        last.then_inc(s["att"], 1)
                    with pe.Fori(0, IMAGES // 4) as r:
                        for b in range(2):
                            turn(r * 2 + b, b)
                        for b in range(2):
                            attend(r * 2 + b, b)

                @block.scalar
                def _(act):
                    act.sem_inc(s["turned_sb"], RING)
                    act.sem_inc(s["att_sb"], RING)
                    g_scalar(act)
                    with act.Fori(0, IMAGES // 4) as r:
                        for b in range(2):
                            g = r * 2 + b
                            act.wait_ge(s["turned"], g + 1 + RING)
                            act.wait_ge(s["att"], g + 1)
                            nc.scalar.activation(val[b][:, :], bankX[b][:, :], ACT.Copy).then_inc(s["turned_sb"], 1)
                        for b in range(2):
                            g = r * 2 + b
                            act.wait_ge(s["att"], g + 1 + RING)
                            nc.scalar.activation(feat[:, bass.ds(g * 512, 512)], bankO[b][:, :], ACT.Copy).then_inc(s["att_sb"], 1)

                @block.vector
                def _(dve):
                    chain = Chain(dve, s["chain"])
                    nc.vector.tensor_scalar(sums[:, :], row_sums[:, :], 1.0 / (ROWS * COLS), None, ALU.mult).then_inc(s["sums"], 1)
                    g_vector(dve, chain)
                    dve.wait_ge(s["gate"], 1)

                    def apply_gate(g, b):
                        dve.wait_ge(s["turned"], g + 1)
                        nc.vector.tensor_tensor(gated[b][:, :].rearrange("p (r c) -> p r c", c=COLS),
                                                att_t[:, bass.ds(g * 512, 512)].rearrange("p (r c) -> p r c", c=COLS),
                                                gate[:, bass.ds(g * 32, 32)].unsqueeze(2).broadcast_to([F, 32, COLS]),
                                                ALU.mult).then_inc(s["gated"], 1)

                    def sum_columns(g):
                        dve.wait_ge(s["att_sb"], g + 1 + RING)
                        dve.sem_inc(s["begun"], 1)
                        nc.vector.reduce_sum(col_sums[:, bass.ds(g * 2 * COLS, 2 * COLS)].rearrange("p (n c) -> p n c", c=COLS),
                                             feat[:, bass.ds(g * 512, 512)].rearrange("p (n r c) -> p n c r", n=2, c=COLS), AX_X)
                    apply_gate(0, 0)
                    apply_gate(1, 1)
                    with dve.Fori(1, IMAGES // 4) as r:
                        for b in range(2):
                            apply_gate(r * 2 + b, b)
                        for b in range(2):
                            sum_columns(r * 2 + b - 2)
                    for b in range(2):
                        sum_columns(IMAGES // 2 - 2 + b)

        def attention_output():
            on = ExitStack()
            with on:
                s = {n: sem(f"cols_{n}") for n in ("sums", "layer", "leaky", "gate", "chain", "gated", "out", "added", "weights", "branch", "branch_sb")}
                sums = sb("cols_sums", [F, 256], on=on)
                gate = sb("cols_gate", [F, 256], on=on)
                gated = [sb(f"cols_gated{b}", [F, 512], on=on) for b in range(RING)]
                branch = sb("cols_branch", [IMAGES, F], on=on)
                picked = [sb(f"cols_picked{b}", [IMAGES, 2 * P], on=on) for b in range(RING)]
                bankG = pb("cols_bankG", 512, on=on)
                bankI = pb("cols_bankI", 512, on=on)
                bankO = [pb(f"cols_bankO{b}", 512, on=on) for b in range(RING)]
                bankB = [pb(f"cols_bankB{b}", 512, on=on) for b in range(RING)]
                g_tensor, g_vector, g_scalar = gate_network(on, "cols", s, bankG, sums, gates_w[:, HID:2 * HID],
                                                            gates_wh[:, 4 * HID:8 * HID], gates_we[:, F:2 * F], gate)
                block = on.enter_context(nc.Block())

                @block.tensor
                def _(pe):
                    pe.sem_inc(s["out"], RING)
                    pe.wait_ge(s["weights"], 3)
                    nc.tensor.matmul(bankI[0:IMAGES, 0:F], K("ones", 1)[:, 0:IMAGES], out_rows[:, 3 * F:4 * F], start=True, stop=False)
                    for kc in range(KC):
                        last = nc.tensor.matmul(bankI[0:IMAGES, 0:F], pooled[:, kc * IMAGES:(kc + 1) * IMAGES], il_w[:, kc * F:(kc + 1) * F],
                                                start=False, stop=(kc == KC - 1))
                    last.then_inc(s["branch"], 1)
                    g_tensor(pe)
                    pe.wait_ge(s["branch_sb"], 1)
                    with pe.Fori(0, IMAGES // 4) as r:
                        for b in range(2):
                            g = r * 2 + b
                            pe.wait_ge(s["gated"], g + 1)
                            pe.wait_ge(s["added"], g + 1)
                            for n in range(2):
                                nc.tensor.matmul(bankB[b][:, n * F:(n + 1) * F], picked[b][:, n * P:(n + 1) * P], branch[:, :],
                                                 start=True, stop=True)
                            for t in range(4):
                                nc.tensor.matmul(bankO[b][:, t * P:(t + 1) * P], K("ones", 1), out_rows[:, 2 * F:3 * F], start=True, stop=False)
                                last = nc.tensor.matmul(bankO[b][:, t * P:(t + 1) * P], gated[b][:, t * P:(t + 1) * P], end_w[:, :],
                                                        start=False, stop=True)
                            last.then_inc(s["out"], 1)

                @block.scalar
                def _(act):
                    act.wait_ge(s["branch"], 1)
                    nc.scalar.activation(branch[:, :], bankI[0:IMAGES, 0:F], ACT.Relu).then_inc(s["branch_sb"], 1)
                    g_scalar(act)

                @block.vector
                def _(dve):
                    chain = Chain(dve, s["chain"])
                    dve.sem_inc(s["added"], RING)
                    nc.vector.tensor_tensor(end_w[:, :], end_w[:, :], scales_b[:, 0:F], ALU.mult).then_inc(s["weights"], 1)
                    for kc in range(KC):
                        nc.vector.tensor_tensor(il_w[:, kc * F:(kc + 1) * F], il_w[:, kc * F:(kc + 1) * F], scales_b[:, F:2 * F],
                                                ALU.mult).then_inc(s["weights"], 1)
                    nc.vector.tensor_scalar(sums[:, :], col_sums[:, :], 1.0 / (ROWS * COLS), None, ALU.mult).then_inc(s["sums"], 1)
                    g_vector(dve, chain)
                    dve.wait_ge(s["gate"], 1)

                    def apply_gate(g, b):
                        dve.wait_ge(s["out"], g + 1)
                        for n in range(2):
                            nc.vector.tensor_tensor(gated[b][:, n * 256:(n + 1) * 256].rearrange("p (r c) -> p r c", c=COLS),
                                                    feat[:, bass.ds(g * 512 + n * 256, 256)].rearrange("p (r c) -> p r c", c=COLS),
                                                    gate[:, bass.ds(g * 32 + n * 16, 16)].unsqueeze(1).broadcast_to([F, ROWS, COLS]), ALU.mult)
                        nc.vector.tensor_copy(picked[b][:, :].rearrange("p (n z) -> p n z", n=2),
                                              K("ident", IMAGES)[:, bass.ds(g * 2, 2)].unsqueeze(2).broadcast_to([IMAGES, 2, P])).then_inc(s["gated"], 1)

                    def add(g, b):
                        dve.wait_ge(s["out"], g + 1 + RING)
                        x4 = x_res[:, bass.ds(g * 4 * C, 4 * C)].rearrange("p (t c) -> p t c", c=C)
                        nc.vector.scalar_tensor_tensor(out=x4[:, :, 0:F], in0=bankO[b][:, :].rearrange("p (t c) -> p t c", c=F), scalar=0.0,
                                                       in1=x4[:, :, 0:F], op0=ALU.max, op1=ALU.add)
                        x22 = x_res[:, bass.ds(g * 4 * C, 4 * C)].rearrange("p (n h c) -> p n h c", n=2, c=C)
                        nc.vector.tensor_tensor(x22[:, :, :, F:2 * F], x22[:, :, :, F:2 * F],
                                                bankB[b][:, 0:2 * F].rearrange("p (n c) -> p n c", n=2).unsqueeze(2).broadcast_to([P, 2, 2, F]),
                                                ALU.add).then_inc(s["added"], 1)
                    apply_gate(0, 0)
                    with dve.Fori(0, IMAGES // 4 - 1) as r:
                        for b in range(2):
                            apply_gate(r * 2 + b + 1, 1 - b)
                            add(r * 2 + b, b)
                    last = IMAGES // 2 - 1
                    apply_gate(last, 1)
                    add(last - 1, 0)
                    add(last, 1)

        with ExitStack() as on:
            s = {n: sem(f"mix_{n}") for n in ("var", "sqrt", "xn", "transposed", "copied", "dft", "chain", "chain_act",
                                              "arg", "sin", "emb", "theta", "magnitude2", "magnitude", "block_diag",
                                              "spectrum", "mixed", "norm", "scaled", "turned", "turned_high", "turned_low", "row", "added")}
            place_tables("konst_mix", on)
            xT = [sb(f"mix_xT{b}", [P, KC * HALVES * P], on=on) for b in range(RING)]
            bankT = [pb(f"mix_bankT{b}", 512, on=on) for b in range(RING)]
            spec_ps = pb("mix_spec", TILES * 2 * MODES, on=on)
            mix_ps = pb("mix_mix", MODES * 2 * TILES, on=on)
            small_ps = pb("mix_small", 512, on=on)
            t_b = sb("mix_t", [2 * MODES, ROWS], on=on)
            w_rep = sb("mix_w", [P, COLS * MODES * 2], on=on)
            w_abs = sb("mix_wabs", [P, COLS * MODES], on=on)
            w_sq = sb("mix_wsq", [P, COLS * MODES], on=on)
            ke = sb("mix_ke", [2 * MODES, 2 * MODES], on=on)
            bias_b = sb("mix_bias", [P, 2 * MODES], on=on)
            arg = sb("mix_arg", [2 * MODES, ROWS], on=on)
            turns = sb("mix_turns", [2 * MODES, ROWS], on=on)
            emb = sb("mix_emb", [2 * MODES, ROWS], on=on)
            emb_x = sb("mix_embx", [2 * MODES, ROWS * COLS], on=on)
            theta = sb("mix_theta", [P, HALVES * 2 * MODES], on=on)
            theta_sq = sb("mix_theta_sq", [P, HALVES * MODES], on=on)
            theta_abs = sb("mix_theta_abs", [P, HALVES * MODES], on=on)
            bd = [sb(f"mix_bd{r}", [P, MODES * P], on=on) for r in range(3)]
            spec = sb("mix_spec_sb", [P, MODES * 3 * TILES], on=on)
            tmp = [sb(f"mix_tmp{b}", [P, IMAGES * MODES], on=on) for b in range(2)]
            rnorm = sb("mix_rnorm", [P, HALVES * MODES], on=on)
            scaled = sb("mix_scaled", [P, TILES * 2 * MODES], on=on)
            def inverse_bank(n):
                return (spec_ps, mix_ps)[n // 2 % 2][:, n % 2 * 512:(n % 2 + 1) * 512], 8 * (n // 4) + n % 4

            turned = [sb(f"mix_turned{n}", [P, 8 * P], HALF, on=on) for n in range(2)]
            idft = [sb(f"mix_idft{n}", [P, C], HALF, on=on) for n in range(2)]

            block = on.enter_context(nc.Block())

            @block.sync
            def _(sp):
                x_rows = A["x"].rearrange("(j p) c -> p j c", p=P)

                def load_x(c):
                    dst = x_res[:, c * CHUNK_T * C:(c + 1) * CHUNK_T * C].rearrange("p (j c) -> p j c", c=C)
                    return sp.dma_start(dst, x_rows[:, c * CHUNK_T:(c + 1) * CHUNK_T, :])
                load_x(0).then_inc(loads["x_first"], 16)
                for kind in ("konst", "konst_mix"):
                    sp.dma_start(konst[kind][:, :], A[kind]).then_inc(loads["konst"], 16)
                sp.wait_ge(loads["spectral"], (3 + ROWS_T) * 16)
                for c in range(1, CHUNKS):
                    load_x(c).then_inc(loads["x"], 16)
                sp.dma_start(router0[:, :], A["L0_ffn_router_w"]).then_inc(loads["router0"], 16)
                sp.wait_ge(loads["x"], (CHUNKS - 1) * 16)
                for dst, name in ((gate0, "gate"), (up0, "up")):
                    sp.dma_start(dst[:, :], A[f"L0_ffn_{name}_w"], max_dma_last_dim=32768).then_inc(loads["w0"], 16)

            @block.scalar
            def _(act):
                act.dma_start(t_b[:, :], A["L0_conv_t"].unsqueeze(0).broadcast_to([2 * MODES, ROWS])).then_inc(loads["spectral"], 16)
                act.dma_start(ke[:, :], A["L0_conv_ke_weights"]).then_inc(loads["spectral"], 16)
                act.dma_start(bias_b[:, :], A["L0_conv_ke_bias"].broadcast_to([P, 2 * MODES])).then_inc(loads["spectral"], 16)
                for r in range(ROWS_T):
                    act.dma_start(w_rep[r * COLS:(r + 1) * COLS, :], A["L0_conv_weights1"]).then_inc(loads["spectral"], 16)
                layer_norm_sqrt(act, s, 0)
                act.wait_ge(s["arg"], 1)
                nc.scalar.activation(emb[:, :], arg[:, :], ACT.Sin).then_inc(s["sin"], 1)
                act.wait_ge(s["magnitude2"], 2)
                nc.scalar.activation(theta_abs[:, :], theta_sq[:, :], ACT.Sqrt).then_inc(s["magnitude"], 1)
                nc.scalar.activation(w_abs[:, :], w_sq[:, :], ACT.Sqrt).then_inc(s["magnitude"], 1)
                act.sem_inc(s["copied"], RING)
                copy_transposes(act, s, xT, bankT, "dft")
                for g in range(2):
                    act.wait_ge(s["turned"], g + 1)
                    nc.scalar.activation(turned[0][:, g * 512:(g + 1) * 512], bankT[g][:, :], ACT.Copy).then_inc(s["turned_high"], 1)

            @block.gpsimd
            def _(pool):
                pool.wait_ge(loads["konst"], 2 * 16)
                pool.wait_ge(loads["spectral"], (3 + ROWS_T) * 16)
                shape = [P, MODES, ROWS_T, COLS]
                w4 = w_rep[:, :].rearrange("p (o m r) -> p m o r", m=MODES, r=2)
                rows = K("row_of").unsqueeze(1).unsqueeze(3)
                for r in range(2):
                    for m in range(MODES):
                        last = nc.gpsimd.tensor_tensor(
                            bd[r][:, m * P:(m + 1) * P].rearrange("p (t o) -> p t o", o=COLS),
                            w4[:, m, :, r].unsqueeze(1).broadcast_to([P, ROWS_T, COLS]),
                            K("row_of").unsqueeze(2).broadcast_to([P, ROWS_T, COLS]), ALU.mult)
                    last.then_inc(s["block_diag"], 1)
                pool.wait_ge(s["magnitude"], 2)
                wa = w_abs[:, :].rearrange("p (o m) -> p m o", m=MODES)
                for m in range(MODES):
                    last = nc.gpsimd.tensor_tensor(
                        bd[2][:, m * P:(m + 1) * P].rearrange("p (t o) -> p t o", o=COLS),
                        wa[:, m, :].unsqueeze(1).broadcast_to([P, ROWS_T, COLS]),
                        K("row_of").unsqueeze(2).broadcast_to([P, ROWS_T, COLS]), ALU.mult)
                last.then_inc(s["block_diag"], 1)

            @block.vector
            def _(dve):
                chain = Chain(dve, s["chain"])
                th = theta[:, :].rearrange("p (h r m) -> p h r m", h=HALVES, r=2)

                def time_weights():
                    dve.wait_ge(loads["konst"], 2 * 16)
                    dve.wait_ge(loads["spectral"], (3 + ROWS_T) * 16)
                    freq, phase = K("freq", 2 * MODES), K("phase", 2 * MODES)
                    chain(nc.vector.tensor_scalar(arg[:, :], t_b[:, :], freq, None, ALU.mult))
                    chain(nc.vector.tensor_scalar(turns[:, :], arg[:, :], phase, 1.0 / TWO_PI, ALU.add, ALU.mult))
                    chain(nc.vector.tensor_scalar(turns[:, :], turns[:, :], ROUND, None, ALU.add))
                    chain(nc.vector.tensor_scalar(turns[:, :], turns[:, :], -ROUND, None, ALU.add))
                    p1 = 6.28125
                    p2 = float(np.round((TWO_PI - p1) * 2 ** 21) / 2 ** 21)
                    for part in (p1, p2, TWO_PI - p1 - p2):
                        chain(nc.vector.scalar_tensor_tensor(out=arg[:, :], in0=turns[:, :], scalar=-part, in1=arg[:, :],
                                                             op0=ALU.mult, op1=ALU.add))
                    chain(nc.vector.tensor_scalar(arg[:, :], arg[:, :], phase, None, ALU.add))
                    pi = float(np.nextafter(np.float32(np.pi), np.float32(0)))
                    nc.vector.tensor_scalar(arg[:, :], arg[:, :], pi, -pi, ALU.min, ALU.max).then_inc(s["arg"], 1)
                    dve.wait_ge(s["sin"], 1)
                    nc.vector.tensor_tensor(emb_x[:, :].rearrange("j (t i) -> j t i", i=COLS),
                                            emb[:, :].unsqueeze(2).broadcast_to([2 * MODES, ROWS, COLS]),
                                            K("head", 2 * MODES).unsqueeze(1).broadcast_to([2 * MODES, ROWS, COLS]),
                                            ALU.mult).then_inc(s["emb"], 1)
                    dve.wait_ge(s["theta"], 1)
                    chain(nc.vector.tensor_tensor(
                        theta[:, :].rearrange("p (h r m) -> p h m r", h=HALVES, r=2),
                        small_ps[:, 0:HALVES * 2 * MODES].rearrange("p (h m r) -> p h m r", h=HALVES, r=2),
                        bias_b[:, :].rearrange("p (m r) -> p m r", r=2).unsqueeze(1).broadcast_to([P, HALVES, MODES, 2]),
                        ALU.add))
                    ths = theta_sq[:, :].rearrange("p (h m) -> p h m", h=HALVES)
                    t0 = tmp[0][:, 0:HALVES * MODES].rearrange("p (h m) -> p h m", h=HALVES)
                    t1 = tmp[1][:, 0:HALVES * MODES].rearrange("p (h m) -> p h m", h=HALVES)
                    chain(nc.vector.tensor_tensor(t0, th[:, :, 0, :], th[:, :, 0, :], ALU.mult))
                    chain(nc.vector.tensor_tensor(t1, th[:, :, 1, :], th[:, :, 1, :], ALU.mult))
                    chain(nc.vector.tensor_tensor(ths, t0, t1, ALU.add))
                    nc.vector.tensor_scalar(ths, ths, 2.0 ** -116, None, ALU.max).then_inc(s["magnitude2"], 1)
                    w3 = w_rep[:, :].rearrange("p (om r) -> p om r", r=2)
                    chain(nc.vector.tensor_tensor(tmp[0][:, :], w3[:, :, 0], w3[:, :, 0], ALU.mult))
                    chain(nc.vector.tensor_tensor(tmp[1][:, :], w3[:, :, 1], w3[:, :, 1], ALU.mult))
                    chain(nc.vector.tensor_tensor(w_sq[:, :], tmp[0][:, :], tmp[1][:, :], ALU.add))
                    nc.vector.tensor_scalar(w_sq[:, :], w_sq[:, :], 2.0 ** -116, None, ALU.max).then_inc(s["magnitude2"], 1)
                    chain(nc.vector.tensor_copy(idft[0][:, :], K("idft")))
                    chain(low_half(nc.vector, idft[1][:, :], K("idft"), idft[0][:, :]))
                    dve.wait_ge(loads["x"], (CHUNKS - 1) * 16)

                dve.wait_ge(loads["x_first"], 16)
                layer_norm(dve, chain, s, 1e-6, between=time_weights)

                dve.wait_ge(s["dft"], IMAGES + RING)
                sp5 = spec_ps[:, :].rearrange("p (b h r m) -> p h r b m", h=HALVES, r=2, m=MODES)
                so5 = spec[:, :].rearrange("p (m v b h) -> p h v b m", v=3, b=IMAGES, h=HALVES)
                v0 = tmp[0][:, :].rearrange("p (b m) -> p b m", m=MODES)
                v1 = tmp[1][:, :].rearrange("p (b m) -> p b m", m=MODES)
                for h in range(HALVES):
                    def wt(r):
                        return th[:, h, r, :].unsqueeze(1).broadcast_to([P, IMAGES, MODES])
                    nc.vector.tensor_tensor(v0, sp5[:, h, 0], wt(0), ALU.mult)
                    chain(nc.vector.tensor_tensor(v1, sp5[:, h, 1], wt(1), ALU.mult))
                    chain(nc.vector.tensor_tensor(so5[:, h, 1], v0, v1, ALU.subtract))
                    nc.vector.tensor_tensor(v0, sp5[:, h, 0], wt(1), ALU.mult)
                    chain(nc.vector.tensor_tensor(v1, sp5[:, h, 1], wt(0), ALU.mult))
                    chain(nc.vector.tensor_tensor(so5[:, h, 2], v0, v1, ALU.add))
                    nc.vector.tensor_scalar(so5[:, h, 0], so5[:, h, 2], -1.0, None, ALU.mult).then_inc(s["spectrum"], 1)
                dve.wait_ge(s["norm"], 1)
                nrm = small_ps[:, 128:128 + HALVES * MODES].rearrange("p (m h) -> p h m", h=HALVES)
                rn = rnorm[:, :].rearrange("p (h m) -> p h m", h=HALVES)
                chain(nc.vector.tensor_scalar(rn, nrm, 1e-12, -1.0, ALU.add, ALU.add))
                chain(nc.vector.tensor_scalar(rn, rn, 0.0, 1.0, ALU.max, ALU.add))
                chain(nc.vector.reciprocal(rn, rn))
                dve.wait_ge(s["mixed"], 1)
                mp = mix_ps[:, :].rearrange("p (m r b h) -> p h r b m", r=2, b=IMAGES, h=HALVES)
                sc = scaled[:, :].rearrange("p (b h r m) -> p h r b m", h=HALVES, r=2, m=MODES)
                for h in range(HALVES):
                    for r in range(2):
                        nc.vector.tensor_tensor(sc[:, h, r], mp[:, h, r],
                                                rn[:, h, :].unsqueeze(1).broadcast_to([P, IMAGES, MODES]),
                                                ALU.mult).then_inc(s["scaled"], 1)
                for g in range(2):
                    dve.wait_ge(s["turned_high"], g + 1)
                    low_half(nc.vector, turned[1][:, g * 512:(g + 1) * 512], bankT[g][:, :], turned[0][:, g * 512:(g + 1) * 512]) \
                        .then_inc(s["turned_low"], 1)
                for n in range(IMAGES):
                    dve.wait_ge(s["row"], n + 1)
                    bank, j = inverse_bank(n)
                    xi = x_res[:, 8 * (n // 4) * C:8 * (n // 4 + 1) * C].rearrange("p (h r c) -> p r h c", h=2, c=C)[:, j % 4]
                    nc.vector.tensor_tensor(xi, xi, bank.rearrange("p (h c) -> p h c", h=2), ALU.add).then_inc(s["added"], 1)

            @block.tensor
            def _(pe):
                pe.sem_inc(s["transposed"], RING)
                pe.sem_inc(s["dft"], RING)
                pe.wait_ge(loads["konst"], 2 * 16)
                pe.wait_ge(loads["spectral"], (3 + ROWS_T) * 16)
                pe.wait_ge(s["emb"], 1)
                for h in range(HALVES):
                    last = nc.tensor.matmul(small_ps[:, h * 32:(h + 1) * 32], emb_x[:, h * P:(h + 1) * P], ke[:, :],
                                            start=True, stop=True)
                last.then_inc(s["theta"], 1)
                dft = K("dft").rearrange("p (k f) -> p k f", k=KC)
                with pe.Fori(0, IMAGES // RING) as q:
                    for b in range(RING):
                        transpose_image(pe, s, q * RING + b, b, bankT[b])
                    for b in range(RING):
                        n = q * RING + b
                        pe.wait_ge(s["copied"], n + 1 + RING)
                        for h in range(HALVES):
                            for kc in range(KC):
                                last = nc.tensor.matmul(spec_ps[:, bass.ds((n * HALVES + h) * 32, 32)],
                                                        xT[b][:, (kc * HALVES + h) * P:(kc * HALVES + h + 1) * P],
                                                        dft[:, kc, :], start=(kc == 0), stop=(kc == KC - 1))
                        last.then_inc(s["dft"], 1)
                pe.wait_ge(s["block_diag"], 3)
                ta = theta_abs[:, :].rearrange("p (h m) -> p m h", h=HALVES)
                pe.wait_ge(s["magnitude"], 2)
                for m in range(MODES):
                    last = nc.tensor.matmul(small_ps[:, 128 + m * HALVES:128 + (m + 1) * HALVES], bd[2][:, m * P:(m + 1) * P],
                                            ta[:, m, :], start=True, stop=True)
                last.then_inc(s["norm"], 1)
                pe.wait_ge(s["spectrum"], HALVES)
                for m in range(MODES):
                    dst = mix_ps[:, m * 64:(m + 1) * 64]
                    nc.tensor.matmul(dst, bd[0][:, m * P:(m + 1) * P], spec[:, m * 96 + 32:m * 96 + 96], start=True, stop=False)
                    last = nc.tensor.matmul(dst, bd[1][:, m * P:(m + 1) * P], spec[:, m * 96:m * 96 + 64], start=False, stop=True)
                last.then_inc(s["mixed"], 1)
                pe.wait_ge(s["scaled"], 2 * HALVES)
                for g in range(8):
                    last = nc.tensor.transpose(bankT[g // 4][:, g % 4 * P:(g % 4 + 1) * P], scaled[:, g * P:(g + 1) * P],
                                               K("ident"))
                    if g % 4 == 3:
                        last.then_inc(s["turned"], 1)
                for n in range(IMAGES):
                    pe.wait_ge(s["turned_low"], n // 8 + 1)
                    if n >= 4:
                        pe.wait_ge(s["added"], n - 3)
                    bank, j0 = inverse_bank(n)
                    for h in range(2):
                        j = j0 + 4 * h
                        r = j % 4 * 32
                        last = product(bank[:, h * C:(h + 1) * C], [x[r:r + 32, j // 4 * P:(j // 4 + 1) * P] for x in turned],
                                       [x[r:r + 32, :] for x in idft], True, True)
                    last.then_inc(s["row"], 1)

        if upto >= 2:
            down0 = [sb(f"down0_{n}", [P, E * (I0 // P) * C], HALF, on=moe0) for n in range(2)]
            with ExitStack() as staging:
                stage = [sb(f"w0_stage{b}", [P, 1024], on=staging) for b in range(RING)]
                router("moe0", router0, "router0", split_weights("w0", stage, [(A["L0_ffn_down_w"], *down0)]))
            mlp("experts0", SLOT_TILES, I0, [up0], down0, [gate0], (("w0", 2 * 16),))
        moe0.close()
        clear_semaphores()
        if upto >= 3:
            entry_sb = sb("entry_sb", [P, 2])
            qk_w = sb("qk_w", [F, 64])
            qk_sb = sb("qk_sb", [64, 2])
            val_w = sb("val_w", [F, F])
            val_sb = sb("val_sb", [F, 2])
            gates_w = sb("gates_w", [F, 2 * HID])
            gates_wh = sb("gates_wh", [HID, 8 * HID])
            gates_we = sb("gates_we", [HID, 2 * F])
            end_w = sb("end_w", [F, F])
            il_w = sb("il_w", [P, KC * F])
            out_rows = sb("out_rows", [1, 4 * F])
            scales_b = sb("scales_b", [P, 2 * F])
            feat = sb("feat", [F, TOKENS])
            pooled = sb("pooled", [P, KC * IMAGES])
            router1 = sb("router1_sb", [P, KC * E])
            place_tables("konst_attn")
            ATTN_LOADS = 13

            def load_attention(sp):
                for dst, name in ((entry_sb, "entry_sb"), (qk_w, "qk_w"), (qk_sb, "qk_sb"), (val_w, "val_w"), (val_sb, "val_sb"),
                                  (gates_w, "gates_w"), (gates_wh, "gates_wh"), (gates_we, "gates_we"), (end_w, "end_w"), (il_w, "il_w"),
                                  (out_rows, "out_rows")):
                    sp.dma_start(dst[:, :], A[name]).then_inc(loads["attn"], 16)
                sp.dma_start(konst["konst_attn"][:, :], A["konst_attn"]).then_inc(loads["attn"], 16)
                sp.dma_start(scales_b[:, :], A["out_rows"][:, 0:2 * F].broadcast_to([P, 2 * F])).then_inc(loads["attn"], 16)
                sp.dma_start(router1[:, :], A["L1_ffn_w_router"]).then_inc(loads["router1"], 16)

            with ExitStack() as on:
                entry_convolution(on)
            up1, down1, ws1, ws2 = ([sb(f"{name}_{n}", [P, width], HALF) for n in range(2)]
                                    for name, width in (("up1", E * KC * I1), ("down1", E * I1 // P * C), ("ws1", KC * IS), ("ws2", IS // P * C)))
            with ExitStack() as on:
                split1 = split_weights("w1", xn, [(A["L1_ffn_w1_stack"], *up1), (A["L1_ffn_w2_stack"], *down1),
                                              (A["L1_ffn_ws1"], *ws1), (A["L1_ffn_ws2"], *ws2)])
                att_t = sb("att_t", [F, TOKENS], on=on)
                att_along = sb("att_along", [P, TILES * P], on=on)
                row_sums = sb("row_sums", [F, IMAGES * ROWS], on=on)
                col_sums = sb("col_sums", [F, IMAGES * COLS], on=on)
                axial_scores(split1)
                axial_along()
                attention_output()
        clear_semaphores()
        if upto >= 4:
            router("moe1", router1, "router1")
            mlp("experts1", SLOT_TILES, I1, up1, down1)
            mlp("shared", TILES, IS, ws1, ws2, experts=False, sink=out)
        else:
            with nc.Block() as block:
                @block.sync
                def _(sp):
                    stored = sem("out_stored")
                    sp.dma_start(out.rearrange("(j p) c -> p j c", p=P), x_res[:, :].rearrange("p (j c) -> p j c", c=C)).then_inc(stored, 16)
                    sp.wait_ge(stored, 16)


def padded_pair(v, h, axis):
    pad = [(0, 0), (0, 0)]
    pad[axis] = (0, 32 - G)
    return np.ascontiguousarray(np.concatenate([np.pad(v, pad), np.pad(h, pad)], axis))


def by_contracted_row(w):
    e, o, c = w.shape
    return np.ascontiguousarray(w.reshape(e, o, c // P, P).transpose(3, 0, 2, 1).reshape(P, -1))


def layouts(inputs):
    a = {k: np.asarray(v) for k, v in inputs.items()}
    t = np.ascontiguousarray
    return {
        **constants()[0],
        "x": t(a["x"].reshape(TOKENS, C)),
        "L0_conv_t": t(a["L0_conv_t"]),
        "L0_conv_weights1": t(a["L0_conv_weights1"].reshape(COLS, -1)),
        "L0_conv_ke_weights": t(a["L0_conv_ke_weights"].reshape(2 * MODES, 2 * MODES)),
        "L0_conv_ke_bias": t(a["L0_conv_ke_bias"].reshape(1, 2 * MODES)),
        "conv_w": t(a["L1_conv_entry_w"].reshape(9, KC, P, F).transpose(2, 0, 1, 3).reshape(P, -1)),
        "entry_sb": t(np.stack([a["L1_conv_entry_s"], a["L1_conv_entry_b"]], 1)),
        "qk_w": padded_pair(a["L1_conv_vqk_w"], a["L1_conv_hqk_w"], 1),
        "qk_sb": padded_pair(np.stack([a["L1_conv_vqk_s"], a["L1_conv_vqk_b"]], 1), np.stack([a["L1_conv_hqk_s"], a["L1_conv_hqk_b"]], 1), 0),
        "val_w": a["L1_conv_val_w"],
        "val_sb": t(np.stack([a["L1_conv_val_s"], a["L1_conv_val_b"]], 1)),
        "gates_w": t(np.concatenate([a["L1_conv_vca_w0"], a["L1_conv_hca_w0"]], 1)),
        "gates_wh": t(np.concatenate([a["L1_conv_vca_wh"], a["L1_conv_hca_wh"]], 0).transpose(1, 0, 2).reshape(HID, -1)),
        "gates_we": t(np.concatenate([a["L1_conv_vca_we"], a["L1_conv_hca_we"]], 1)),
        "end_w": a["L1_conv_end_w"],
        "il_w": t(a["L1_conv_il_w"].reshape(KC, P, F).transpose(1, 0, 2).reshape(P, -1)),
        "out_rows": t(np.concatenate([a[f"L1_conv_{n}"] for n in ("end_s", "il_s", "end_b", "il_b")])[None]),
        "L1_ffn_w_router": by_contracted_row(a["L1_ffn_w_router"][None]),
        "L1_ffn_ws1": by_contracted_row(a["L1_ffn_ws1"][None]),
        "L1_ffn_ws2": by_contracted_row(a["L1_ffn_ws2"][None]),
        "L1_ffn_w1_stack": by_contracted_row(a["L1_ffn_w1_stack"]),
        "L1_ffn_w2_stack": by_contracted_row(a["L1_ffn_w2_stack"]),
        "L0_ffn_router_w": by_contracted_row(a["L0_ffn_router_w"][None]),
        "L0_ffn_gate_w": by_contracted_row(a["L0_ffn_gate_w"]),
        "L0_ffn_up_w": by_contracted_row(a["L0_ffn_up_w"]),
        "L0_ffn_down_w": by_contracted_row(a["L0_ffn_down_w"]),
    }


def kernel(**inputs):
    import concourse.bacc as bacc
    from concourse.bass_utils import run_bass_kernel_spmd

    nc = bacc.Bacc("TRN2", target_bir_lowering=False, num_devices=1)
    arrays = layouts(inputs)
    ins = {n: nc.dram_tensor("in_" + n, a.shape, mybir.dt.from_np(a.dtype), kind="ExternalInput").ap() for n, a in arrays.items()}
    out = nc.dram_tensor("out", (TOKENS, C), F32, kind="ExternalOutput").ap()
    build(nc, ins, out)
    r = run_bass_kernel_spmd(nc, [{"in_" + n: a for n, a in arrays.items()}], core_ids=[0])
    return r.results[0]["out"].reshape(IMAGES, ROWS, COLS, C)
```
